# Optimizing a Trainium2 kernel written in Bass

```python
import numpy as np
import jax
import jax.numpy as jnp

def _softmax(x, axis=-1):
    return jax.nn.softmax(x, axis=axis)

def _gelu(x):
    return jax.nn.gelu(x, approximate=True)

def _silu(x):
    return jax.nn.silu(x)

def _sigmoid(x):
    return jax.nn.sigmoid(x)

def _layernorm(x, axis=-1, eps=1e-05):
    m = jnp.mean(x, axis=axis, keepdims=True)
    v = jnp.var(x, axis=axis, keepdims=True)
    return (x - m) / jnp.sqrt(v + eps)

def _scatter_add(tgt, idx, src, axis=0):
    return tgt.at[idx].add(src)

def _segment_sum(src, seg, n):
    return jax.ops.segment_sum(src, seg, n)
kernel_name = 'mk_decoder_preln_d4_seqx_r4_cb394e'

def setup_inputs(seed: int=0):
    np.random.seed(seed)
    _w = jnp.asarray

    def _rec_inputs():
        import jax
        import jax.numpy as jnp
        _rk = jax.random.key(seed)
        x = 7.22e-05 + 1 * jax.random.normal(jax.random.fold_in(_rk, 1), (16, 128, 256), jnp.float32)
        _lenS = 128 - jax.random.randint(jax.random.fold_in(_rk, 7), (16,), 0, max(1, 128 // 4) + 1, jnp.int32)
        _lenS2 = 128 - jax.random.randint(jax.random.fold_in(_rk, 8), (16,), 0, max(1, 128 // 4) + 1, jnp.int32)
        _ctx_1024P = jax.random.normal(jax.random.fold_in(_rk, 11), (16, 16, 256), jnp.float32)
        _ctx_1024c = jax.random.dirichlet(jax.random.fold_in(_rk, 511), 0.3 * jnp.ones((16,), jnp.float32), (16, 128))
        _ctx_1024t = jnp.einsum('bsk,bkd->bsd', _ctx_1024c, _ctx_1024P)
        _ctx_1024t = _ctx_1024t * jax.lax.rsqrt(jnp.mean(jnp.square(_ctx_1024t)) + 1e-12) * 0.953939
        ctx_1024 = 4.13588e-05 + 0.999923 * (_ctx_1024t + 0.3 * jax.random.normal(jax.random.fold_in(_rk, 611), (16, 128, 256), jnp.float32))
        fside_BxS2_0 = jax.random.uniform(jax.random.fold_in(_rk, 14), (16, 128), jnp.float32, 0.0, 0.999833)
        _validS = jnp.arange(128)[None, :] < _lenS[:, None]
        _validS2 = jnp.arange(128)[None, :] < _lenS2[:, None]
        _causal = jnp.tril(jnp.ones((128, 128), dtype=bool))
        mask_Bx1xSxS2_bk1 = jnp.broadcast_to(_validS2[:, None, None, :], (16, 1, 128, 128))
        mask_BxS2xS_ik0 = jnp.where(jnp.broadcast_to(_validS[:, None, :], (16, 128, 128)), 0, 1).astype(jnp.int32)
        mask_BxS2_ff1 = jnp.where(jnp.ones((16, 128), dtype=bool), 1.0, 0.0).astype(jnp.float32)
        return (x, ctx_1024, fside_BxS2_0, mask_Bx1xSxS2_bk1, mask_BxS2xS_ik0, mask_BxS2_ff1)
    x, ctx_1024, fside_BxS2_0, mask_Bx1xSxS2_bk1, mask_BxS2xS_ik0, mask_BxS2_ff1 = _rec_inputs()

    def _L0_attn_setup():
        import jax, jax.numpy as jnp
        import numpy as np
        B, T, C, I = (4, 1024, 256, 1024)

        def rmsnorm(x, w, eps=1e-06):
            return x * jax.lax.rsqrt(jnp.mean(x * x, axis=-1, keepdims=True) + eps) * w

        def shift(h):
            return jnp.pad(h, ((0, 0), (1, 0), (0, 0)))[:, :-1]

        def wkv_scan(k, v, w, u):
            ew = jnp.exp(jnp.clip(w, -20.0, 20.0))

            def step(carry, kv):
                a, b = carry
                kt, vt = kv
                ekt = jnp.exp(jnp.clip(u + kt, -20.0, 20.0))
                out = (a + ekt * vt) / (b + ekt + 1e-08)
                ek = jnp.exp(jnp.clip(kt, -20.0, 20.0))
                return ((ew * a + ek * vt, ew * b + ek), out)
            init = (jnp.zeros((k.shape[0], k.shape[2]), jnp.float32), jnp.zeros((k.shape[0], k.shape[2]), jnp.float32))
            _, out = jax.lax.scan(step, init, (k.swapaxes(0, 1), v.swapaxes(0, 1)))
            return out.swapaxes(0, 1)
        key = jax.random.key(seed)
        ks = jax.random.split(key, 16)
        s = 1.0 / np.sqrt(C)
        si = 1.0 / np.sqrt(I)
        return {'x': jax.random.normal(ks[0], (B, T, C), jnp.float32), 'ln1_w': jnp.ones((C,), jnp.float32), 'ln2_w': jnp.ones((C,), jnp.float32), 'time_decay': jax.random.normal(ks[1], (C,), jnp.float32) * 0.1 - 5.0, 'time_first': jax.random.normal(ks[2], (C,), jnp.float32) * 0.01, 'time_mix_k': jnp.full((C,), 0.5, jnp.float32), 'time_mix_v': jnp.full((C,), 0.5, jnp.float32), 'time_mix_r': jnp.full((C,), 0.5, jnp.float32), 'W_key': jax.random.normal(ks[3], (C, C), jnp.float32) * s, 'W_value': jax.random.normal(ks[4], (C, C), jnp.float32) * s, 'W_recept': jax.random.normal(ks[5], (C, C), jnp.float32) * s, 'W_out': jax.random.normal(ks[6], (C, C), jnp.float32) * s, 'time_mix_k2': jnp.full((C,), 0.5, jnp.float32), 'time_mix_r2': jnp.full((C,), 0.5, jnp.float32), 'W_key2': jax.random.normal(ks[7], (C, I), jnp.float32) * s, 'W_value2': jax.random.normal(ks[8], (I, C), jnp.float32) * si, 'W_recept2': jax.random.normal(ks[9], (C, C), jnp.float32) * s}
    _L0_attn_all = _L0_attn_setup()
    _L0_attn_in = {k: v for k, v in _L0_attn_all.items() if k in ('ln1_w', 'ln2_w', 'time_decay', 'time_first', 'time_mix_k', 'time_mix_v', 'time_mix_r', 'W_key', 'W_value', 'W_recept', 'W_out', 'time_mix_k2', 'time_mix_r2', 'W_key2', 'W_value2', 'W_recept2')}
    del _L0_attn_all

    def _L0_xattn_setup():
        import jax, jax.numpy as jnp
        import numpy as np
        B, S, D, H = (4, 512, 256, 16)
        HD = D // H
        key = jax.random.key(seed)
        ks = jax.random.split(key, 12)
        scale = 1.0 / np.sqrt(D)
        inp = {'queries': jax.random.normal(ks[0], (B, S, D), jnp.float32), 'keys': jax.random.normal(ks[1], (B, S, D), jnp.float32), 'values': jax.random.normal(ks[2], (B, S, D), jnp.float32), 'mask': jax.random.randint(ks[3], (B, 1, S, S), 0, 2).astype(bool), 'Wq': jax.random.normal(ks[4], (D, D), jnp.float32) * scale, 'bq': jnp.zeros((D,), jnp.float32), 'Wk': jax.random.normal(ks[5], (D, D), jnp.float32) * scale, 'bk': jnp.zeros((D,), jnp.float32), 'Wv': jax.random.normal(ks[6], (D, D), jnp.float32) * scale, 'bv': jnp.zeros((D,), jnp.float32), 'Wo': jax.random.normal(ks[7], (D, D), jnp.float32) * scale, 'bo': jnp.zeros((D,), jnp.float32)}
        return inp
    _L0_xattn_all = _L0_xattn_setup()
    _L0_xattn_in = {k: v for k, v in _L0_xattn_all.items() if k in ('Wq', 'bq', 'Wk', 'bk', 'Wv', 'bv', 'Wo', 'bo')}
    del _L0_xattn_all

    def _L0_ffn_setup():
        import jax, jax.numpy as jnp
        import numpy as np
        EPS = 1e-06
        LN_EPS = 1e-05

        def _absmean_core(W):
            gamma = jnp.mean(jnp.abs(W)) + EPS
            Ws = W / gamma
            Wq = jnp.sign(Ws) * jnp.minimum(jnp.round(jnp.abs(Ws)), 1.0)
            return (Wq, gamma)

        @jax.custom_vjp
        def absmean(W):
            return _absmean_core(W)[0]

        def _absmean_fwd(W):
            Wq, gamma = _absmean_core(W)
            return (Wq, gamma)

        def _absmean_bwd(gamma, g):
            return (g / gamma,)
        absmean.defvjp(_absmean_fwd, _absmean_bwd)

        def layernorm(x, w, b, eps=LN_EPS):
            mu = jnp.mean(x, axis=-1, keepdims=True)
            var = jnp.mean((x - mu) ** 2, axis=-1, keepdims=True)
            return (x - mu) * jax.lax.rsqrt(var + eps) * w + b
        key = jax.random.key(seed)
        k1, k2, k3 = jax.random.split(key, 3)
        d, h = (256, 1024)
        B, T = (8, 512)
        return {'x': jax.random.normal(k1, (B, T, d), jnp.float32), 'W_fc': jax.random.normal(k2, (h, d), jnp.float32), 'ln_w': jnp.ones((h,), jnp.float32), 'ln_b': jnp.zeros((h,), jnp.float32), 'W_proj': jax.random.normal(k3, (d, h), jnp.float32)}
    _L0_ffn_all = _L0_ffn_setup()
    _L0_ffn_in = {k: v for k, v in _L0_ffn_all.items() if k in ('W_fc', 'ln_w', 'ln_b', 'W_proj')}
    del _L0_ffn_all

    def _L1_attn_setup():
        import jax, jax.numpy as jnp
        import numpy as np
        import math
        N_HEAD = 16
        ROPE_BASE = 10000.0

        def _rope_as_in_source(x):
            B, H, T, hd = x.shape
            theta = 1.0 / ROPE_BASE ** (jnp.arange(0, hd, 2, dtype=jnp.float32) / hd)
            ang = jnp.arange(H, dtype=jnp.float32)[:, None] * theta[None, :]
            cos = jnp.cos(ang)[None, :, None, :]
            sin = jnp.sin(ang)[None, :, None, :]
            xr = x.reshape(B, H, T, hd // 2, 2)
            out = jnp.stack([xr[..., 0] * cos - xr[..., 1] * sin, xr[..., 1] * cos + xr[..., 0] * sin], axis=-1)
            return out.reshape(B, H, T, hd)
        key = jax.random.key(seed)
        ks = jax.random.split(key, 5)
        B, T, C = (2, 512, 256)
        s = 0.02
        return {'x': jax.random.normal(ks[0], (B, T, C), dtype=jnp.float32), 'W_attn': jax.random.normal(ks[1], (C, 3 * C), dtype=jnp.float32) * s, 'b_attn': jnp.zeros((3 * C,), dtype=jnp.float32), 'W_proj': jax.random.normal(ks[2], (C, C), dtype=jnp.float32) * s, 'b_proj': jnp.zeros((C,), dtype=jnp.float32)}
    _L1_attn_all = _L1_attn_setup()
    _L1_attn_in = {k: v for k, v in _L1_attn_all.items() if k in ('W_attn', 'b_attn', 'W_proj', 'b_proj')}
    del _L1_attn_all

    def _L1_xattn_setup():
        import jax, jax.numpy as jnp
        import numpy as np
        H, P = (16, 4)
        B, L, D = (2, 1024, 256)
        rng = jax.random.key(seed)
        ks = jax.random.split(rng, 12)
        w = lambda k, shape, s=0.02: jax.random.normal(k, shape, jnp.float32) * s
        return {'query': jax.random.normal(ks[0], (B, L, D), jnp.float32), 'key': jax.random.normal(ks[1], (B, L, D), jnp.float32), 'value': jax.random.normal(ks[2], (B, L, D), jnp.float32), 'w_qk': w(ks[3], (D, 2 * D)), 'b_qk': jnp.zeros((2 * D,), jnp.float32), 'w_value': w(ks[4], (D, D)), 'b_value': jnp.zeros((D,), jnp.float32), 'w_off': w(ks[5], (D, H * P * 2)), 'b_off': w(ks[6], (H * P * 2,), 0.3), 'w_attw': w(ks[7], (D, H * P)), 'b_attw': jnp.zeros((H * P,), jnp.float32), 'w_out': w(ks[8], (D, D)), 'b_out': jnp.zeros((D,), jnp.float32)}
    _L1_xattn_all = _L1_xattn_setup()
    _L1_xattn_in = {k: v for k, v in _L1_xattn_all.items() if k in ('w_qk', 'b_qk', 'w_value', 'b_value', 'w_off', 'b_off', 'w_attw', 'b_attw', 'w_out', 'b_out')}
    del _L1_xattn_all

    def _L1_ffn_setup():
        import jax, jax.numpy as jnp
        import numpy as np
        BEST_K = 2

        def _expert(xf, w1, w3, w2):
            return jax.nn.silu(xf @ w1) * (xf @ w3) @ w2
        key = jax.random.key(seed)
        ks = jax.random.split(key, 9)
        E, S_sh, D, H = (8, 2, 256, 128)
        B, S = (2, 512)
        w = lambda k, shape: jax.random.normal(k, shape, dtype=jnp.float32) * 0.02
        return {'x': jax.random.normal(ks[0], (B, S, D), dtype=jnp.float32), 'router_w': w(ks[1], (D, E)), 'router_b': jnp.zeros((E,), dtype=jnp.float32), 'routed_w1': w(ks[2], (E, D, H)), 'routed_w3': w(ks[3], (E, D, H)), 'routed_w2': w(ks[4], (E, H, D)), 'shared_w1': w(ks[5], (S_sh, D, H)), 'shared_w3': w(ks[6], (S_sh, D, H)), 'shared_w2': w(ks[7], (S_sh, H, D))}
    _L1_ffn_all = _L1_ffn_setup()
    _L1_ffn_in = {k: v for k, v in _L1_ffn_all.items() if k in ('router_w', 'router_b', 'routed_w1', 'routed_w3', 'routed_w2', 'shared_w1', 'shared_w3', 'shared_w2')}
    del _L1_ffn_all

    def _L2_attn_setup():
        import jax, jax.numpy as jnp
        import numpy as np
        B, S, D, H, A = (2, 512, 256, 16, 64)
        INIT_STD = 0.02
        key = jax.random.key(seed)
        ks = jax.random.split(key, 5)
        return {'residual': jax.random.normal(ks[0], (B, S, D), dtype=jnp.float32), 'Wq': jax.random.normal(ks[1], (H, D, A), dtype=jnp.float32) * INIT_STD, 'Wk': jax.random.normal(ks[2], (H, D, A), dtype=jnp.float32) * INIT_STD, 'Wv': jax.random.normal(ks[3], (H, D, A), dtype=jnp.float32) * INIT_STD, 'Wo': jax.random.normal(ks[4], (H, A, D), dtype=jnp.float32) * INIT_STD, 'bq': jnp.zeros((H, A), dtype=jnp.float32), 'bk': jnp.zeros((H, A), dtype=jnp.float32), 'bv': jnp.zeros((H, A), dtype=jnp.float32), 'bo': jnp.zeros((D,), dtype=jnp.float32)}
    _L2_attn_all = _L2_attn_setup()
    _L2_attn_in = {k: v for k, v in _L2_attn_all.items() if k in ('Wq', 'Wk', 'Wv', 'Wo', 'bq', 'bk', 'bv', 'bo')}
    del _L2_attn_all

    def _L2_xattn_setup():
        import jax, jax.numpy as jnp
        import numpy as np
        B, T, V, C = (32, 64, 250, 256)
        H, DH = (8, 64)
        INNER = H * DH
        K = 5
        SCALE = DH ** (-0.5)

        def layer_norm(x, w, b, eps=1e-05):
            mu = jnp.mean(x, axis=-1, keepdims=True)
            var = jnp.mean(jnp.square(x - mu), axis=-1, keepdims=True)
            return (x - mu) * jax.lax.rsqrt(var + eps) * w + b
        key = jax.random.key(seed)
        ks = jax.random.split(key, 8)
        x = jax.random.normal(ks[0], (B, T, C), dtype=jnp.float32)
        vision = jax.random.normal(ks[1], (B, V, C), dtype=jnp.float32)
        idx = jax.random.randint(ks[2], (B, T, K), 0, V)
        mask = jnp.zeros((B, V, T), jnp.int32)
        mask = mask.at[jnp.arange(B)[:, None, None], idx, jnp.arange(T)[None, :, None]].set(1)
        Wq = jax.random.normal(ks[3], (C, INNER), dtype=jnp.float32) * 0.02
        Wkv = jax.random.normal(ks[4], (C, 2 * INNER), dtype=jnp.float32) * 0.02
        Wout = jax.random.normal(ks[5], (INNER, C), dtype=jnp.float32) * 0.02
        return {'x': x, 'vision': vision, 'ln_w': jnp.ones((C,), jnp.float32), 'ln_b': jnp.zeros((C,), jnp.float32), 'Wq': Wq, 'Wkv': Wkv, 'Wout': Wout, 'attention_mask': mask, 'num_support': K}
    _L2_xattn_all = _L2_xattn_setup()
    _L2_xattn_in = {k: v for k, v in _L2_xattn_all.items() if k in ('ln_w', 'ln_b', 'Wq', 'Wkv', 'Wout')}
    del _L2_xattn_all

    def _L2_ffn_setup():
        import jax, jax.numpy as jnp
        import numpy as np
        B, S, H, NH, E, F = (4, 256, 256, 16, 8, 1024)
        D = H // NH
        EPS = 1e-05

        def _layernorm(x, g, b):
            mu = jnp.mean(x, axis=-1, keepdims=True)
            var = jnp.var(x, axis=-1, keepdims=True)
            return (x - mu) * jax.lax.rsqrt(var + EPS) * g + b
        key = jax.random.key(seed)
        ks = jax.random.split(key, 16)
        s = 0.02
        return {'x': jax.random.normal(ks[0], (B, S, H), jnp.float32), 'ln1_g': jnp.ones((H,), jnp.float32), 'ln1_b': jnp.zeros((H,), jnp.float32), 'ln2_g': jnp.ones((H,), jnp.float32), 'ln2_b': jnp.zeros((H,), jnp.float32), 'wq': jax.random.normal(ks[1], (H, H), jnp.float32) * s, 'bq': jnp.zeros((H,), jnp.float32), 'wk': jax.random.normal(ks[2], (H, H), jnp.float32) * s, 'bk': jnp.zeros((H,), jnp.float32), 'wv': jax.random.normal(ks[3], (H, H), jnp.float32) * s, 'bv': jnp.zeros((H,), jnp.float32), 'wo': jax.random.normal(ks[4], (H, H), jnp.float32) * s, 'bo': jnp.zeros((H,), jnp.float32), 'gate_w': jax.random.normal(ks[5], (H, E), jnp.float32) * s, 'gate_b': jnp.zeros((E,), jnp.float32), 'w1': jax.random.normal(ks[6], (E, H, F), jnp.float32) * s, 'b1': jnp.zeros((E, F), jnp.float32), 'w2': jax.random.normal(ks[7], (E, F, H), jnp.float32) * s, 'b2': jnp.zeros((E, H), jnp.float32)}
    _L2_ffn_all = _L2_ffn_setup()
    _L2_ffn_in = {k: v for k, v in _L2_ffn_all.items() if k in ('ln1_g', 'ln1_b', 'ln2_g', 'ln2_b', 'wq', 'bq', 'wk', 'bk', 'wv', 'bv', 'wo', 'bo', 'gate_w', 'gate_b', 'w1', 'b1', 'w2', 'b2')}
    del _L2_ffn_all

    def _L3_attn_setup():
        import jax, jax.numpy as jnp
        import numpy as np
        B, S, D = (4, 1024, 256)
        GROUP = 64
        HEAD = 128
        INNER = 512
        key = jax.random.key(seed)
        ks = jax.random.split(key, 16)
        s = 0.02
        return {'x': jax.random.normal(ks[0], (B, S, D), jnp.float32), 'Wv': jax.random.normal(ks[1], (D, INNER), jnp.float32) * s, 'bv': jnp.zeros((INNER,), jnp.float32), 'Wg': jax.random.normal(ks[2], (D, INNER), jnp.float32) * s, 'bg': jnp.zeros((INNER,), jnp.float32), 'Win': jax.random.normal(ks[3], (D, HEAD), jnp.float32) * s, 'bin_': jnp.zeros((HEAD,), jnp.float32), 'Wout': jax.random.normal(ks[4], (INNER, D), jnp.float32) * s, 'bout': jnp.zeros((D,), jnp.float32), 'g_qq': 1.0 + jax.random.normal(ks[5], (HEAD,), jnp.float32) * s, 'b_qq': jnp.zeros((HEAD,), jnp.float32), 'g_qk': 1.0 + jax.random.normal(ks[6], (HEAD,), jnp.float32) * s, 'b_qk': jnp.zeros((HEAD,), jnp.float32), 'g_lq': 1.0 + jax.random.normal(ks[7], (HEAD,), jnp.float32) * s, 'b_lq': jnp.zeros((HEAD,), jnp.float32), 'g_lk': 1.0 + jax.random.normal(ks[8], (HEAD,), jnp.float32) * s, 'b_lk': jnp.zeros((HEAD,), jnp.float32)}
    _L3_attn_all = _L3_attn_setup()
    _L3_attn_in = {k: v for k, v in _L3_attn_all.items() if k in ('Wv', 'bv', 'Wg', 'bg', 'Win', 'bin_', 'Wout', 'bout', 'g_qq', 'b_qq', 'g_qk', 'b_qk', 'g_lq', 'b_lq', 'g_lk', 'b_lk')}
    del _L3_attn_all

    def _L3_xattn_setup():
        import jax, jax.numpy as jnp
        import numpy as np
        EMBED_DIM = 256
        NUM_HEADS = 16
        NUM_KV = 4
        KEY_DIM = EMBED_DIM // NUM_HEADS
        SCALE = 1.0 / float(KEY_DIM) ** 0.5
        key = jax.random.key(seed)
        ks = jax.random.split(key, 10)
        B, S, E = (4, 512, EMBED_DIM)
        kv_dim = KEY_DIM * NUM_KV
        return {'query': jax.random.normal(ks[0], (B, S, E), dtype=jnp.float32), 'key': jax.random.normal(ks[1], (B, S, E), dtype=jnp.float32), 'value': jax.random.normal(ks[2], (B, S, E), dtype=jnp.float32), 'session_deltas': jax.random.uniform(ks[3], (B, S), dtype=jnp.float32), 'mask': jnp.ones((B, S), dtype=jnp.float32), 'Wq': jax.random.normal(ks[4], (E, E), dtype=jnp.float32) * E ** (-0.5), 'Wk': jax.random.normal(ks[5], (E, kv_dim), dtype=jnp.float32) * E ** (-0.5), 'Wv': jax.random.normal(ks[6], (E, kv_dim), dtype=jnp.float32) * E ** (-0.5), 'Wo': jax.random.normal(ks[7], (E, E), dtype=jnp.float32) * E ** (-0.5), 'time_bias_weight': jax.random.normal(ks[8], ()) * 0.01}
    _L3_xattn_all = _L3_xattn_setup()
    _L3_xattn_in = {k: v for k, v in _L3_xattn_all.items() if k in ('Wq', 'Wk', 'Wv', 'Wo', 'time_bias_weight')}
    del _L3_xattn_all

    def _L3_ffn_setup():
        import jax, jax.numpy as jnp
        import numpy as np
        EMBED = 256
        D_FF = 4 * EMBED
        N_EXPERTS = 8
        TOP_K = 2
        B, S = (2, 256)
        key = jax.random.key(seed)
        ks = jax.random.split(key, 10)
        sc_d = 1.0 / np.sqrt(EMBED)
        sc_h = 1.0 / np.sqrt(D_FF)
        return {'inputs': jax.random.normal(ks[0], (B, S, EMBED), jnp.float32), 'rw1': jax.random.normal(ks[1], (EMBED, D_FF), jnp.float32) * sc_d, 'rb1': jnp.zeros((D_FF,), jnp.float32), 'rw2': jax.random.normal(ks[2], (D_FF, N_EXPERTS), jnp.float32) * sc_h, 'rb2': jnp.zeros((N_EXPERTS,), jnp.float32), 'W1': jax.random.normal(ks[3], (N_EXPERTS, EMBED, D_FF), jnp.float32) * sc_d, 'b1': jnp.zeros((N_EXPERTS, D_FF), jnp.float32), 'W2': jax.random.normal(ks[4], (N_EXPERTS, D_FF, EMBED), jnp.float32) * sc_h, 'b2': jnp.zeros((N_EXPERTS, EMBED), jnp.float32)}
    _L3_ffn_all = _L3_ffn_setup()
    _L3_ffn_in = {k: v for k, v in _L3_ffn_all.items() if k in ('rw1', 'rb1', 'rw2', 'rb2', 'W1', 'b1', 'W2', 'b2')}
    del _L3_ffn_all
    return {'x': x, 'ctx_1024': ctx_1024, 'fside_BxS2_0': fside_BxS2_0, 'mask_Bx1xSxS2_bk1': mask_Bx1xSxS2_bk1, 'mask_BxS2xS_ik0': mask_BxS2xS_ik0, 'mask_BxS2_ff1': mask_BxS2_ff1, 'L0_attn_ln1_w': _L0_attn_in['ln1_w'], 'L0_attn_ln2_w': _L0_attn_in['ln2_w'], 'L0_attn_time_decay': _L0_attn_in['time_decay'], 'L0_attn_time_first': _L0_attn_in['time_first'], 'L0_attn_time_mix_k': _L0_attn_in['time_mix_k'], 'L0_attn_time_mix_v': _L0_attn_in['time_mix_v'], 'L0_attn_time_mix_r': _L0_attn_in['time_mix_r'], 'L0_attn_W_key': _L0_attn_in['W_key'], 'L0_attn_W_value': _L0_attn_in['W_value'], 'L0_attn_W_recept': _L0_attn_in['W_recept'], 'L0_attn_W_out': _L0_attn_in['W_out'], 'L0_attn_time_mix_k2': _L0_attn_in['time_mix_k2'], 'L0_attn_time_mix_r2': _L0_attn_in['time_mix_r2'], 'L0_attn_W_key2': _L0_attn_in['W_key2'], 'L0_attn_W_value2': _L0_attn_in['W_value2'], 'L0_attn_W_recept2': _L0_attn_in['W_recept2'], 'L0_xattn_Wq': _L0_xattn_in['Wq'], 'L0_xattn_bq': _L0_xattn_in['bq'], 'L0_xattn_Wk': _L0_xattn_in['Wk'], 'L0_xattn_bk': _L0_xattn_in['bk'], 'L0_xattn_Wv': _L0_xattn_in['Wv'], 'L0_xattn_bv': _L0_xattn_in['bv'], 'L0_xattn_Wo': _L0_xattn_in['Wo'], 'L0_xattn_bo': _L0_xattn_in['bo'], 'L0_ffn_W_fc': _L0_ffn_in['W_fc'], 'L0_ffn_ln_w': _L0_ffn_in['ln_w'], 'L0_ffn_ln_b': _L0_ffn_in['ln_b'], 'L0_ffn_W_proj': _L0_ffn_in['W_proj'], 'L1_attn_W_attn': _L1_attn_in['W_attn'], 'L1_attn_b_attn': _L1_attn_in['b_attn'], 'L1_attn_W_proj': _L1_attn_in['W_proj'], 'L1_attn_b_proj': _L1_attn_in['b_proj'], 'L1_xattn_w_qk': _L1_xattn_in['w_qk'], 'L1_xattn_b_qk': _L1_xattn_in['b_qk'], 'L1_xattn_w_value': _L1_xattn_in['w_value'], 'L1_xattn_b_value': _L1_xattn_in['b_value'], 'L1_xattn_w_off': _L1_xattn_in['w_off'], 'L1_xattn_b_off': _L1_xattn_in['b_off'], 'L1_xattn_w_attw': _L1_xattn_in['w_attw'], 'L1_xattn_b_attw': _L1_xattn_in['b_attw'], 'L1_xattn_w_out': _L1_xattn_in['w_out'], 'L1_xattn_b_out': _L1_xattn_in['b_out'], 'L1_ffn_router_w': _L1_ffn_in['router_w'], 'L1_ffn_router_b': _L1_ffn_in['router_b'], 'L1_ffn_routed_w1': _L1_ffn_in['routed_w1'], 'L1_ffn_routed_w3': _L1_ffn_in['routed_w3'], 'L1_ffn_routed_w2': _L1_ffn_in['routed_w2'], 'L1_ffn_shared_w1': _L1_ffn_in['shared_w1'], 'L1_ffn_shared_w3': _L1_ffn_in['shared_w3'], 'L1_ffn_shared_w2': _L1_ffn_in['shared_w2'], 'L2_attn_Wq': _L2_attn_in['Wq'], 'L2_attn_Wk': _L2_attn_in['Wk'], 'L2_attn_Wv': _L2_attn_in['Wv'], 'L2_attn_Wo': _L2_attn_in['Wo'], 'L2_attn_bq': _L2_attn_in['bq'], 'L2_attn_bk': _L2_attn_in['bk'], 'L2_attn_bv': _L2_attn_in['bv'], 'L2_attn_bo': _L2_attn_in['bo'], 'L2_xattn_ln_w': _L2_xattn_in['ln_w'], 'L2_xattn_ln_b': _L2_xattn_in['ln_b'], 'L2_xattn_Wq': _L2_xattn_in['Wq'], 'L2_xattn_Wkv': _L2_xattn_in['Wkv'], 'L2_xattn_Wout': _L2_xattn_in['Wout'], 'L2_ffn_ln1_g': _L2_ffn_in['ln1_g'], 'L2_ffn_ln1_b': _L2_ffn_in['ln1_b'], 'L2_ffn_ln2_g': _L2_ffn_in['ln2_g'], 'L2_ffn_ln2_b': _L2_ffn_in['ln2_b'], 'L2_ffn_wq': _L2_ffn_in['wq'], 'L2_ffn_bq': _L2_ffn_in['bq'], 'L2_ffn_wk': _L2_ffn_in['wk'], 'L2_ffn_bk': _L2_ffn_in['bk'], 'L2_ffn_wv': _L2_ffn_in['wv'], 'L2_ffn_bv': _L2_ffn_in['bv'], 'L2_ffn_wo': _L2_ffn_in['wo'], 'L2_ffn_bo': _L2_ffn_in['bo'], 'L2_ffn_gate_w': _L2_ffn_in['gate_w'], 'L2_ffn_gate_b': _L2_ffn_in['gate_b'], 'L2_ffn_w1': _L2_ffn_in['w1'], 'L2_ffn_b1': _L2_ffn_in['b1'], 'L2_ffn_w2': _L2_ffn_in['w2'], 'L2_ffn_b2': _L2_ffn_in['b2'], 'L3_attn_Wv': _L3_attn_in['Wv'], 'L3_attn_bv': _L3_attn_in['bv'], 'L3_attn_Wg': _L3_attn_in['Wg'], 'L3_attn_bg': _L3_attn_in['bg'], 'L3_attn_Win': _L3_attn_in['Win'], 'L3_attn_bin_': _L3_attn_in['bin_'], 'L3_attn_Wout': _L3_attn_in['Wout'], 'L3_attn_bout': _L3_attn_in['bout'], 'L3_attn_g_qq': _L3_attn_in['g_qq'], 'L3_attn_b_qq': _L3_attn_in['b_qq'], 'L3_attn_g_qk': _L3_attn_in['g_qk'], 'L3_attn_b_qk': _L3_attn_in['b_qk'], 'L3_attn_g_lq': _L3_attn_in['g_lq'], 'L3_attn_b_lq': _L3_attn_in['b_lq'], 'L3_attn_g_lk': _L3_attn_in['g_lk'], 'L3_attn_b_lk': _L3_attn_in['b_lk'], 'L3_xattn_Wq': _L3_xattn_in['Wq'], 'L3_xattn_Wk': _L3_xattn_in['Wk'], 'L3_xattn_Wv': _L3_xattn_in['Wv'], 'L3_xattn_Wo': _L3_xattn_in['Wo'], 'L3_xattn_time_bias_weight': _L3_xattn_in['time_bias_weight'], 'L3_ffn_rw1': _L3_ffn_in['rw1'], 'L3_ffn_rb1': _L3_ffn_in['rb1'], 'L3_ffn_rw2': _L3_ffn_in['rw2'], 'L3_ffn_rb2': _L3_ffn_in['rb2'], 'L3_ffn_W1': _L3_ffn_in['W1'], 'L3_ffn_b1': _L3_ffn_in['b1'], 'L3_ffn_W2': _L3_ffn_in['W2'], 'L3_ffn_b2': _L3_ffn_in['b2']}

def reference(x, ctx_1024, fside_BxS2_0, mask_Bx1xSxS2_bk1, mask_BxS2xS_ik0, mask_BxS2_ff1, L0_attn_ln1_w, L0_attn_ln2_w, L0_attn_time_decay, L0_attn_time_first, L0_attn_time_mix_k, L0_attn_time_mix_v, L0_attn_time_mix_r, L0_attn_W_key, L0_attn_W_value, L0_attn_W_recept, L0_attn_W_out, L0_attn_time_mix_k2, L0_attn_time_mix_r2, L0_attn_W_key2, L0_attn_W_value2, L0_attn_W_recept2, L0_xattn_Wq, L0_xattn_bq, L0_xattn_Wk, L0_xattn_bk, L0_xattn_Wv, L0_xattn_bv, L0_xattn_Wo, L0_xattn_bo, L0_ffn_W_fc, L0_ffn_ln_w, L0_ffn_ln_b, L0_ffn_W_proj, L1_attn_W_attn, L1_attn_b_attn, L1_attn_W_proj, L1_attn_b_proj, L1_xattn_w_qk, L1_xattn_b_qk, L1_xattn_w_value, L1_xattn_b_value, L1_xattn_w_off, L1_xattn_b_off, L1_xattn_w_attw, L1_xattn_b_attw, L1_xattn_w_out, L1_xattn_b_out, L1_ffn_router_w, L1_ffn_router_b, L1_ffn_routed_w1, L1_ffn_routed_w3, L1_ffn_routed_w2, L1_ffn_shared_w1, L1_ffn_shared_w3, L1_ffn_shared_w2, L2_attn_Wq, L2_attn_Wk, L2_attn_Wv, L2_attn_Wo, L2_attn_bq, L2_attn_bk, L2_attn_bv, L2_attn_bo, L2_xattn_ln_w, L2_xattn_ln_b, L2_xattn_Wq, L2_xattn_Wkv, L2_xattn_Wout, L2_ffn_ln1_g, L2_ffn_ln1_b, L2_ffn_ln2_g, L2_ffn_ln2_b, L2_ffn_wq, L2_ffn_bq, L2_ffn_wk, L2_ffn_bk, L2_ffn_wv, L2_ffn_bv, L2_ffn_wo, L2_ffn_bo, L2_ffn_gate_w, L2_ffn_gate_b, L2_ffn_w1, L2_ffn_b1, L2_ffn_w2, L2_ffn_b2, L3_attn_Wv, L3_attn_bv, L3_attn_Wg, L3_attn_bg, L3_attn_Win, L3_attn_bin_, L3_attn_Wout, L3_attn_bout, L3_attn_g_qq, L3_attn_b_qq, L3_attn_g_qk, L3_attn_b_qk, L3_attn_g_lq, L3_attn_b_lq, L3_attn_g_lk, L3_attn_b_lk, L3_xattn_Wq, L3_xattn_Wk, L3_xattn_Wv, L3_xattn_Wo, L3_xattn_time_bias_weight, L3_ffn_rw1, L3_ffn_rb1, L3_ffn_rw2, L3_ffn_rb2, L3_ffn_W1, L3_ffn_b1, L3_ffn_W2, L3_ffn_b2):
    import jax
    import jax.numpy as jnp

    def _L0_attn_ref(x, ln1_w, ln2_w, time_decay, time_first, time_mix_k, time_mix_v, time_mix_r, W_key, W_value, W_recept, W_out, time_mix_k2, time_mix_r2, W_key2, W_value2, W_recept2):
        import jax, jax.numpy as jnp
        import numpy as np
        B, T, C, I = (4, 1024, 256, 1024)

        def rmsnorm(x, w, eps=1e-06):
            return x * jax.lax.rsqrt(jnp.mean(x * x, axis=-1, keepdims=True) + eps) * w

        def shift(h):
            return jnp.pad(h, ((0, 0), (1, 0), (0, 0)))[:, :-1]

        def wkv_scan(k, v, w, u):
            ew = jnp.exp(jnp.clip(w, -20.0, 20.0))

            def step(carry, kv):
                a, b = carry
                kt, vt = kv
                ekt = jnp.exp(jnp.clip(u + kt, -20.0, 20.0))
                out = (a + ekt * vt) / (b + ekt + 1e-08)
                ek = jnp.exp(jnp.clip(kt, -20.0, 20.0))
                return ((ew * a + ek * vt, ew * b + ek), out)
            init = (jnp.zeros((k.shape[0], k.shape[2]), jnp.float32), jnp.zeros((k.shape[0], k.shape[2]), jnp.float32))
            _, out = jax.lax.scan(step, init, (k.swapaxes(0, 1), v.swapaxes(0, 1)))
            return out.swapaxes(0, 1)
        h = rmsnorm(x, ln1_w)
        sh = shift(h)
        xk = h * time_mix_k + sh * (1 - time_mix_k)
        xv = h * time_mix_v + sh * (1 - time_mix_v)
        xr = h * time_mix_r + sh * (1 - time_mix_r)
        k = xk @ W_key
        v = xv @ W_value
        r = jax.nn.sigmoid(xr @ W_recept)
        w = -jnp.exp(time_decay)
        u = time_first
        wkv = wkv_scan(k.astype(jnp.float32), v.astype(jnp.float32), w, u).astype(x.dtype)
        x = x + r * wkv @ W_out
        h = rmsnorm(x, ln2_w)
        sh = shift(h)
        xk = h * time_mix_k2 + sh * (1 - time_mix_k2)
        xr = h * time_mix_r2 + sh * (1 - time_mix_r2)
        k2 = jnp.square(jax.nn.relu(xk @ W_key2))
        r2 = jax.nn.sigmoid(xr @ W_recept2)
        return x + r2 * (k2 @ W_value2)

    def _L0_xattn_ref(queries, keys, values, mask, Wq, bq, Wk, bk, Wv, bv, Wo, bo):
        import jax, jax.numpy as jnp
        import numpy as np
        B, S, D, H = (4, 512, 256, 16)
        HD = D // H
        b, sq, d = queries.shape

        def split_heads(x):
            return x.reshape(b, x.shape[1], H, HD).transpose(0, 2, 1, 3)
        q = split_heads(queries @ Wq + bq)
        k = split_heads(keys @ Wk + bk)
        v = split_heads(values @ Wv + bv)
        scores = jnp.einsum('bhqd,bhkd->bhqk', q, k) / jnp.sqrt(jnp.float32(HD))
        scores = jnp.where(mask, jnp.float32(-1000000000000000.0), scores)
        attn = jax.nn.softmax(scores, axis=-1)
        ctx = jnp.einsum('bhqk,bhkd->bhqd', attn, v)
        ctx = ctx.transpose(0, 2, 1, 3).reshape(b, sq, d)
        return ctx @ Wo + bo

    def _L0_ffn_ref(x, W_fc, ln_w, ln_b, W_proj):
        import jax, jax.numpy as jnp
        import numpy as np
        EPS = 1e-06
        LN_EPS = 1e-05

        def _absmean_core(W):
            gamma = jnp.mean(jnp.abs(W)) + EPS
            Ws = W / gamma
            Wq = jnp.sign(Ws) * jnp.minimum(jnp.round(jnp.abs(Ws)), 1.0)
            return (Wq, gamma)

        @jax.custom_vjp
        def absmean(W):
            return _absmean_core(W)[0]

        def _absmean_fwd(W):
            Wq, gamma = _absmean_core(W)
            return (Wq, gamma)

        def _absmean_bwd(gamma, g):
            return (g / gamma,)
        absmean.defvjp(_absmean_fwd, _absmean_bwd)

        def layernorm(x, w, b, eps=LN_EPS):
            mu = jnp.mean(x, axis=-1, keepdims=True)
            var = jnp.mean((x - mu) ** 2, axis=-1, keepdims=True)
            return (x - mu) * jax.lax.rsqrt(var + eps) * w + b
        h = jnp.einsum('btd,hd->bth', x, absmean(W_fc))
        h = jax.nn.gelu(h, approximate=False)
        h = layernorm(h, ln_w, ln_b)
        return jnp.einsum('bth,dh->btd', h, absmean(W_proj))

    def _L1_attn_ref(x, W_attn, b_attn, W_proj, b_proj):
        import jax, jax.numpy as jnp
        import numpy as np
        import math
        N_HEAD = 16
        ROPE_BASE = 10000.0

        def _rope_as_in_source(x):
            B, H, T, hd = x.shape
            theta = 1.0 / ROPE_BASE ** (jnp.arange(0, hd, 2, dtype=jnp.float32) / hd)
            ang = jnp.arange(H, dtype=jnp.float32)[:, None] * theta[None, :]
            cos = jnp.cos(ang)[None, :, None, :]
            sin = jnp.sin(ang)[None, :, None, :]
            xr = x.reshape(B, H, T, hd // 2, 2)
            out = jnp.stack([xr[..., 0] * cos - xr[..., 1] * sin, xr[..., 1] * cos + xr[..., 0] * sin], axis=-1)
            return out.reshape(B, H, T, hd)
        B, T, C = x.shape
        H = N_HEAD
        hd = C // H
        qkv = x @ W_attn + b_attn
        q, k, v = jnp.split(qkv, 3, axis=2)
        q = q.reshape(B, T, H, hd).transpose(0, 2, 1, 3)
        k = k.reshape(B, T, H, hd).transpose(0, 2, 1, 3)
        v = v.reshape(B, T, H, hd).transpose(0, 2, 1, 3)
        q = _rope_as_in_source(q)
        k = _rope_as_in_source(k)
        att = jnp.einsum('bhqd,bhkd->bhqk', q, k) * (1.0 / math.sqrt(hd))
        causal = jnp.tril(jnp.ones((T, T), dtype=bool))
        att = jnp.where(causal[None, None, :, :], att, -jnp.inf)
        att = jax.nn.softmax(att, axis=-1)
        y = jnp.einsum('bhqk,bhkd->bhqd', att, v)
        y = y.transpose(0, 2, 1, 3).reshape(B, T, C)
        return y @ W_proj + b_proj

    def _L1_xattn_ref(query, key, value, w_qk, b_qk, w_value, b_value, w_off, b_off, w_attw, b_attw, w_out, b_out):
        import jax, jax.numpy as jnp
        import numpy as np
        H, P = (16, 4)
        B, L, D = value.shape
        Dh = D // H
        _qk = query @ w_qk + b_qk
        v = (value @ w_value + b_value).reshape(B, L, H, Dh).transpose(0, 2, 1, 3)
        off = (query @ w_off + b_off).reshape(B, L, H, P, 2)
        attw = jax.nn.softmax((query @ w_attw + b_attw).reshape(B, L, H, P), axis=-1)
        ref_y = jnp.linspace(0.0, 1.0, L)
        sx = jnp.clip(off[..., 0], 0.0, 1.0)
        sy = jnp.clip(ref_y[None, :, None, None] + off[..., 1], 0.0, 1.0)
        ix = ((sx + 1.0) * L - 1.0) * 0.5
        iy = ((sy + 1.0) * 1.0 - 1.0) * 0.5
        x0 = jnp.floor(ix)
        fx = ix - x0
        x0i = x0.astype(jnp.int32)
        x1i = x0i + 1
        m0 = ((x0i >= 0) & (x0i < L)).astype(v.dtype)
        m1 = ((x1i >= 0) & (x1i < L)).astype(v.dtype)
        y0 = jnp.floor(iy)
        fy = iy - y0
        hy = jnp.where(y0 == 0.0, 1.0 - fy, 0.0) + jnp.where(y0 == -1.0, fy, 0.0)
        tr = lambda a: a.transpose(0, 2, 1, 3)

        def gather(idx):
            idxc = jnp.clip(idx, 0, L - 1).reshape(B, H, L * P, 1)
            return jnp.take_along_axis(v, idxc, axis=2).reshape(B, H, L, P, Dh)
        val0 = gather(tr(x0i))
        val1 = gather(tr(x1i))
        wx0 = tr((1.0 - fx) * m0 * hy)
        wx1 = tr(fx * m1 * hy)
        sampled = val0 * wx0[..., None] + val1 * wx1[..., None]
        out = jnp.einsum('bhlpd,bhlp->blhd', sampled, tr(attw)).reshape(B, L, D)
        return out @ w_out + b_out

    def _L1_ffn_ref(x, router_w, router_b, routed_w1, routed_w3, routed_w2, shared_w1, shared_w3, shared_w2):
        import jax, jax.numpy as jnp
        import numpy as np
        BEST_K = 2

        def _expert(xf, w1, w3, w2):
            return jax.nn.silu(xf @ w1) * (xf @ w3) @ w2
        B, S, D = x.shape
        T = B * S
        xf = x.reshape(T, D)
        logits = xf @ router_w + router_b
        topk_vals, topk_idx = jax.lax.top_k(logits, BEST_K)
        sparse = jnp.full_like(logits, -jnp.inf)
        sparse = sparse.at[jnp.arange(T)[:, None], topk_idx].set(topk_vals)
        gates = jax.nn.softmax(sparse, axis=-1)
        routed = jax.vmap(_expert, in_axes=(None, 0, 0, 0))(xf, routed_w1, routed_w3, routed_w2)
        routed_out = jnp.einsum('etd,te->td', routed, gates)
        shared_out = jax.vmap(_expert, in_axes=(None, 0, 0, 0))(xf, shared_w1, shared_w3, shared_w2).sum(axis=0)
        return (routed_out + shared_out).reshape(B, S, D)

    def _L2_attn_ref(residual, Wq, Wk, Wv, Wo, bq, bk, bv, bo):
        import jax, jax.numpy as jnp
        import numpy as np
        B, S, D, H, A = (2, 512, 256, 16, 64)
        INIT_STD = 0.02
        q = jnp.einsum('bsd,hda->bhsa', residual, Wq) + bq[None, :, None, :]
        k = jnp.einsum('bsd,hda->bhsa', residual, Wk) + bk[None, :, None, :]
        v = jnp.einsum('bsd,hda->bhsa', residual, Wv) + bv[None, :, None, :]
        scale = 1.0 / jnp.sqrt(jnp.float32(q.shape[-1]))
        scores = jnp.einsum('bhsa,bhta->bhst', q, k) * scale
        s = scores.shape[-1]
        causal = jnp.tril(jnp.ones((s, s), dtype=bool))
        masked = jnp.where(causal, scores, jnp.float32(-100000.0))
        pattern = jax.nn.softmax(masked, axis=-1)
        z = jnp.einsum('bhst,bhta->bshа'.replace('а', 'a'), pattern, v)
        out = jnp.einsum('bsha,had->bsd', z, Wo) + bo
        return out

    def _L2_xattn_ref(x, vision, ln_w, ln_b, Wq, Wkv, Wout, attention_mask, num_support):
        import jax, jax.numpy as jnp
        import numpy as np
        B, T, V, C = (32, 64, 250, 256)
        H, DH = (8, 64)
        INNER = H * DH
        K = 5
        SCALE = DH ** (-0.5)

        def layer_norm(x, w, b, eps=1e-05):
            mu = jnp.mean(x, axis=-1, keepdims=True)
            var = jnp.mean(jnp.square(x - mu), axis=-1, keepdims=True)
            return (x - mu) * jax.lax.rsqrt(var + eps) * w + b
        Bb, Tt, Cc = x.shape
        Vv = vision.shape[1]
        am_t = jnp.transpose(attention_mask, (0, 2, 1))
        idxs = jnp.where(am_t != 0, jnp.arange(Vv, dtype=jnp.int32), Vv)
        padded = -jax.lax.top_k(-idxs, num_support)[0]
        vision_pad = jnp.concatenate([vision, jnp.zeros((Bb, 1, Cc), vision.dtype)], axis=1)
        vg = vision_pad[jnp.arange(Bb)[:, None, None], padded]
        valid = padded != Vv
        xn = layer_norm(x, ln_w, ln_b)
        q = jnp.einsum('btc,ce->bte', xn, Wq) * SCALE
        kv = jnp.einsum('btkc,ce->btke', vg, Wkv)
        k, v = jnp.split(kv, 2, axis=-1)
        qh = q.reshape(Bb, Tt, H, DH)
        kh = k.reshape(Bb, Tt, num_support, H, DH)
        vh = v.reshape(Bb, Tt, num_support, H, DH)
        sim = jnp.einsum('bthd,btkhd->bthk', qh, kh)
        sim = sim + jnp.where(valid, 0.0, -10000.0)[:, :, None, :]
        attn = jax.nn.softmax(sim, axis=-1)
        attn = attn * valid[:, :, None, :].astype(attn.dtype)
        out = jnp.einsum('bthk,btkhd->bthd', attn, vh).reshape(Bb, Tt, INNER)
        return jnp.einsum('bte,ec->btc', out, Wout)

    def _L2_ffn_ref(x, ln1_g, ln1_b, ln2_g, ln2_b, wq, bq, wk, bk, wv, bv, wo, bo, gate_w, gate_b, w1, b1, w2, b2):
        import jax, jax.numpy as jnp
        import numpy as np
        B, S, H, NH, E, F = (4, 256, 256, 16, 8, 1024)
        D = H // NH
        EPS = 1e-05

        def _layernorm(x, g, b):
            mu = jnp.mean(x, axis=-1, keepdims=True)
            var = jnp.var(x, axis=-1, keepdims=True)
            return (x - mu) * jax.lax.rsqrt(var + EPS) * g + b
        b, s, h = x.shape
        hn = _layernorm(x, ln1_g, ln1_b)
        q = (hn @ wq + bq).reshape(b, s, NH, D).transpose(0, 2, 1, 3)
        k = (hn @ wk + bk).reshape(b, s, NH, D).transpose(0, 2, 1, 3)
        v = (hn @ wv + bv).reshape(b, s, NH, D).transpose(0, 2, 1, 3)
        scores = jnp.einsum('bhqd,bhkd->bhqk', q, k) / jnp.sqrt(jnp.float32(D))
        attn = jax.nn.softmax(scores, axis=-1)
        o = jnp.einsum('bhqk,bhkd->bhqd', attn, v)
        o = o.transpose(0, 2, 1, 3).reshape(b, s, h)
        x = x + (o @ wo + bo)
        hn2 = _layernorm(x, ln2_g, ln2_b).reshape(-1, h)
        logits = hn2 @ gate_w + gate_b
        idx = jnp.argmax(logits, axis=-1)
        mid = jax.nn.relu(jnp.einsum('th,ehf->etf', hn2, w1) + b1[:, None, :])
        y = jnp.einsum('etf,efh->eth', mid, w2) + b2[:, None, :]
        moe = y[idx, jnp.arange(hn2.shape[0])]
        return x + moe.reshape(b, s, h)

    def _L3_attn_ref(x, Wv, bv, Wg, bg, Win, bin_, Wout, bout, g_qq, b_qq, g_qk, b_qk, g_lq, b_lq, g_lk, b_lk):
        import jax, jax.numpy as jnp
        import numpy as np
        B, S, D = (4, 1024, 256)
        GROUP = 64
        HEAD = 128
        INNER = 512
        b, s, d = x.shape
        g = s // GROUP
        xc = x.reshape(b, g, GROUP, d)
        v = jax.nn.silu(xc @ Wv + bv)
        gate = jax.nn.silu(xc @ Wg + bg)
        x_ = jax.nn.silu(xc @ Win + bin_)
        quad_q = x_ * g_qq + b_qq
        quad_k = x_ * g_qk + b_qk
        lin_q = x_ * g_lq + b_lq
        lin_k = x_ * g_lk + b_lk
        scale = jnp.asarray(INNER ** 0.5, x.dtype)
        attn = jnp.einsum('bgns,bgms->bgnm', quad_q, quad_k) / scale
        causal_mask = jnp.triu(jnp.ones((GROUP, GROUP), bool), 1)
        attn = jnp.where(causal_mask, 0.0, attn)
        attn = jnp.square(jax.nn.relu(attn))
        v_quad = jnp.einsum('bgnm,bgme->bgne', attn, v)
        kv = jnp.einsum('bgcs,bgce->bgse', lin_k, v)
        kv = jnp.cumsum(kv, axis=1) - kv
        v_lin = jnp.einsum('bgcs,bgse->bgce', lin_q, kv)
        o = (v_quad + v_lin) * gate
        o = o @ Wout + bout
        return o.reshape(b, s, d)

    def _L3_xattn_ref(query, key, value, session_deltas, mask, Wq, Wk, Wv, Wo, time_bias_weight):
        import jax, jax.numpy as jnp
        import numpy as np
        EMBED_DIM = 256
        NUM_HEADS = 16
        NUM_KV = 4
        KEY_DIM = EMBED_DIM // NUM_HEADS
        SCALE = 1.0 / float(KEY_DIM) ** 0.5
        B, S, E = query.shape
        H, G, D = (NUM_HEADS, NUM_KV, KEY_DIM)
        n_rep = H // G
        q = (query @ Wq).reshape(B, S, H, D).transpose(0, 2, 1, 3)
        k = (key @ Wk).reshape(B, S, G, D).transpose(0, 2, 1, 3)
        v = (value @ Wv).reshape(B, S, G, D).transpose(0, 2, 1, 3)
        k_rep = jnp.repeat(k, n_rep, axis=1)
        v_rep = jnp.repeat(v, n_rep, axis=1)
        scores = jnp.einsum('bhqd,bhkd->bhqk', q, k_rep) * SCALE
        ct = jnp.cumsum(session_deltas, axis=1)
        pairwise_delta = jnp.abs(ct[:, :, None] - ct[:, None, :])
        time_bias = time_bias_weight * jnp.log1p(pairwise_delta)
        scores = scores + time_bias[:, None, :, :]
        scores = scores + (1.0 - mask[:, None, None, :].astype(scores.dtype)) * -1000000000.0
        w = jax.nn.softmax(scores, axis=-1)
        out = jnp.einsum('bhqk,bhkd->bhqd', w, v_rep)
        out = out.transpose(0, 2, 1, 3).reshape(B, S, E)
        return out @ Wo

    def _L3_ffn_ref(inputs, rw1, rb1, rw2, rb2, W1, b1, W2, b2):
        import jax, jax.numpy as jnp
        import numpy as np
        EMBED = 256
        D_FF = 4 * EMBED
        N_EXPERTS = 8
        TOP_K = 2
        B, S = (2, 256)
        Bb, Ss, D = inputs.shape
        T = Bb * Ss
        xf = inputs.reshape(T, D)
        score = jax.nn.relu(xf @ rw1 + rb1) @ rw2 + rb2
        _, topi = jax.lax.top_k(score, TOP_K)
        mask = jnp.zeros(score.shape, bool).at[jnp.arange(T)[:, None], topi].set(True)
        gate = jax.nn.softmax(jnp.where(mask, score, -jnp.inf), axis=-1)
        out = jnp.zeros_like(xf)
        for e in range(N_EXPERTS):
            h = jax.nn.relu(xf @ W1[e] + b1[e])
            y = h @ W2[e] + b2[e]
            out = out + gate[:, e:e + 1] * y
        return out.reshape(Bb, Ss, D)
    x = x + _L0_attn_ref(_layernorm(x, axis=-1), L0_attn_ln1_w, L0_attn_ln2_w, L0_attn_time_decay, L0_attn_time_first, L0_attn_time_mix_k, L0_attn_time_mix_v, L0_attn_time_mix_r, L0_attn_W_key, L0_attn_W_value, L0_attn_W_recept, L0_attn_W_out, L0_attn_time_mix_k2, L0_attn_time_mix_r2, L0_attn_W_key2, L0_attn_W_value2, L0_attn_W_recept2)
    x = x + _L0_xattn_ref(_layernorm(x, axis=-1), ctx_1024, ctx_1024, mask_Bx1xSxS2_bk1, L0_xattn_Wq, L0_xattn_bq, L0_xattn_Wk, L0_xattn_bk, L0_xattn_Wv, L0_xattn_bv, L0_xattn_Wo, L0_xattn_bo)
    x = x + _L0_ffn_ref(_layernorm(x, axis=-1), L0_ffn_W_fc, L0_ffn_ln_w, L0_ffn_ln_b, L0_ffn_W_proj)
    x = x + _L1_attn_ref(_layernorm(x, axis=-1), L1_attn_W_attn, L1_attn_b_attn, L1_attn_W_proj, L1_attn_b_proj)
    x = x + _L1_xattn_ref(_layernorm(x, axis=-1), ctx_1024, ctx_1024, L1_xattn_w_qk, L1_xattn_b_qk, L1_xattn_w_value, L1_xattn_b_value, L1_xattn_w_off, L1_xattn_b_off, L1_xattn_w_attw, L1_xattn_b_attw, L1_xattn_w_out, L1_xattn_b_out)
    x = x + _L1_ffn_ref(_layernorm(x, axis=-1), L1_ffn_router_w, L1_ffn_router_b, L1_ffn_routed_w1, L1_ffn_routed_w3, L1_ffn_routed_w2, L1_ffn_shared_w1, L1_ffn_shared_w3, L1_ffn_shared_w2)
    x = x + _L2_attn_ref(_layernorm(x, axis=-1), L2_attn_Wq, L2_attn_Wk, L2_attn_Wv, L2_attn_Wo, L2_attn_bq, L2_attn_bk, L2_attn_bv, L2_attn_bo)
    x = x + _L2_xattn_ref(_layernorm(x, axis=-1), ctx_1024, L2_xattn_ln_w, L2_xattn_ln_b, L2_xattn_Wq, L2_xattn_Wkv, L2_xattn_Wout, mask_BxS2xS_ik0, 5)
    x = x + _L2_ffn_ref(_layernorm(x, axis=-1), L2_ffn_ln1_g, L2_ffn_ln1_b, L2_ffn_ln2_g, L2_ffn_ln2_b, L2_ffn_wq, L2_ffn_bq, L2_ffn_wk, L2_ffn_bk, L2_ffn_wv, L2_ffn_bv, L2_ffn_wo, L2_ffn_bo, L2_ffn_gate_w, L2_ffn_gate_b, L2_ffn_w1, L2_ffn_b1, L2_ffn_w2, L2_ffn_b2)
    x = x + _L3_attn_ref(_layernorm(x, axis=-1), L3_attn_Wv, L3_attn_bv, L3_attn_Wg, L3_attn_bg, L3_attn_Win, L3_attn_bin_, L3_attn_Wout, L3_attn_bout, L3_attn_g_qq, L3_attn_b_qq, L3_attn_g_qk, L3_attn_b_qk, L3_attn_g_lq, L3_attn_b_lq, L3_attn_g_lk, L3_attn_b_lk)
    x = x + _L3_xattn_ref(_layernorm(x, axis=-1), ctx_1024, ctx_1024, fside_BxS2_0, mask_BxS2_ff1, L3_xattn_Wq, L3_xattn_Wk, L3_xattn_Wv, L3_xattn_Wo, L3_xattn_time_bias_weight)
    x = x + _L3_ffn_ref(_layernorm(x, axis=-1), L3_ffn_rw1, L3_ffn_rb1, L3_ffn_rw2, L3_ffn_rb2, L3_ffn_W1, L3_ffn_b1, L3_ffn_W2, L3_ffn_b2)
    return x

_drawn_inputs = setup_inputs


def setup_inputs(seed=0):
    import zlib

    import numpy as np

    out = dict(_drawn_inputs(seed))
    spreads = {'L0_attn_ln1_w': (1.0, 0.2),
     'L0_attn_ln2_w': (1.0, 0.2),
     'L0_attn_time_mix_k': (0.5, 0.2),
     'L0_attn_time_mix_v': (0.5, 0.2),
     'L0_attn_time_mix_r': (0.5, 0.2),
     'L0_attn_time_mix_k2': (0.5, 0.2),
     'L0_attn_time_mix_r2': (0.5, 0.2),
     'L0_xattn_bq': (0.0, 0.1),
     'L0_xattn_bk': (0.0, 0.1),
     'L0_xattn_bv': (0.0, 0.1),
     'L0_xattn_bo': (0.0, 0.1),
     'L0_ffn_ln_w': (1.0, 0.2),
     'L0_ffn_ln_b': (0.0, 0.1),
     'L1_attn_b_attn': (0.0, 0.1),
     'L1_attn_b_proj': (0.0, 0.1),
     'L1_xattn_b_qk': (0.0, 0.1),
     'L1_xattn_b_value': (0.0, 0.1),
     'L1_xattn_b_attw': (0.0, 0.1),
     'L1_xattn_b_out': (0.0, 0.1),
     'L1_ffn_router_b': (0.0, 0.1),
     'L2_attn_bq': (0.0, 0.1),
     'L2_attn_bk': (0.0, 0.1),
     'L2_attn_bv': (0.0, 0.1),
     'L2_attn_bo': (0.0, 0.1),
     'L2_xattn_ln_w': (1.0, 0.2),
     'L2_xattn_ln_b': (0.0, 0.1),
     'L2_ffn_ln1_g': (1.0, 0.2),
     'L2_ffn_ln1_b': (0.0, 0.1),
     'L2_ffn_ln2_g': (1.0, 0.2),
     'L2_ffn_ln2_b': (0.0, 0.1),
     'L2_ffn_bq': (0.0, 0.1),
     'L2_ffn_bk': (0.0, 0.1),
     'L2_ffn_bv': (0.0, 0.1),
     'L2_ffn_bo': (0.0, 0.1),
     'L2_ffn_gate_b': (0.0, 0.1),
     'L2_ffn_b1': (0.0, 0.1),
     'L2_ffn_b2': (0.0, 0.1),
     'L3_attn_bv': (0.0, 0.1),
     'L3_attn_bg': (0.0, 0.1),
     'L3_attn_bin_': (0.0, 0.1),
     'L3_attn_bout': (0.0, 0.1),
     'L3_attn_b_qq': (0.0, 0.1),
     'L3_attn_b_qk': (0.0, 0.1),
     'L3_attn_b_lq': (0.0, 0.1),
     'L3_attn_b_lk': (0.0, 0.1),
     'L3_ffn_rb1': (0.0, 0.1),
     'L3_ffn_rb2': (0.0, 0.1),
     'L3_ffn_b1': (0.0, 0.1),
     'L3_ffn_b2': (0.0, 0.1)}
    factors = {}
    for name, (base, spread) in spreads.items():
        noise = np.random.default_rng([zlib.crc32(name.encode()), seed]).standard_normal(out[name].shape)
        drawn = base * np.exp(spread * noise) if base else spread * noise
        out[name] = jnp.asarray(drawn.astype(out[name].dtype))
    for name, factor in factors.items():
        out[name] = (out[name] * factor).astype(out[name].dtype)
    return out
```

```python
import concourse.bass as bass
from concourse import mybir
from contextlib import ExitStack

F32 = mybir.dt.float32
U8 = mybir.dt.uint8
I32 = mybir.dt.int32
ALU = mybir.AluOpType
ACT = mybir.ActivationFunctionType
AX = mybir.AxisListType

P = 128
NB = 16
D = 256
KC = D // P
GR = 4
NG = NB // GR
TG = GR * P
ARENA = 8192
VECS = 2560
LEAD = 2
FMAX = 3.0e38
LN_EPS = 1e-5

STAGES = range(0, 12)


def done(n):
    return n + (1 + LEAD)


class Chip:

    def __init__(self, nc, ins, out, ctx):
        self.nc, self.ins, self.out, self.ctx = nc, ins, out, ctx
        self.block_sems = []
        self.X = self.sb("X", [P, NB, D])
        self.ident = self.sb("ident", [P, P])
        self.upper = self.sb("upper", [P, P])
        self.causal = self.sb("causal", [P, P])
        self.ones = self.sb("ones", [P, TG])
        self.block_of = {hd: self.sb(f"block_of_{hd}", [P, P // hd]) for hd in (16, 64)}
        self.arena = [self.sb("arena0", [P, ARENA]), self.sb("arena1", [P, ARENA])]
        self.vecs = [self.sb("vecs0", [P, VECS]), self.sb("vecs1", [P, VECS])]
        self.bn = self.sb("bn", [P, NB, 6])
        self.mv = self.sb("mv", [P, NB, 2])
        self.var = self.sb("var", [P, NB])
        self.std = self.sb("std", [P, NB])
        self.rstd = self.sb("rstd", [P, NB])
        self.rstd2 = self.sb("rstd2", [P, NB])

    def sb(self, name, shape, dt=F32, ctx=None):
        return (ctx or self.ctx).enter_context(self.nc.sbuf_tensor(name, shape, dt))

    def ps(self, name, ctx, cols=512):
        return ctx.enter_context(self.nc.psum_tensor(name, [P, cols], F32))

    def sem(self, name):
        self.block_sems.append(self.nc.alloc_semaphore(name=name))
        return self.block_sems[-1]

    def lasting_sem(self, name):
        return self.ctx.enter_context(self.nc.semaphore(name))

    def end_block(self):
        self.nc.clear_and_free_semaphores(self.block_sems)
        self.block_sems = []
        self.nc.all_engine_barrier()


class Weights:

    def __init__(self, chip, tag, side):
        self.chip, self.side = chip, side
        self.loaded = chip.lasting_sem(f"{tag}_weights_loaded")
        self.at = {True: 0, False: 0}
        self.dmas = []
        self.streams = []

    def room(self, n, big=True):
        a = self.chip.arena[self.side] if big else self.chip.vecs[self.side]
        o = self.at[big]
        self.at[big] = o + n
        assert self.at[big] <= (ARENA if big else VECS), (big, self.at)
        return a[:, o:o + n]

    def matrix(self, src, big=True):
        k, n = src.shape
        v = self.room(k // P * n, big).rearrange("p (c n) -> p c n", c=k // P)
        self.dmas.append((v, src.rearrange("(c p) n -> p c n", p=P)))
        return v

    def repeated(self, src, copies):
        k, n = src.shape
        h = n // 16
        v = self.room(k // P * n * copies).rearrange("p (c n) -> p c n", c=k // P)
        w = v.rearrange("p c (h r d) -> p c h r d", r=copies, d=16)
        s = src.rearrange("(c p) (h d) -> p c h d", p=P, d=16)
        for c in range(k // P):
            for r in range(copies):
                self.dmas.append((w[:, c, :, r, :], s[:, c]))
        return v

    def columns(self, src):
        n = src.shape[0] // P
        v = self.room(n, False)
        self.dmas.append((v, src.rearrange("(c p) -> p c", p=P)))
        return v

    def row(self, src):
        n = src.shape[0]
        v = self.room(n, False)[0:1, :]
        self.dmas.append((v, src.rearrange("(a n) -> a n", a=1)))
        return v

    def everywhere(self, src):
        n = src.shape[0]
        v = self.room(n, False)
        self.dmas.append((v, src.partition_broadcast(P)))
        return v

    def load(self, sp):
        for dst, src in self.dmas:
            sp.dma_start(dst, src, allow_slow_non_contiguous=True).then_inc(self.loaded, 16)
        for dst, src, signal in self.streams:
            sp.dma_start(dst, src).then_inc(signal, 16)

    def wait(self, eng):
        eng.wait_ge(self.loaded, 16 * len(self.dmas))


def ln_stats_vector(chip, dve, src, s, twice=False, eps=LN_EPS, second_eps=LN_EPS, have=False):
    if not have:
        with dve.Fori(0, NB) as b:
            dve.bn_stats(chip.bn[:, b, :], src[:, b, :])
        dve.drain()
    for b in range(NB):
        dve.bn_aggr(chip.mv[:, b, :], chip.bn[:, b, :])
    dve.drain()
    dve.tensor_scalar(chip.var[:, :], chip.mv[:, :, 1], eps, None, ALU.add).then_inc(s["var_ready"], 1)
    dve.wait_ge(s["std_ready"], 1)
    dve.reciprocal(chip.rstd[:, :], chip.std[:, :])
    dve.drain()
    if twice:
        dve.tensor_tensor(chip.rstd2[:, :], chip.rstd[:, :], chip.rstd[:, :], ALU.mult)
        dve.drain()
        dve.tensor_tensor(chip.rstd2[:, :], chip.rstd2[:, :], chip.mv[:, :, 1], ALU.mult)
        dve.drain()
        dve.tensor_scalar(chip.var[:, :], chip.rstd2[:, :], second_eps, None, ALU.add).then_inc(s["var_ready"], 1)
        dve.wait_ge(s["std_ready"], 2)
        dve.reciprocal(chip.rstd2[:, :], chip.std[:, :])
        dve.drain()
        dve.tensor_tensor(chip.rstd2[:, :], chip.rstd2[:, :], chip.rstd[:, :], ALU.mult)
        dve.drain()


def ln_stats_scalar(chip, act, s, twice=False):
    for n in range(2 if twice else 1):
        act.wait_ge(s["var_ready"], n + 1)
        act.activation(chip.std[:, :], chip.var[:, :], ACT.Sqrt).then_inc(s["std_ready"], 1)


def setup_block(chip, first):
    nc = chip.nc
    zeroed = chip.sem("arenas_zeroed")
    const_step = chip.sem("const_step")
    x_loaded = chip.sem("x_loaded")
    with nc.Block() as block:
        @block.gpsimd
        def _(pool):
            pool.memset(chip.arena[1][:, :], 0.0).then_inc(zeroed, 1)
            pool.memset(chip.vecs[1][:, :], 0.0).then_inc(zeroed, 1)
            pool.memset(chip.ident[:, :], 0.0).then_inc(const_step, 1)
            pool.memset(chip.upper[:, :], 1.0).then_inc(const_step, 1)
            pool.memset(chip.causal[:, :], 0.0).then_inc(const_step, 1)
            pool.memset(chip.ones[:, :], 1.0).then_inc(const_step, 1)
            for m in chip.block_of.values():
                pool.memset(m[:, :], 1.0).then_inc(const_step, 1)
            pool.wait_ge(const_step, 6)
            pool.affine_select(out=chip.ident[:, :], in_=chip.ident[:, :], compare_op=ALU.not_equal, fill=1.0,
                               base=0, pattern=[[-1, P]], channel_multiplier=1).then_inc(const_step, 1)
            pool.affine_select(out=chip.upper[:, :], in_=chip.upper[:, :], compare_op=ALU.is_ge, fill=0.0,
                               base=0, pattern=[[1, P]], channel_multiplier=-1).then_inc(const_step, 1)
            pool.affine_select(out=chip.causal[:, :], in_=chip.causal[:, :], compare_op=ALU.is_ge, fill=-1e30,
                               base=0, pattern=[[-1, P]], channel_multiplier=1).then_inc(const_step, 1)
            for hd, m in chip.block_of.items():
                pool.affine_select(out=m[:, :], in_=m[:, :], compare_op=ALU.is_ge, fill=0.0,
                                   base=0, pattern=[[-hd, P // hd]], channel_multiplier=1).then_inc(const_step, 1)
            pool.wait_ge(const_step, 11)
            for hd, m in chip.block_of.items():
                pool.affine_select(out=m[:, :], in_=m[:, :], compare_op=ALU.is_ge, fill=0.0,
                                   base=hd - 1, pattern=[[hd, P // hd]], channel_multiplier=-1).then_inc(const_step, 1)

        @block.vector
        def _(dve):
            dve.memset(chip.arena[0][:, :], 0.0).then_inc(zeroed, 1)
            dve.memset(chip.vecs[0][:, :], 0.0).then_inc(zeroed, 1)

        @block.sync
        def _(sp):
            sp.dma_start(chip.X[:, :, :], chip.ins["x"].rearrange("b s d -> s b d")).then_inc(x_loaded, 16)
            sp.wait_ge(zeroed, 4)
            first.load(sp)
            sp.wait_ge(x_loaded, 16)


def store_block(chip):
    nc = chip.nc
    stored = chip.sem("x_stored")
    with nc.Block() as block:
        @block.sync
        def _(sp):
            sp.dma_start(chip.out.rearrange("b s d -> s b d"), chip.X[:, :, :]).then_inc(stored, 16)
            sp.wait_ge(stored, 16)


class AttentionPlan:

    def __init__(self, tag, heads, hd, scale, mask, source="self", kv_heads=None, causal_gap=None,
                 double_ln=False, residual="X"):
        self.tag, self.heads, self.hd, self.scale, self.mask, self.source = tag, heads, hd, scale, mask, source
        self.kv_heads = kv_heads or heads
        self.double_ln, self.residual = double_ln, residual
        self.causal_gap = causal_gap
        self.per_chunk = P // hd
        self.chunks = heads // self.per_chunk
        self.vw = self.kv_heads * hd
        self.ow = heads * hd


def attention_block(chip, plan, w, prefetch, have_stats):
    nc, ins = chip.nc, chip.ins
    t, H, hd = plan.tag, plan.heads, plan.hd
    ctxsrc = plan.source == "ctx"
    pads = plan.mask == "support"
    UH = 4
    U = H // UH
    NU = GR * U
    SW = P + 1 if pads else P
    OW, VW, C = plan.ow, plan.vw, plan.chunks
    vrows = max(1, 512 // VW) if VW >= 256 else 2
    vcols = min(VW, 512)
    vtasks = [(j, c) for j in range(0, GR, vrows) for c in range(0, VW, vcols)]
    ocs = OW // P
    otasks = [(c, min(c + 4, ocs)) for c in range(0, ocs, 4)]
    front = [("y", 0), ("y", 1)]
    if ctxsrc:
        front += [("c", 0), ("c", 1)]
    if plan.mask == "timebias":
        front += [("ct", 0), ("km", 0)]
    if pads:
        front += [("valid", 0), ("count", 0)]
    front += [("q", c) for c in range(C)] + [("k", c) for c in range(C)] + [("v", n) for n in range(len(vtasks))]
    where, n_front = {}, [0, 0]
    for f in front:
        b = 0 if f[0] == "v" and "bv" in w.v else sum(n_front) % 2 if f[0] != "v" else int(n_front[1] < n_front[0])
        where[f] = (b, n_front[b])
        n_front[b] += 1
    per_group = [n_front[0] + GR, n_front[1] + GR * len(otasks)]
    obufs = 2 if OW <= 512 else 1

    with ExitStack() as scope:
        sb = lambda n, s, d=F32: chip.sb(f"{t}_{n}", s, d, scope)
        sem = lambda n: chip.sem(f"{t}_{n}")
        yn = sb("yn", [P, GR, D])
        yT = sb("yT", [P, KC, TG])
        if ctxsrc:
            cn = sb("cn", [P, GR, D])
            cT = sb("cT", [P, KC, TG])
        else:
            cT = yT
        qT = sb("qT", [P, C, TG])
        kB = sb("kB", [P, C, GR, plan.per_chunk, P])
        if "bk" in w.v:
            bkB = sb("bkB", [P, C, plan.per_chunk])
        v = sb("v", [P, GR, VW])
        sm = sb("sm", [P, 2, UH, SW])
        nmx = sb("nmx", [P, 2, UH])
        p = sb("p", [P, 2, UH, SW])
        pT = sb("pT", [P, 2, UH, P])
        rsum = sb("rsum", [P, 2, H])
        rinv = sb("rinv", [P, H])
        on = sb("on", [P, OW])
        oT = sb("oT", [P, ocs, P])
        maskadd = sb("maskadd", [P, GR, P])
        if plan.mask == "keymask":
            raw = sb("raw", [P, GR, P], U8)
        if pads:
            raw = sb("raw", [P, GR, P], I32)
            valid = sb("valid", [P, GR, P])
            count = sb("count", [P, GR, P])
            npad = sb("npad", [P, GR])
            npad1 = sb("npad1", [P, GR])
            lnpad = sb("lnpad", [P, GR])
            padcol = sb("padcol", [P, GR])
        if plan.mask == "timebias":
            deltas = sb("deltas", [P, NB])
            ctcol = sb("ctcol", [P, NB])
            dwide = sb("dwide", [P, GR, P])
            gap = sb("gap", [P, GR, P])
            bias = sb("bias", [P, GR, P])
            keyrow = sb("keyrow", [1, NB * P])
            keyadd = sb("keyadd", [P, GR, P])
        proj = [chip.ps(f"{t}_proj0", scope), chip.ps(f"{t}_proj1", scope)]
        psS = [chip.ps(f"{t}_scores0", scope), chip.ps(f"{t}_scores1", scope)]
        psT = [chip.ps(f"{t}_probsT0", scope), chip.ps(f"{t}_probsT1", scope)]
        psO = chip.ps(f"{t}_out", scope, 1024)

        s = {n: sem(n) for n in ("var_ready", "std_ready")}
        yn_ready = sem("yn_ready")
        filled = [sem("proj0_filled"), sem("proj1_filled")]
        emptied = [sem("proj0_emptied"), sem("proj1_emptied")]
        scores_ready = sem("scores_ready")
        masked_ready = sem("masked_ready")
        probs_ready = sem("probs_ready")
        probsT_ready = sem("probsT_ready")
        probsT_copied = sem("probsT_copied")
        unit_begun = sem("unit_begun")
        bias_added = sem("bias_added")
        bkB_ready = sem("bkB_ready")
        sp_turn = sem("sp_turn")
        pv_done = sem("pv_done")
        out_normal = sem("out_normal")
        ctx_loaded = sem("ctx_loaded")
        mask_loaded = sem("mask_loaded")
        step_done = sem("mask_step")
        step_back = sem("mask_back")
        wide_ready = sem("wide_ready")

        with nc.Block() as block:
            @block.sync
            def _(sp):
                if ctxsrc:
                    sp.dma_start(cn[:, :, :], ins["ctx_1024"][0:GR].rearrange("b s d -> s b d")).then_inc(ctx_loaded, 16)
                if plan.mask == "keymask":
                    src = ins["mask_Bx1xSxS2_bk1"].rearrange("b a q k -> q (b a) k")
                if pads:
                    src = ins["mask_BxS2xS_ik0"].rearrange("b v t -> v b t")
                if plan.mask in ("keymask", "support"):
                    sp.dma_start(raw[:, :, :], src[:, 0:GR, :]).then_inc(mask_loaded, 16)
                if plan.mask == "timebias":
                    sp.dma_start(deltas[:, :], ins["fside_BxS2_0"].rearrange("b s -> s b"), allow_slow_non_contiguous=True).then_inc(mask_loaded, 16)
                    sp.dma_start(keyrow[:, :], ins["mask_BxS2_ff1"].rearrange("b s -> (b s)").rearrange("(a n) -> a n", a=1)).then_inc(mask_loaded, 16)
                if prefetch:
                    prefetch.load(sp)
                if ctxsrc:
                    with sp.Fori(0, NG - 1) as g:
                        for kc in range(KC):
                            b, n = where[("c", kc)]
                            sp.wait_ge(filled[b], done(g * per_group[b] + n))
                        sp.sem_inc(sp_turn, 1)
                        sp.dma_start(cn[:, :, :], ins["ctx_1024"][bass.ds(g * GR + GR, GR)].rearrange("b s d -> s b d")).then_inc(ctx_loaded, 16)
                        if plan.mask in ("keymask", "support"):
                            sp.wait_ge(wide_ready, done(g))
                            sp.sem_inc(sp_turn, 1)
                            sp.dma_start(raw[:, :, :], src[:, bass.ds(g * GR + GR, GR), :]).then_inc(mask_loaded, 16)

            @block.tensor
            def _(pe):
                for x in (filled[0], filled[1], scores_ready, probsT_ready, pv_done):
                    pe.sem_inc(x, LEAD)
                w.wait(pe)
                if plan.mask == "timebias":
                    pe.wait_ge(mask_loaded, 32)
                    pe.matmul(psS[0][:, 0:NB], chip.upper[:, :], deltas[:, :], start=True, stop=True).then_inc(step_back, 1)

                with pe.Fori(0, NG) as g:
                    used = [0, 0]

                    def claim(b):
                        pe.wait_ge(emptied[b], done(g * per_group[b] + used[b] - 1))
                        used[b] += 1
                        return proj[b]

                    def have(f):
                        b, n = where[f]
                        pe.wait_ge(emptied[b], done(g * per_group[b] + n))

                    pe.wait_ge(yn_ready, done(g))
                    for f in front:
                        b = where[f][0]
                        kind, i = f
                        if kind == "c" and i == 0:
                            pe.wait_ge(ctx_loaded, g * 16 + 16)
                        if kind in ("ct", "valid") and i == 0:
                            pe.wait_ge(wide_ready, done(g))
                        if kind == "q" and i == 0:
                            have(("y", 0))
                            have(("y", 1))
                        if kind == "k" and i == 0 and ctxsrc:
                            have(("c", 0))
                            have(("c", 1))
                        bank = claim(b)
                        if kind in "yc":
                            x = yn if kind == "y" else cn
                            for j in range(GR):
                                mm = pe.transpose(bank[:, j * P:(j + 1) * P], x[:, j, i * P:(i + 1) * P], chip.ident[:, :])
                        elif kind in "qk":
                            for kc in range(KC):
                                mm = pe.matmul(bank[:, :], w.v[kind][:, kc, i * P:(i + 1) * P],
                                               (yT if kind == "q" else cT)[:, kc, :], start=(kc == 0), stop=(kc == KC - 1))
                        elif kind == "v":
                            j0, c0 = vtasks[i]
                            for j in range(j0, j0 + vrows):
                                o = bank[:, (j - j0) * vcols:(j - j0 + 1) * vcols]
                                for kc in range(KC):
                                    mm = pe.matmul(o, cT[:, kc, j * P:(j + 1) * P], w.v["v"][:, kc, c0:c0 + vcols], start=(kc == 0), stop=(kc == KC - 1))
                        elif kind == "ct":
                            for j in range(GR):
                                mm = pe.matmul(bank[:, j * P:(j + 1) * P], dwide[:, j, :], chip.upper[:, :], start=True, stop=True)
                        elif kind == "km":
                            mm = pe.matmul(bank[:, :], chip.ones[0:1, 0:P], keyrow[0:1, bass.ds(g * TG, TG)], start=True, stop=True)
                        elif kind == "valid":
                            for j in range(GR):
                                mm = pe.matmul(bank[:, j * P:(j + 1) * P], valid[:, j, :], chip.ident[:, :], start=True, stop=True)
                        elif kind == "count":
                            for j in range(GR):
                                mm = pe.matmul(bank[:, j * P:(j + 1) * P], valid[:, j, :], chip.upper[:, :], start=True, stop=True)
                        mm.then_inc(filled[b], 1)
                    for b in range(2):
                        pe.wait_ge(emptied[b], done(g * per_group[b] + n_front[b] - 1))

                    for st in range(NU + 5):
                        if st < NU:
                            u = st
                            j = u // U
                            pe.wait_ge(masked_ready, done(g * NU + u - 2))
                            width = min(UH, plan.per_chunk)
                            for i in range(0, UH, width):
                                c, o = divmod(u % U * UH + i, plan.per_chunk)
                                mm = pe.matmul(psS[u % 2][:, i * P:(i + width) * P], qT[:, c, j * P:(j + 1) * P],
                                               kB[:, c, j, o:o + width, :], start=True, stop=True)
                            mm.then_inc(scores_ready, 1)
                        if 0 <= st - 1 < NU:
                            u = st - 1
                            pe.wait_ge(probs_ready, done(g * NU + u))
                            pe.wait_ge(probsT_copied, done(g * NU + u - 2))
                            for i in range(UH):
                                mm = pe.transpose(psT[u % 2][:, i * P:(i + 1) * P], p[:, u % 2, i, 0:P], chip.ident[:, :])
                            mm.then_inc(probsT_ready, 1)
                        if 0 <= st - 2 < NU:
                            u = st - 2
                            j = u // U
                            ob = j % obufs * 512
                            if u % U == 0:
                                pe.wait_ge(out_normal, done(g * GR + j - obufs))
                            pe.wait_ge(probsT_copied, done(g * NU + u))
                            for i in range(UH):
                                h = u % U * UH + i
                                hv = h * plan.kv_heads // H
                                mm = pe.matmul(psO[:, ob + h * hd:ob + (h + 1) * hd], pT[:, u % 2, i, :],
                                               v[:, j, hv * hd:(hv + 1) * hd], start=True, stop=True)
                            if u % U == U - 1:
                                mm.then_inc(pv_done, 1)
                        if 0 <= st - 3 < NU and (st - 3) % U == U - 1:
                            j = (st - 3) // U
                            pe.wait_ge(out_normal, done(g * GR + j))
                            for c0, c1 in otasks:
                                bank = claim(1)
                                for c in range(c0, c1):
                                    mm = pe.transpose(bank[:, (c - c0) * P:(c - c0 + 1) * P], on[:, c * P:(c + 1) * P], chip.ident[:, :])
                                mm.then_inc(filled[1], 1)
                        if 0 <= st - 4 < NU and (st - 4) % U == U - 1:
                            bank = claim(0)
                            pe.wait_ge(emptied[1], done(g * per_group[1] + used[1] - 1))
                            for c in range(ocs):
                                mm = pe.matmul(bank[:, 0:D], oT[:, c, :], w.v["o"][:, c, :], start=(c == 0), stop=(c == ocs - 1))
                            mm.then_inc(filled[0], 1)

            def empty_bank(eng, b, g, f):
                kind, i = f
                eng.wait_ge(filled[b], done(g * per_group[b] + where[f][1]))
                bank = proj[b]
                add = mul = None
                if kind == "y":
                    dst, src = yT[:, i, :], bank[:, :]
                    if "g" in w.v:
                        mul, add = w.v["g"][:, i:i + 1], w.v["b"][:, i:i + 1]
                elif kind == "c":
                    dst, src = cT[:, i, :], bank[:, :]
                elif kind == "q":
                    dst, src = qT[:, i, :], bank[:, :]
                    if "bq" in w.v:
                        add = w.v["bq"][:, i:i + 1]
                elif kind == "k":
                    src = bank[:, :].rearrange("p (j t) -> p j t", j=GR)
                    for o in range(plan.per_chunk):
                        dst, own = kB[:, i, :, o, :], chip.block_of[hd][:, o:o + 1]
                        if b == 0:
                            op = eng.tensor_scalar(dst, src, w.v["bk"][:, i:i + 1] if "bk" in w.v else 0.0, own, ALU.add, ALU.mult)
                        elif "bk" in w.v:
                            op = eng.activation(dst, src, ACT.Identity, bias=bkB[:, i, o:o + 1], scale=own)
                        else:
                            op = eng.activation(dst, src, ACT.Copy, scale=own)
                    return op
                elif kind == "v":
                    j0, c0 = vtasks[i]
                    dst = v[:, j0:j0 + vrows, c0:c0 + vcols]
                    src = bank[:, 0:vrows * vcols].rearrange("p (j c) -> p j c", j=vrows)
                    if "bv" in w.v:
                        return eng.tensor_tensor(dst, src, w.v["bv"][:, c0:c0 + vcols].unsqueeze(1).to_broadcast([P, vrows, vcols]), ALU.add)
                elif kind == "km":
                    dst, src = keyadd[:, :, :], bank[:, :].rearrange("p (j k) -> p j k", j=GR)
                    return eng.tensor_scalar(dst, src, 1e9 / plan.scale, -1e9 / plan.scale, ALU.mult, ALU.add) if b == 0 else \
                        eng.activation(dst, src, ACT.Copy, bias=-1e9 / plan.scale, scale=1e9 / plan.scale)
                elif kind == "count":
                    dst, src = count[:, :, :], bank[:, :].rearrange("p (j k) -> p j k", j=GR)
                if b == 0:
                    if mul is not None:
                        return eng.tensor_scalar(dst, src, mul, add, ALU.mult, ALU.add)
                    if add is not None:
                        return eng.tensor_scalar(dst, src, add, None, ALU.add)
                    return eng.tensor_copy(dst, src)
                if mul is not None:
                    return eng.activation(dst, src, ACT.Identity, bias=add, scale=mul)
                if add is not None:
                    return eng.activation(dst, src, ACT.Identity, bias=add)
                return eng.copy(dst, src)

            @block.vector
            def _(dve):
                for x in (yn_ready, emptied[0], masked_ready, probsT_copied, out_normal, wide_ready):
                    dve.sem_inc(x, LEAD)
                w.wait(dve)
                if "bk" in w.v:
                    for c in range(C):
                        op = dve.tensor_scalar(bkB[:, c, :], chip.block_of[hd][:, :], w.v["bk"][:, c:c + 1], None, ALU.mult)
                    op.then_inc(bkB_ready, 1)
                ln_stats_vector(chip, dve, chip.X, s, plan.double_ln, have=have_stats)
                if plan.mask == "timebias":
                    dve.wait_ge(step_back, 1)
                    dve.tensor_copy(ctcol[:, :], psS[0][:, 0:NB])
                    dve.drain()
                if plan.mask == "none":
                    dve.memset(maskadd[:, 0, :], 0.0)
                    dve.drain()
                resid = chip.X if plan.residual == "X" else chip.Y
                with dve.Fori(0, NG) as g:
                    for j in range(GR):
                        b = g * GR + j
                        if plan.residual == "Y":
                            dve.tensor_scalar(chip.Y[:, b, :], chip.X[:, b, :], chip.mv[:, b, 0:1], chip.rstd[:, bass.ds(b, 1)],
                                              ALU.subtract, ALU.mult)
                        scale = chip.rstd2 if plan.double_ln else chip.rstd
                        ln = dve.tensor_scalar(yn[:, j, :], chip.X[:, b, :], chip.mv[:, b, 0:1], scale[:, bass.ds(b, 1)],
                                               ALU.subtract, ALU.mult)
                    ln.then_inc(yn_ready, 1)
                    if plan.mask == "keymask":
                        dve.wait_ge(mask_loaded, g * 16 + 16)
                        dve.tensor_scalar(maskadd[:, :, :], raw[:, :, :], -1e15 / plan.scale, None, ALU.mult).then_inc(wide_ready, 1)
                    if pads:
                        dve.wait_ge(mask_loaded, g * 16 + 16)
                        dve.tensor_scalar(valid[:, :, :], raw[:, :, :], 0.0, None, ALU.not_equal).then_inc(wide_ready, 1)
                    if plan.mask == "timebias":
                        dve.tensor_copy(dwide[:, :, :], deltas[:, bass.ds(g * GR, GR)].unsqueeze(2).to_broadcast([P, GR, P])).then_inc(wide_ready, 1)
                    for f in front:
                        if where[f][0]:
                            continue
                        if f[0] == "ct":
                            dve.wait_ge(filled[0], done(g * per_group[0] + where[f][1]))
                            for j in range(GR):
                                op = dve.tensor_scalar(gap[:, j, :], proj[0][:, j * P:(j + 1) * P], ctcol[:, bass.ds(g * GR + j, 1)], None, ALU.subtract)
                            op.then_inc(emptied[0], 1)
                            dve.drain()
                            dve.sem_inc(step_done, 1)
                        elif f[0] == "valid":
                            dve.wait_ge(filled[0], done(g * per_group[0] + where[f][1]))
                            dve.wait_ge(emptied[1], done(g * per_group[1] + where[("count", 0)][1]))
                            dve.scalar_tensor_tensor(out=maskadd[:, :, :], in0=count[:, :, :], scalar=plan.causal_gap + 0.5,
                                                     in1=proj[0][:, :].rearrange("p (j k) -> p j k", j=GR),
                                                     op0=ALU.is_lt, op1=ALU.mult).then_inc(emptied[0], 1)
                            dve.tensor_scalar(npad[:, :], count[:, :, P - 1], -1.0, plan.causal_gap, ALU.mult, ALU.add)
                            dve.drain()
                            dve.tensor_scalar(maskadd[:, :, :], maskadd[:, :, :], -1.0, 1e30, ALU.add, ALU.mult)
                            dve.tensor_scalar(npad1[:, :], npad[:, :], 1.0, None, ALU.max)
                            dve.drain()
                            dve.sem_inc(step_done, 1)
                            dve.tensor_scalar(npad[:, :], npad[:, :], 0.5, 1e30, ALU.is_lt, ALU.mult)
                            dve.drain()
                            dve.wait_ge(step_back, g + 1)
                            dve.tensor_tensor(padcol[:, :], npad[:, :], lnpad[:, :], ALU.subtract)
                            dve.drain()
                            dve.tensor_scalar(padcol[:, :], padcol[:, :], 1e4, None, ALU.add)
                            dve.drain()
                        else:
                            empty_bank(dve, 0, g, f).then_inc(emptied[0], 1)
                    if plan.mask == "timebias":
                        dve.wait_ge(step_back, g + 2)
                        dve.wait_ge(emptied[1], done(g * per_group[1] + where[("km", 0)][1]))
                        dve.tensor_scalar(bias[:, :, :], bias[:, :, :], w.v["tb"], 1.0 / plan.scale, ALU.mult, ALU.mult)
                        dve.drain()
                        dve.tensor_tensor(maskadd[:, :, :], bias[:, :, :], keyadd[:, :, :], ALU.add)
                        dve.drain()

                    used = [n_front[0]]

                    for st in range(NU + 6):
                        if st < NU:
                            u = st
                            j = u // U
                            dve.wait_ge(scores_ready, done(g * NU + u))
                            dve.wait_ge(probs_ready, done(g * NU + u - 2))
                            if pads:
                                dve.tensor_copy(sm[:, u % 2, :, P], padcol[:, j:j + 1].to_broadcast([P, UH]))
                            dve.sem_inc(unit_begun, 1)
                            for i in range(UH):
                                m = {"causal": chip.causal[:, :], "none": maskadd[:, 0, :]}.get(plan.mask, maskadd[:, j, :])
                                op = dve.tensor_tensor_reduce(sm[:, u % 2, i, 0:P], psS[u % 2][:, i * P:(i + 1) * P], m, -plan.scale,
                                                              padcol[:, j:j + 1] if pads else FMAX,
                                                              ALU.add, ALU.min, nmx[:, u % 2, i:i + 1])
                            op.then_inc(masked_ready, 1)
                        if 0 <= st - 1 < NU:
                            u = st - 1
                            dve.wait_ge(probsT_ready, done(g * NU + u))
                            dve.tensor_copy(pT[:, u % 2, :, :], psT[u % 2][:, :].rearrange("p (i q) -> p i q", i=UH)).then_inc(probsT_copied, 1)
                        if 0 <= st - 5 < NU and (st - 5) % U == U - 1:
                            b = g * GR + (st - 5) // U
                            dve.wait_ge(filled[0], done(g * per_group[0] + used[0]))
                            used[0] += 1
                            if "bo" in w.v and (st - 5) // U == 0:
                                dve.wait_ge(bias_added, done(g))
                            dve.tensor_tensor(resid[:, b, :], resid[:, b, :], proj[0][:, 0:D], ALU.add).then_inc(emptied[0], 1)
                            dve.drain()
                            dve.bn_stats(chip.bn[:, b, :], resid[:, b, :])
                        if 0 <= st - 3 < NU and (st - 3) % U == U - 1:
                            j = (st - 3) // U
                            dve.wait_ge(pv_done, done(g * GR + j))
                            dve.reciprocal(rinv[:, :], rsum[:, j % 2, :])
                            dve.drain()
                            dve.wait_ge(filled[1], done(g * per_group[1] + n_front[1] + j * len(otasks) - 1))
                            o = psO[:, j % obufs * 512:j % obufs * 512 + OW].rearrange("p (h d) -> p h d", h=H)
                            dve.tensor_tensor(on[:, :].rearrange("p (h d) -> p h d", h=H), o,
                                              rinv[:, :].unsqueeze(2).to_broadcast([P, H, hd]), ALU.mult).then_inc(out_normal, 1)

            @block.gpsimd
            def _(pool):
                if "bo" not in w.v:
                    return
                pool.sem_inc(bias_added, LEAD)
                w.wait(pool)
                rows = chip.X if plan.residual == "X" else chip.Y
                with pool.Fori(0, NG) as g:
                    pool.wait_ge(yn_ready, done(g))
                    pool.tensor_tensor(rows[:, bass.ds(g * GR, GR), :], rows[:, bass.ds(g * GR, GR), :],
                                       w.v["bo"][:, :].unsqueeze(1).to_broadcast([P, GR, D]), ALU.add).then_inc(bias_added, 1)

            @block.scalar
            def _(act):
                for x in (emptied[1], probs_ready):
                    act.sem_inc(x, LEAD)
                ln_stats_scalar(chip, act, s, plan.double_ln)
                w.wait(act)
                if "bk" in w.v:
                    act.wait_ge(bkB_ready, 1)
                act.preload_act_table(ACT.Exp)
                with act.Fori(0, NG) as g:
                    for f in front:
                        if where[f][0]:
                            empty_bank(act, 1, g, f).then_inc(emptied[1], 1)
                        if f[0] == "count":
                            act.wait_ge(step_done, g + 1)
                            act.activation(lnpad[:, :], npad1[:, :], ACT.Ln).then_inc(step_back, 1)
                        if f[0] == "km":
                            act.wait_ge(step_done, g + 1)
                            act.activation(gap[:, :, :], gap[:, :, :], ACT.Abs)
                            act.drain()
                            act.activation(bias[:, :, :], gap[:, :, :], ACT.Ln, bias=1.0).then_inc(step_back, 1)
                    used = [n_front[1]]
                    for st in range(NU + 4):
                        if st < NU:
                            u = st
                            j = u // U
                            act.wait_ge(masked_ready, done(g * NU + u))
                            act.wait_ge(probsT_ready, done(g * NU + u - 2))
                            if u % U == 0:
                                act.wait_ge(out_normal, done(g * GR + j - 2))
                            for i in range(UH):
                                h = u % U * UH + i
                                op = act.activation(p[:, u % 2, i, :], sm[:, u % 2, i, :], ACT.Exp, bias=nmx[:, u % 2, i:i + 1], scale=-1.0,
                                                    accum_out=rsum[:, j % 2, h:h + 1])
                            op.then_inc(probs_ready, 1)
                        if 0 <= st - 3 < NU and (st - 3) % U == U - 1:
                            for c0, c1 in otasks:
                                act.wait_ge(filled[1], done(g * per_group[1] + used[0]))
                                used[0] += 1
                                act.copy(oT[:, c0:c1, :], proj[1][:, 0:(c1 - c0) * P].rearrange("p (c q) -> p c q", c=c1 - c0)).then_inc(emptied[1], 1)


def l0_xattn_weights(chip, side):
    i, w = chip.ins, Weights(chip, "l0x", side)
    w.v = dict(q=w.matrix(i["L0_xattn_Wq"]), k=w.matrix(i["L0_xattn_Wk"]), v=w.matrix(i["L0_xattn_Wv"]), o=w.matrix(i["L0_xattn_Wo"]),
               bq=w.columns(i["L0_xattn_bq"]), bk=w.columns(i["L0_xattn_bk"]), bv=w.everywhere(i["L0_xattn_bv"]), bo=w.everywhere(i["L0_xattn_bo"]))
    return w


def l1_attn_weights(chip, side):
    i, w = chip.ins, Weights(chip, "l1a", side)
    wa, ba = i["L1_attn_W_attn"], i["L1_attn_b_attn"]
    w.v = dict(q=w.matrix(wa[:, 0:D]), k=w.matrix(wa[:, D:2 * D]), v=w.matrix(wa[:, 2 * D:3 * D]), o=w.matrix(i["L1_attn_W_proj"]),
               bq=w.columns(ba[0:D]), bk=w.columns(ba[D:2 * D]), bv=w.everywhere(ba[2 * D:3 * D]), bo=w.everywhere(i["L1_attn_b_proj"]))
    return w


def l2_attn_weights(chip, side):
    i, w = chip.ins, Weights(chip, "l2a", side)

    def heads(src):
        v = w.room(KC * 1024).rearrange("p (c h a) -> p c h a", c=KC, a=64)
        for c in range(KC):
            w.dmas.append((v[:, c], src[:, c * P:(c + 1) * P, :].rearrange("h p a -> p h a")))
        return v.rearrange("p c h a -> p c (h a)")

    w.v = dict(q=heads(i["L2_attn_Wq"]), k=heads(i["L2_attn_Wk"]), v=heads(i["L2_attn_Wv"]),
               o=w.matrix(i["L2_attn_Wo"].rearrange("h a d -> (h a) d")),
               bq=w.columns(i["L2_attn_bq"].rearrange("h a -> (h a)")), bk=w.columns(i["L2_attn_bk"].rearrange("h a -> (h a)")),
               bv=w.everywhere(i["L2_attn_bv"].rearrange("h a -> (h a)")), bo=w.everywhere(i["L2_attn_bo"]))
    return w


def l2_xattn_weights(chip, side):
    i, w = chip.ins, Weights(chip, "l2x", side)
    kv = i["L2_xattn_Wkv"]
    w.v = dict(q=w.matrix(i["L2_xattn_Wq"]), k=w.matrix(kv[:, 0:512]), v=w.matrix(kv[:, 512:1024]), o=w.matrix(i["L2_xattn_Wout"]),
               g=w.columns(i["L2_xattn_ln_w"]), b=w.columns(i["L2_xattn_ln_b"]))
    return w


def l2_ffn_attn_weights(chip, side):
    i, w = chip.ins, Weights(chip, "l2fa", side)
    w.v = dict(q=w.matrix(i["L2_ffn_wq"]), k=w.matrix(i["L2_ffn_wk"]), v=w.matrix(i["L2_ffn_wv"]), o=w.matrix(i["L2_ffn_wo"]),
               bq=w.columns(i["L2_ffn_bq"]), bk=w.columns(i["L2_ffn_bk"]), bv=w.everywhere(i["L2_ffn_bv"]), bo=w.everywhere(i["L2_ffn_bo"]),
               g=w.columns(i["L2_ffn_ln1_g"]), b=w.columns(i["L2_ffn_ln1_b"]))
    return w


def l3_xattn_weights(chip, side):
    i, w = chip.ins, Weights(chip, "l3x", side)
    w.v = dict(q=w.matrix(i["L3_xattn_Wq"]), k=w.repeated(i["L3_xattn_Wk"], 4), v=w.matrix(i["L3_xattn_Wv"]), o=w.matrix(i["L3_xattn_Wo"]),
               tb=w.everywhere(i["L3_xattn_time_bias_weight"]))
    return w


PLANS = {
    "l0x": (l0_xattn_weights, AttentionPlan("l0x", 16, 16, 0.25, "keymask", "ctx")),
    "l1a": (l1_attn_weights, AttentionPlan("l1a", 16, 16, 0.25, "causal")),
    "l2a": (l2_attn_weights, AttentionPlan("l2a", 16, 64, 0.125, "causal")),
    "l2x": (l2_xattn_weights, AttentionPlan("l2x", 8, 64, 0.125, "support", "ctx", causal_gap=5.0, double_ln=True)),
    "l2fa": (l2_ffn_attn_weights, AttentionPlan("l2fa", 16, 16, 0.25, "none", double_ln=True, residual="Y")),
    "l3x": (l3_xattn_weights, AttentionPlan("l3x", 16, 16, 0.25, "timebias", "ctx", kv_heads=4)),
}


class ExpertPlan:

    def __init__(self, tag, names, hidden, keep, deep_router=False, from_y=False):
        self.tag, self.names, self.hidden, self.keep = tag, names, hidden, keep
        self.deep_router, self.from_y = deep_router, from_y


NE = 8


def gates_vector(chip, dve, act_sems, plan, logits, tiles):
    iota, lg, hit, one, two, best, best2, at, e, g1, gates = tiles
    over_e = lambda x: x[:, :].unsqueeze(2).to_broadcast([P, NB, NE])
    ranks = iota[:, :].unsqueeze(1).to_broadcast([P, NB, NE])
    for i in range(NE):
        dve.memset(iota[:, i:i + 1], float(i - NE))
    dve.tensor_copy(lg[:, :, :], logits)
    dve.drain()

    def first_max(best, onehot):
        dve.tensor_reduce(best[:, :], lg[:, :, :], AX.X, ALU.max)
        dve.drain()
        dve.tensor_tensor(hit[:, :, :], lg[:, :, :], over_e(best), ALU.is_equal)
        dve.drain()
        dve.tensor_tensor(hit[:, :, :], hit[:, :, :], ranks, ALU.mult)
        dve.drain()
        dve.tensor_reduce(at[:, :], hit[:, :, :], AX.X, ALU.min)
        dve.drain()
        dve.tensor_tensor(onehot[:, :, :], over_e(at), ranks, ALU.is_equal)
        dve.drain()

    if plan.keep == 1:
        first_max(best, gates)
        return
    first_max(best, one)
    dve.scalar_tensor_tensor(out=lg[:, :, :], in0=one[:, :, :], scalar=-1e30, in1=lg[:, :, :], op0=ALU.mult, op1=ALU.add)
    dve.drain()
    first_max(best2, two)
    dve.tensor_tensor(e[:, :], best2[:, :], best[:, :], ALU.subtract).then_inc(act_sems["gap_ready"], 1)
    dve.wait_ge(act_sems["exp_ready"], 1)
    dve.tensor_scalar(g1[:, :], e[:, :], 1.0, None, ALU.add)
    dve.drain()
    dve.reciprocal(g1[:, :], g1[:, :])
    dve.drain()
    dve.tensor_tensor(e[:, :], e[:, :], g1[:, :], ALU.mult)
    dve.drain()
    dve.tensor_tensor(one[:, :, :], one[:, :, :], over_e(g1), ALU.mult)
    dve.tensor_tensor(two[:, :, :], two[:, :, :], over_e(e), ALU.mult)
    dve.drain()
    dve.tensor_tensor(gates[:, :, :], one[:, :, :], two[:, :, :], ALU.add)
    dve.drain()


def gates_scalar(act, act_sems, plan, tiles):
    e = tiles[8]
    if plan.keep == 2:
        act.wait_ge(act_sems["gap_ready"], 1)
        act.activation(e[:, :], e[:, :], ACT.Exp).then_inc(act_sems["exp_ready"], 1)


def gate_tiles(sb):
    return (sb("iota", [P, NE]), sb("logits", [P, NB, NE]), sb("hit", [P, NB, NE]), sb("one", [P, NB, NE]), sb("two", [P, NB, NE]),
            sb("best", [P, NB]), sb("best2", [P, NB]), sb("at", [P, NB]), sb("e", [P, NB]), sb("g1", [P, NB]), sb("gates", [P, NB, NE]))


def small_experts_block(chip, plan, w, prefetch, have_stats):
    nc, t = chip.nc, plan.tag
    NX = NE + 2
    with ExitStack() as scope:
        sb = lambda n, s, d=F32: chip.sb(f"{t}_{n}", s, d, scope)
        sem = lambda n: chip.sem(f"{t}_{n}")
        yn = sb("yn", [P, 2, GR, D])
        yT = sb("yT", [P, KC, NB * P])
        silu = sb("silu", [P, 2, TG])
        hT = sb("hT", [P, 2, TG])
        tiles = gate_tiles(sb)
        gates = tiles[-1]
        bank = [chip.ps(f"{t}_bank{i}", scope) for i in range(8)]
        s = {n: sem(n) for n in ("var_ready", "std_ready")}
        act_sems = {n: sem(n) for n in ("gap_ready", "exp_ready")}
        yn_ready = sem("yn_ready")
        turned = [sem("turned0"), sem("turned1")]
        yT_ready = [sem("yT0_ready"), sem("yT1_ready")]
        logits_ready = sem("logits_ready")
        gate_ready, up_ready = sem("gate_ready"), sem("up_ready")
        silu_ready = sem("silu_ready")
        hidden_ready = sem("hidden_ready")
        out_ready = sem("out_ready")
        out_added = sem("out_added")

        with nc.Block() as block:
            @block.sync
            def _(sp):
                if prefetch:
                    prefetch.load(sp)

            @block.tensor
            def _(pe):
                for x in (gate_ready, up_ready, out_ready):
                    pe.sem_inc(x, LEAD)
                w.wait(pe)
                for g in range(NG):
                    pe.wait_ge(yn_ready, g + 1)
                    for kc in range(KC):
                        if g:
                            pe.wait_ge(yT_ready[kc], g)
                        for j in range(GR):
                            mm = pe.transpose(bank[kc][:, j * P:(j + 1) * P], yn[:, g % 2, j, kc * P:(kc + 1) * P], chip.ident[:, :])
                        mm.then_inc(turned[kc], 1)
                for b in range(NB):
                    if b % GR == 0:
                        for kc in range(KC):
                            pe.wait_ge(yT_ready[kc], b // GR + 1)
                    o = bank[2][:, b * NE:(b + 1) * NE]
                    pe.matmul(o, chip.ones[0:1, 0:P], w.v["rb"], start=True, stop=False)
                    for kc in range(KC):
                        mm = pe.matmul(o, yT[:, kc, b * P:(b + 1) * P], w.v["rw"][:, kc, :], start=False, stop=(kc == KC - 1))
                mm.then_inc(logits_ready, 1)
                pe.wait_ge(hidden_ready, LEAD)
                with pe.Fori(0, NG) as g:
                    for i in range(NX + 1):
                        if i < NX:
                            n = g * NX + i
                            for m, ready, freed in (("w1", gate_ready, silu_ready), ("w3", up_ready, hidden_ready)):
                                pe.wait_ge(freed, done(n - 2))
                                o = bank[(0 if m == "w1" else 2) + i % 2]
                                for kc in range(KC):
                                    mm = pe.matmul(o[:, :], w.v[m][:, i, kc, :], yT[:, kc, bass.ds(g * TG, TG)], start=(kc == 0), stop=(kc == KC - 1))
                                mm.then_inc(ready, 1)
                        if i >= 1:
                            x = i - 1
                            pe.wait_ge(hidden_ready, done(g * NX + x))
                            if x <= NE:
                                pe.wait_ge(out_added, done(g * (NE + 1) + x - 1))
                            for j in range(GR):
                                mm = pe.matmul(bank[4 + j][:, 0:D], hT[:, x % 2, j * P:(j + 1) * P], w.v["w2"][:, x, :],
                                               start=(x <= NE), stop=(x != NE))
                            if x != NE:
                                mm.then_inc(out_ready, 1)

            @block.vector
            def _(dve):
                for x in (out_added,):
                    dve.sem_inc(x, LEAD)
                ln_stats_vector(chip, dve, chip.X, s, have=have_stats)
                w.wait(dve)
                for g in range(NG):
                    if g >= 2:
                        for kc in range(KC):
                            dve.wait_ge(turned[kc], g - 1)
                    for j in range(GR):
                        b = g * GR + j
                        op = dve.tensor_scalar(yn[:, g % 2, j, :], chip.X[:, b, :], chip.mv[:, b, 0:1], chip.rstd[:, b:b + 1], ALU.subtract, ALU.mult)
                    op.then_inc(yn_ready, 1)
                    dve.wait_ge(turned[0], g + 1)
                    dve.tensor_copy(yT[:, 0, g * TG:(g + 1) * TG], bank[0][:, :]).then_inc(yT_ready[0], 1)
                dve.wait_ge(logits_ready, 1)
                gates_vector(chip, dve, act_sems, plan, bank[2][:, 0:NB * NE].rearrange("p (b e) -> p b e", b=NB), tiles)
                dve.sem_inc(hidden_ready, LEAD)
                with dve.Fori(0, NG) as g:
                    for i in range(NX + 2):
                        if i < NX:
                            n = g * NX + i
                            dve.wait_ge(silu_ready, done(n))
                            dve.wait_ge(up_ready, done(n))
                            dve.tensor_tensor(hT[:, i % 2, :], silu[:, i % 2, :], bank[2 + i % 2][:, :], ALU.mult).then_inc(hidden_ready, 1)
                        x = i - 1
                        if 0 <= x < NE or x == NX - 1:
                            m = min(x, NE)
                            dve.wait_ge(out_ready, done(g * (NE + 1) + m))
                            for j in range(GR):
                                b = g * GR + j
                                if x < NE:
                                    op = dve.scalar_tensor_tensor(out=chip.X[:, b, :], in0=bank[4 + j][:, 0:D], scalar=gates[:, b, x:x + 1],
                                                                  in1=chip.X[:, b, :], op0=ALU.mult, op1=ALU.add)
                                else:
                                    op = dve.tensor_tensor(chip.X[:, b, :], chip.X[:, b, :], bank[4 + j][:, 0:D], ALU.add)
                            op.then_inc(out_added, 1)

            @block.scalar
            def _(act):
                act.sem_inc(silu_ready, LEAD)
                ln_stats_scalar(chip, act, s)
                for g in range(NG):
                    act.wait_ge(turned[1], g + 1)
                    act.copy(yT[:, 1, g * TG:(g + 1) * TG], bank[1][:, :]).then_inc(yT_ready[1], 1)
                gates_scalar(act, act_sems, plan, tiles)
                act.preload_act_table(ACT.Silu)
                act.wait_ge(hidden_ready, LEAD)
                with act.Fori(0, NG) as g:
                    for i in range(NX):
                        n = g * NX + i
                        act.wait_ge(gate_ready, done(n))
                        act.wait_ge(hidden_ready, done(n - 2))
                        act.activation(silu[:, i % 2, :], bank[i % 2][:, :], ACT.Silu).then_inc(silu_ready, 1)


def streamed_experts_block(chip, plan, w, prefetch, have_stats):
    nc, ins, t = chip.nc, chip.ins, plan.tag
    FC = plan.hidden // P
    W1, W2 = ins[plan.names[0]], ins[plan.names[1]]
    src = chip.Y if plan.from_y else chip.X
    with ExitStack() as scope:
        sb = lambda n, s, d=F32: chip.sb(f"{t}_{n}", s, d, scope)
        sem = lambda n: chip.sem(f"{t}_{n}")
        yn = sb("yn", [P, GR, D])
        yT = sb("yT", [P, KC, NB * P])
        hT = sb("hT", [P, FC, TG])
        tiles = gate_tiles(sb)
        gates = tiles[-1]
        hbank = [chip.ps(f"{t}_hidden{i}", scope) for i in range(2)]
        obank = [chip.ps(f"{t}_out{i}", scope) for i in range(2)]
        lbank = chip.ps(f"{t}_logits_ps", scope)
        s = {n: sem(n) for n in ("var_ready", "std_ready")}
        act_sems = {n: sem(n) for n in ("gap_ready", "exp_ready")}
        yn_ready = sem("yn_ready")
        filled = [sem("hidden0_filled"), sem("hidden1_filled")]
        emptied = [sem("hidden0_emptied"), sem("hidden1_emptied")]
        logits_ready = sem("logits_ready")
        out_ready = sem("out_ready")
        out_added = sem("out_added")
        act_turn = sem("act_turn")

        with nc.Block() as block:
            @block.sync
            def _(sp):
                def load_expert(e, half):
                    sp.dma_start(w.v["W1"][half], W1[bass.ds(e, 1)].rearrange("a (c p) f -> p (a c) f", p=P)).then_inc(w.v["stream"][half], 16)
                    sp.dma_start(w.v["W2"][half], W2[bass.ds(e, 1)].rearrange("a (c p) d -> p (a c) d", p=P)).then_inc(w.v["stream"][half], 16)

                if plan.deep_router:
                    sp.wait_ge(logits_ready, 1)
                load_expert(1, 1)
                if prefetch:
                    prefetch.load(sp)
                with sp.Fori(0, NE // 2 - 1) as i:
                    for half in range(2):
                        sp.wait_ge(out_ready, done(i * (2 * NB) + (half * NB + NB - 1)))
                        load_expert(i * 2 + 2 + half, half)

            @block.tensor
            def _(pe):
                for x in (*filled, out_ready):
                    pe.sem_inc(x, LEAD)
                w.wait(pe)

                def first_layer(wts, g, base, extra=0):
                    for f in range(FC):
                        b = f % 2
                        pe.wait_ge(emptied[b], done(base + f // 2 - 1))
                        for kc in range(KC):
                            mm = pe.matmul(hbank[b][:, :], wts[:, kc, f * P:(f + 1) * P], yT[:, kc, g * TG:(g + 1) * TG],
                                           start=(kc == 0), stop=(kc == KC - 1))
                        mm.then_inc(filled[b], 1)

                for g in range(NG):
                    pe.wait_ge(yn_ready, g + 1)
                    for kc in range(KC):
                        pe.wait_ge(emptied[kc], done(g - 1))
                        for j in range(GR):
                            mm = pe.transpose(hbank[kc][:, j * P:(j + 1) * P], yn[:, j, kc * P:(kc + 1) * P], chip.ident[:, :])
                        mm.then_inc(filled[kc], 1)
                for kc in range(KC):
                    pe.wait_ge(emptied[kc], done(NG - 1))
                base = NG
                for g in range(NG):
                    if plan.deep_router:
                        first_layer(w.v["W1"][1], g, base)
                        base += FC // 2
                    for j in range(GR):
                        b = g * GR + j
                        o = lbank[:, b * NE:(b + 1) * NE]
                        pe.matmul(o, chip.ones[0:1, 0:P], w.v["rb"], start=True, stop=False)
                        if plan.deep_router:
                            for f in range(FC):
                                pe.wait_ge(emptied[f % 2], done(base - FC // 2 + f // 2))
                                mm = pe.matmul(o, hT[:, f, j * P:(j + 1) * P], w.v["rw"][:, f, :], start=False, stop=(f == FC - 1))
                        else:
                            for kc in range(KC):
                                mm = pe.matmul(o, yT[:, kc, b * P:(b + 1) * P], w.v["rw"][:, kc, :], start=False, stop=(kc == KC - 1))
                mm.then_inc(logits_ready, 1)
                with pe.Fori(0, NE // 2) as i:
                    for half in range(2):
                        pe.wait_ge(w.v["stream"][half], i * 32 + 32)
                        for g in range(NG):
                            n = i * (2 * NG * FC // 2) + (base + (half * NG + g) * FC // 2)
                            first_layer(w.v["W1"][half], g, n)
                            for j in range(GR):
                                m = i * (2 * NB) + (half * NB + g * GR + j)
                                pe.wait_ge(out_added, done(m - 2))
                                o = obank[j % 2][:, 0:D]
                                for f in range(FC):
                                    if j == 0:
                                        pe.wait_ge(emptied[f % 2], done(n + f // 2))
                                    pe.matmul(o, hT[:, f, j * P:(j + 1) * P], w.v["W2"][half][:, f, :], start=(f == 0), stop=False)
                                mm = pe.matmul(o, chip.ones[0:1, 0:P], w.v["b2"][0:1, bass.ds(i * 2 * D + half * D, D)], start=False, stop=True)
                                mm.then_inc(out_ready, 1)

            def y_affine(eng, kc, dst, src):
                if "g" in w.v:
                    mul, add = w.v["g"][:, kc:kc + 1], w.v["b"][:, kc:kc + 1]
                    if kc == 0:
                        return eng.tensor_scalar(dst, src, mul, add, ALU.mult, ALU.add)
                    return eng.activation(dst, src, ACT.Identity, bias=add, scale=mul)
                return eng.tensor_copy(dst, src) if kc == 0 else eng.copy(dst, src)

            def relu(eng, b, g, base, bias):
                for f in range(b, FC, 2):
                    eng.wait_ge(filled[b], done(base + f // 2))
                    if b == 0:
                        op = eng.tensor_scalar(hT[:, f, :], hbank[0][:, :], bias(f), 0.0, ALU.add, ALU.max)
                    else:
                        eng.sem_inc(act_turn, 1)
                        op = eng.activation(hT[:, f, :], hbank[1][:, :], ACT.Relu, bias=bias(f))
                    op.then_inc(emptied[b], 1)

            @block.vector
            def _(dve):
                for x in (emptied[0], out_added):
                    dve.sem_inc(x, LEAD)
                w.wait(dve)
                ln_stats_vector(chip, dve, src, s, have=have_stats)
                for g in range(NG):
                    if g >= 1:
                        dve.wait_ge(filled[1], done(g - 1))
                    for j in range(GR):
                        b = g * GR + j
                        op = dve.tensor_scalar(yn[:, j, :], src[:, b, :], chip.mv[:, b, 0:1], chip.rstd[:, b:b + 1], ALU.subtract, ALU.mult)
                    op.then_inc(yn_ready, 1)
                    dve.wait_ge(filled[0], done(g))
                    y_affine(dve, 0, yT[:, 0, g * TG:(g + 1) * TG], hbank[0][:, :]).then_inc(emptied[0], 1)
                if plan.from_y:
                    dve.tensor_tensor(chip.X[:, :, :], chip.X[:, :, :], chip.Y[:, :, :], ALU.add)
                base = NG
                if plan.deep_router:
                    for g in range(NG):
                        relu(dve, 0, g, base, lambda f: w.v["rb1"][:, f:f + 1])
                        base += FC // 2
                dve.wait_ge(logits_ready, 1)
                gates_vector(chip, dve, act_sems, plan, lbank[:, 0:NB * NE].rearrange("p (b e) -> p b e", b=NB), tiles)
                with dve.Fori(0, NE // 2) as i:
                    for half in range(2):
                        for g in range(NG):
                            n = i * (2 * NG * FC // 2) + (base + (half * NG + g) * FC // 2)
                            relu(dve, 0, g, n, lambda f: w.v["b1"][:, bass.ds(i * 2 * FC + (half * FC + f), 1)])
                            for j in range(GR):
                                b = g * GR + j
                                dve.wait_ge(out_ready, done(i * (2 * NB) + (half * NB + b)))
                                dve.scalar_tensor_tensor(out=chip.X[:, b, :], in0=obank[j % 2][:, 0:D], scalar=gates[:, b, bass.ds(i * 2 + half, 1)],
                                                         in1=chip.X[:, b, :], op0=ALU.mult, op1=ALU.add).then_inc(out_added, 1)

            @block.scalar
            def _(act):
                act.sem_inc(emptied[1], LEAD)
                ln_stats_scalar(chip, act, s)
                w.wait(act)
                for g in range(NG):
                    act.wait_ge(filled[1], done(g))
                    y_affine(act, 1, yT[:, 1, g * TG:(g + 1) * TG], hbank[1][:, :]).then_inc(emptied[1], 1)
                base = NG
                if plan.deep_router:
                    for g in range(NG):
                        relu(act, 1, g, base, lambda f: w.v["rb1"][:, f:f + 1])
                        base += FC // 2
                gates_scalar(act, act_sems, plan, tiles)
                with act.Fori(0, NE // 2) as i:
                    for half in range(2):
                        for g in range(NG):
                            n = i * (2 * NG * FC // 2) + (base + (half * NG + g) * FC // 2)
                            relu(act, 1, g, n, lambda f: w.v["b1"][:, bass.ds(i * 2 * FC + (half * FC + f), 1)])


def l1_ffn_weights(chip, side):
    i, w = chip.ins, Weights(chip, "l1f", side)
    NX = NE + 2

    def both(m, split):
        n = 2 * P if split else D
        v = w.room(NX * n)
        routed, shared = i["L1_ffn_routed_" + m], i["L1_ffn_shared_" + m]
        if split:
            v = v.rearrange("p (e c h) -> p e c h", e=NX, c=KC)
            for c in range(KC):
                w.dmas.append((v[:, 0:NE, c], routed[:, c * P:(c + 1) * P, :].rearrange("e p h -> p e h")))
                w.dmas.append((v[:, NE:NX, c], shared[:, c * P:(c + 1) * P, :].rearrange("e p h -> p e h")))
            return v
        v = v.rearrange("p (e d) -> p e d", e=NX)
        w.dmas.append((v[:, 0:NE], routed.rearrange("e p d -> p e d")))
        w.dmas.append((v[:, NE:NX], shared.rearrange("e p d -> p e d")))
        return v

    w.v = dict(w1=both("w1", True), w3=both("w3", True), w2=both("w2", False), rw=w.matrix(i["L1_ffn_router_w"], False), rb=w.row(i["L1_ffn_router_b"]))
    return w


def stream_buffers(chip, w, plan):
    W1, W2 = chip.ins[plan.names[0]], chip.ins[plan.names[1]]
    F = plan.hidden
    first = [w.room(KC * F).rearrange("p (c f) -> p c f", c=KC) for _ in range(2)]
    second = [w.room(F // P * D).rearrange("p (c d) -> p c d", c=F // P) for _ in range(2)]
    stream = [chip.lasting_sem(f"{plan.tag}_stream{h}") for h in range(2)]
    w.streams.append((first[0], W1[0].rearrange("(c p) f -> p c f", p=P), stream[0]))
    w.streams.append((second[0], W2[0].rearrange("(c p) d -> p c d", p=P), stream[0]))
    return dict(W1=first, W2=second, stream=stream)


def l2_ffn_moe_weights(chip, side):
    i, w = chip.ins, Weights(chip, "l2fm", side)
    w.v = dict(stream_buffers(chip, w, EXPERTS["l2fm"]), rw=w.matrix(i["L2_ffn_gate_w"], False), rb=w.row(i["L2_ffn_gate_b"]),
               b1=w.columns(i["L2_ffn_b1"].rearrange("e f -> (e f)")), b2=w.row(i["L2_ffn_b2"].rearrange("e d -> (e d)")),
               g=w.columns(i["L2_ffn_ln2_g"]), b=w.columns(i["L2_ffn_ln2_b"]))
    return w


def l3_ffn_weights(chip, side):
    i, w = chip.ins, Weights(chip, "l3f", side)
    w.v = dict(stream_buffers(chip, w, EXPERTS["l3f"]), rw=w.matrix(i["L3_ffn_rw2"], False), rb=w.row(i["L3_ffn_rb2"]), rb1=w.columns(i["L3_ffn_rb1"]),
               b1=w.columns(i["L3_ffn_b1"].rearrange("e f -> (e f)")), b2=w.row(i["L3_ffn_b2"].rearrange("e d -> (e d)")))
    w.dmas.append((w.v["W1"][1], i["L3_ffn_rw1"].rearrange("(c p) f -> p c f", p=P)))
    return w


EXPERTS = {
    "l1f": ExpertPlan("l1f", None, P, 2),
    "l2fm": ExpertPlan("l2fm", ("L2_ffn_w1", "L2_ffn_w2"), 1024, 1, from_y=True),
    "l3f": ExpertPlan("l3f", ("L3_ffn_W1", "L3_ffn_W2"), 1024, 2, deep_router=True),
}


def gau_weights(chip, side):
    i, w = chip.ins, Weights(chip, "gau", side)
    n = "L3_attn_"
    w.v = dict(v=w.matrix(i[n + "Wv"]), g=w.matrix(i[n + "Wg"]), x=w.matrix(i[n + "Win"]), o=w.matrix(i[n + "Wout"]),
               bv=w.row(i[n + "bv"]), bg=w.row(i[n + "bg"]), bo=w.row(i[n + "bout"]), bx=w.columns(i[n + "bin_"]),
               mul=[w.columns(i[n + "g_" + k]) for k in ("qq", "qk", "lq", "lk")],
               add=[w.columns(i[n + "b_" + k]) for k in ("qq", "qk", "lq", "lk")])
    return w


def gau_block(chip, w, prefetch, have_stats):
    nc = chip.nc
    INNER, CH = 512, 64
    OC = INNER // P
    with ExitStack() as scope:
        sb = lambda n, s, d=F32: chip.sb(f"gau_{n}", s, d, scope)
        sem = lambda n: chip.sem(f"gau_{n}")
        yn = sb("yn", [P, GR, D])
        yT = sb("yT", [P, KC, TG])
        xs = sb("xs", [P, TG])
        feats = [sb(n, [P, TG]) for n in ("qq", "qk", "lq", "lk")]
        v = sb("v", [P, GR, INNER])
        gate = sb("gate", [P, GR, INNER])
        within = sb("within", [P, P])
        pos = sb("pos", [P, GR, P])
        aT = sb("aT", [P, GR, P])
        o = sb("o", [P, 2, INNER])
        oT = sb("oT", [P, OC, P])
        bank = [chip.ps(f"gau_bank{i}", scope) for i in range(8)]
        s = {n: sem(n) for n in ("var_ready", "std_ready")}
        yn_ready = sem("yn_ready")
        turned = [sem("turned0"), sem("turned1")]
        yT_ready = [sem("yT0_ready"), sem("yT1_ready")]
        x_filled = sem("x_filled")
        xs_ready = sem("xs_ready")
        feats_ready = sem("feats_ready")
        vg_filled = sem("vg_filled")
        vg_ready = sem("vg_ready")
        scores_ready = sem("scores_ready")
        aT_ready = sem("aT_ready")
        o_filled = sem("o_filled")
        o_ready = sem("o_ready")
        oT_filled = sem("oT_filled")
        oT_ready = sem("oT_ready")
        y_filled = sem("y_filled")
        y_added = sem("y_added")

        with nc.Block() as block:
            @block.sync
            def _(sp):
                if prefetch:
                    prefetch.load(sp)

            @block.tensor
            def _(pe):
                for x in (*turned, x_filled, vg_filled, scores_ready, o_filled, oT_filled, y_filled):
                    pe.sem_inc(x, LEAD)
                w.wait(pe)
                with pe.Fori(0, NG) as g:
                    pe.wait_ge(yn_ready, done(g))
                    for kc in range(KC):
                        pe.wait_ge(yT_ready[kc], done(g - 1))
                        for j in range(GR):
                            mm = pe.transpose(bank[kc][:, j * P:(j + 1) * P], yn[:, j, kc * P:(kc + 1) * P], chip.ident[:, :])
                        mm.then_inc(turned[kc], 1)
                    for kc in range(KC):
                        pe.wait_ge(yT_ready[kc], done(g))
                    for kc in range(KC):
                        mm = pe.matmul(bank[2][:, :], w.v["x"][:, kc, :], yT[:, kc, :], start=(kc == 0), stop=(kc == KC - 1))
                    mm.then_inc(x_filled, 1)
                    for j in range(GR):
                        for m in range(2):
                            n = g * (2 * GR) + (2 * j + m)
                            pe.wait_ge(vg_ready, done(n - 2))
                            for kc in range(KC):
                                pe.matmul(bank[4 + m][:, :], yT[:, kc, j * P:(j + 1) * P], w.v["vg"[m]][:, kc, :], start=(kc == 0), stop=False)
                            pe.matmul(bank[4 + m][:, :], chip.ones[0:1, 0:P], w.v[("bv", "bg")[m]], start=False, stop=True).then_inc(vg_filled, 1)
                    pe.wait_ge(feats_ready, done(g))
                    qq, qk, lq, lk = feats
                    for j in range(GR):
                        pe.matmul(bank[2][:, j * P:(j + 1) * P], qk[:, j * P:(j + 1) * P], qq[:, j * P:(j + 1) * P], start=True, stop=True)
                    for j in range(GR):
                        mm = pe.matmul(bank[3][0:CH, j * CH:(j + 1) * CH], lk[:, j * P:j * P + CH], lq[:, j * P + CH:(j + 1) * P], start=True, stop=True)
                    mm.then_inc(scores_ready, 1)
                    pe.wait_ge(aT_ready, done(g))
                    pe.wait_ge(vg_ready, done(g * (2 * GR) + 2 * GR - 1))

                    def attend(j):
                        pe.wait_ge(o_ready, done(g * GR + j - 2))
                        pe.matmul(bank[6 + j % 2][:, :], aT[:, j, :], v[:, j, :], start=True, stop=True).then_inc(o_filled, 1)

                    def project(j):
                        pe.wait_ge(o_ready, done(g * GR + j))
                        pe.wait_ge(oT_ready, done(g * GR + j - 1))
                        for c in range(OC):
                            mm = pe.transpose(bank[3][:, c * P:(c + 1) * P], o[:, j % 2, c * P:(c + 1) * P], chip.ident[:, :])
                        mm.then_inc(oT_filled, 1)
                        pe.wait_ge(oT_ready, done(g * GR + j))
                        pe.wait_ge(y_added, done(g * GR + j - 1))
                        for c in range(OC):
                            pe.matmul(bank[2][:, 0:D], oT[:, c, :], w.v["o"][:, c, :], start=(c == 0), stop=False)
                        pe.matmul(bank[2][:, 0:D], chip.ones[0:1, 0:P], w.v["bo"], start=False, stop=True).then_inc(y_filled, 1)

                    attend(0)
                    for j in range(GR):
                        if j + 1 < GR:
                            attend(j + 1)
                        project(j)

            @block.vector
            def _(dve):
                for x in (yn_ready, yT_ready[0], feats_ready, aT_ready, o_ready, y_added):
                    dve.sem_inc(x, LEAD)
                dve.tensor_copy(within[:, :], chip.upper[:, :])
                dve.drain()
                dve.memset(within[0:CH, CH:P], 0.0)
                ln_stats_vector(chip, dve, chip.X, s, have=have_stats)
                w.wait(dve)
                with dve.Fori(0, NG) as g:
                    for j in range(GR):
                        b = g * GR + j
                        op = dve.tensor_scalar(yn[:, j, :], chip.X[:, b, :], chip.mv[:, b, 0:1], chip.rstd[:, bass.ds(b, 1)], ALU.subtract, ALU.mult)
                    op.then_inc(yn_ready, 1)
                    dve.wait_ge(turned[0], done(g))
                    dve.tensor_copy(yT[:, 0, :], bank[0][:, :]).then_inc(yT_ready[0], 1)
                    dve.wait_ge(xs_ready, done(g))
                    for f, mul, add in zip(feats, w.v["mul"], w.v["add"]):
                        op = dve.tensor_scalar(f[:, :], xs[:, :], mul, add, ALU.mult, ALU.add)
                    op.then_inc(feats_ready, 1)
                    dve.wait_ge(scores_ready, done(g))
                    dve.tensor_scalar(pos[:, :, :], bank[2][:, :].rearrange("p (j q) -> p j q", j=GR), INNER ** -0.5, 0.0, ALU.mult, ALU.max)
                    dve.drain()
                    dve.tensor_tensor(aT[:, :, :], pos[:, :, :], within[:, :].unsqueeze(1).to_broadcast([P, GR, P]), ALU.mult)
                    dve.drain()
                    dve.tensor_tensor(aT[:, :, :], aT[:, :, :], pos[:, :, :], ALU.mult)
                    dve.drain()
                    dve.tensor_copy(aT[0:CH, :, CH:P], bank[3][0:CH, 0:GR * CH].rearrange("p (j q) -> p j q", j=GR)).then_inc(aT_ready, 1)

                    def add(j):
                        b = g * GR + j
                        dve.wait_ge(y_filled, done(b))
                        dve.tensor_tensor(chip.X[:, b, :], chip.X[:, b, :], bank[2][:, 0:D], ALU.add).then_inc(y_added, 1)

                    for j in range(GR):
                        dve.wait_ge(o_filled, done(g * GR + j))
                        if j >= 2:
                            add(j - 2)
                        dve.tensor_tensor(o[:, j % 2, :], bank[6 + j % 2][:, :], gate[:, j, :], ALU.mult).then_inc(o_ready, 1)
                    add(GR - 2)
                    add(GR - 1)

            @block.scalar
            def _(act):
                for x in (yT_ready[1], xs_ready, vg_ready, oT_ready):
                    act.sem_inc(x, LEAD)
                ln_stats_scalar(chip, act, s)
                w.wait(act)
                act.preload_act_table(ACT.Silu)
                with act.Fori(0, NG) as g:
                    act.wait_ge(turned[1], done(g))
                    act.copy(yT[:, 1, :], bank[1][:, :]).then_inc(yT_ready[1], 1)
                    act.wait_ge(x_filled, done(g))
                    act.activation(xs[:, :], bank[2][:, :], ACT.Silu, bias=w.v["bx"]).then_inc(xs_ready, 1)
                    for j in range(GR):
                        for m, dst in enumerate((v, gate)):
                            act.wait_ge(vg_filled, done(g * (2 * GR) + (2 * j + m)))
                            act.activation(dst[:, j, :], bank[4 + m][:, :], ACT.Silu).then_inc(vg_ready, 1)
                    for j in range(GR):
                        act.wait_ge(oT_filled, done(g * GR + j))
                        act.copy(oT[:, :, :], bank[3][:, :].rearrange("p (c q) -> p c q", c=OC)).then_inc(oT_ready, 1)


def l0_ffn_weights(chip, side):
    i, w = chip.ins, Weights(chip, "l0f", side)
    w.v = dict(fc=w.matrix(i["L0_ffn_W_fc"]), proj=w.matrix(i["L0_ffn_W_proj"]), g=w.columns(i["L0_ffn_ln_w"]), b=w.columns(i["L0_ffn_ln_b"]))
    return w


def ternary_ffn_block(chip, w, prefetch, have_stats):
    nc = chip.nc
    F = 1024
    FC = F // P
    with ExitStack() as scope:
        sb = lambda n, s, d=F32: chip.sb(f"l0f_{n}", s, d, scope)
        sem = lambda n: chip.sem(f"l0f_{n}")
        mag = sb("mag", [P, FC * D])
        below = sb("below", [P, FC * D])
        rowsum = sb("rowsum", [P, 2])
        half = sb("half", [P, 2])
        neghalf = sb("neghalf", [P, 2])
        allones = chip.ones[:, 0:P]
        fcT = sb("fcT", [P, KC, F])
        projT = sb("projT", [P, FC, D])
        yn = sb("yn", [P, GR, D])
        yT = sb("yT", [P, KC, TG])
        h = sb("h", [P, GR, F])
        hT = sb("hT", [P, FC, TG])
        hbn = sb("hbn", [P, GR, 2, 6])
        hmv = sb("hmv", [P, GR, 2])
        hvar = sb("hvar", [P, GR])
        hstd = sb("hstd", [P, GR])
        hrstd = sb("hrstd", [P, GR])
        tbank = [chip.ps(f"l0f_turn{i}", scope) for i in range(2)]
        hbank = [chip.ps(f"l0f_hidden{i}", scope) for i in range(2)]
        obank = [chip.ps(f"l0f_out{i}", scope) for i in range(2)]
        s = {n: sem(n) for n in ("var_ready", "std_ready")}
        mags_ready = sem("mags_ready")
        sums_ready = sem("sums_ready")
        ternary_ready = sem("ternary_ready")
        yn_ready = sem("yn_ready")
        turned = [sem("turned0"), sem("turned1")]
        copied = [sem("copied0"), sem("copied1")]
        h_filled = sem("h_filled")
        gelu_done = sem("gelu_done")
        hvar_ready, hstd_ready = sem("hvar_ready"), sem("hstd_ready")
        hn_ready = sem("hn_ready")
        out_filled, out_added = sem("out_filled"), sem("out_added")
        WT = (FC * KC // 4)
        PER = 1 + FC // 2
        weight_turns = 2 * WT // 2

        with nc.Block() as block:
            @block.sync
            def _(sp):
                if prefetch:
                    prefetch.load(sp)

            @block.tensor
            def _(pe):
                for x in (*turned, h_filled, out_filled):
                    pe.sem_inc(x, LEAD)
                pe.wait_ge(mags_ready, 2)
                pe.matmul(obank[0][:, 0:2], allones, rowsum[:, :], start=True, stop=True).then_inc(sums_ready, 1)
                n = 0
                for m, src in enumerate((w.v["fc"], w.v["proj"])):
                    pe.wait_ge(ternary_ready, m + 1)
                    for q in range(WT):
                        b = n % 2
                        pe.wait_ge(copied[b], done(n // 2 - 1))
                        for i in range(4):
                            r, c = (q % 2 * 4 + i, q // 2) if m == 0 else (q // 2, q % 2 * 4 + i)
                            mm = pe.transpose(tbank[b][:, i * P:(i + 1) * P], src[:, r, c * P:(c + 1) * P], chip.ident[:, :])
                        mm.then_inc(turned[b], 1)
                        n += 1
                with pe.Fori(0, NG) as g:
                    pe.wait_ge(yn_ready, done(g))
                    for kc in range(KC):
                        pe.wait_ge(copied[kc], done(g * PER + weight_turns - 1))
                        for j in range(GR):
                            mm = pe.transpose(tbank[kc][:, j * P:(j + 1) * P], yn[:, j, kc * P:(kc + 1) * P], chip.ident[:, :])
                        mm.then_inc(turned[kc], 1)
                    for kc in range(KC):
                        pe.wait_ge(copied[kc], done(g * PER + weight_turns))
                    for j in range(GR):
                        for c in range(2):
                            pe.wait_ge(gelu_done, done(g * (2 * GR) + (2 * j + c) - 2))
                            for kc in range(KC):
                                mm = pe.matmul(hbank[c][:, :], yT[:, kc, j * P:(j + 1) * P], fcT[:, kc, c * 512:(c + 1) * 512],
                                               start=(kc == 0), stop=(kc == KC - 1))
                            mm.then_inc(h_filled, 1)
                    pe.wait_ge(hn_ready, done(g))
                    for f in range(FC):
                        b = f % 2
                        pe.wait_ge(copied[b], done(g * PER + weight_turns + f // 2))
                        for j in range(GR):
                            mm = pe.transpose(tbank[b][:, j * P:(j + 1) * P], h[:, j, f * P:(f + 1) * P], chip.ident[:, :])
                        mm.then_inc(turned[b], 1)
                    for b in range(2):
                        pe.wait_ge(copied[b], done(g * PER + weight_turns + FC // 2))
                    for j in range(GR):
                        pe.wait_ge(out_added, done(g * GR + j - 2))
                        for f in range(FC):
                            mm = pe.matmul(obank[j % 2][:, 0:D], hT[:, f, j * P:(j + 1) * P], projT[:, f, :], start=(f == 0), stop=(f == FC - 1))
                        mm.then_inc(out_filled, 1)

            def copy_weight(eng, b):
                n = 0
                for m in range(2):
                    for q in range(WT):
                        if n % 2 == b:
                            eng.wait_ge(turned[b], done(n // 2))
                            src = tbank[b][:, :]
                            if m == 0:
                                dst = fcT[:, q // 2, q % 2 * 512:(q % 2 + 1) * 512]
                            else:
                                dst = projT[:, q % 2 * 4:q % 2 * 4 + 4, q // 2 * P:(q // 2 + 1) * P]
                                src = src.rearrange("p (i d) -> p i d", i=4)
                            (eng.tensor_copy(dst, src) if b == 0 else eng.copy(dst, src)).then_inc(copied[b], 1)
                        n += 1

            @block.vector
            def _(dve):
                for x in (copied[0], yn_ready, hvar_ready, hn_ready, out_added):
                    dve.sem_inc(x, LEAD)
                ln_stats_vector(chip, dve, chip.X, s, have=have_stats)
                w.wait(dve)
                dve.wait_ge(sums_ready, 1)
                dve.tensor_scalar(half[:, :], obank[0][:, 0:2], 1.0 / (F * D), 1e-6, ALU.mult, ALU.add)
                dve.drain()
                dve.tensor_scalar(neghalf[:, :], half[:, :], -0.5, None, ALU.mult)
                dve.tensor_scalar(half[:, :], half[:, :], 0.5, None, ALU.mult)
                dve.drain()
                for m, src in enumerate((w.v["fc"], w.v["proj"])):
                    flat = src.rearrange("p c n -> p (c n)")
                    dve.tensor_scalar(below[:, :], flat, neghalf[:, m:m + 1], None, ALU.is_lt)
                    dve.drain()
                    dve.scalar_tensor_tensor(out=flat, in0=flat, scalar=half[:, m:m + 1], in1=below[:, :], op0=ALU.is_gt,
                                             op1=ALU.subtract).then_inc(ternary_ready, 1)
                    dve.drain()
                copy_weight(dve, 0)
                with dve.Fori(0, NG) as g:
                    for j in range(GR):
                        b = g * GR + j
                        op = dve.tensor_scalar(yn[:, j, :], chip.X[:, b, :], chip.mv[:, b, 0:1], chip.rstd[:, bass.ds(b, 1)], ALU.subtract, ALU.mult)
                    op.then_inc(yn_ready, 1)
                    dve.wait_ge(turned[0], done(g * PER + weight_turns))
                    dve.tensor_copy(yT[:, 0, :], tbank[0][:, :]).then_inc(copied[0], 1)
                    for j in range(GR):
                        dve.wait_ge(gelu_done, done(g * (2 * GR) + 2 * j + 1))
                        for c in range(2):
                            dve.bn_stats(hbn[:, j, c, :], h[:, j, c * 512:(c + 1) * 512])
                        dve.drain()
                        dve.bn_aggr(hmv[:, j, :], hbn[:, j, :, :])
                    dve.drain()
                    dve.tensor_scalar(hvar[:, :], hmv[:, :, 1], LN_EPS, None, ALU.add).then_inc(hvar_ready, 1)
                    dve.wait_ge(hstd_ready, done(g))
                    dve.reciprocal(hrstd[:, :], hstd[:, :])
                    dve.drain()
                    for j in range(GR):
                        op = dve.tensor_scalar(h[:, j, :], h[:, j, :], hmv[:, j, 0:1], hrstd[:, j:j + 1], ALU.subtract, ALU.mult)
                    op.then_inc(hn_ready, 1)
                    for f in range(0, FC, 2):
                        dve.wait_ge(turned[0], done(g * PER + weight_turns + 1 + f // 2))
                        dve.tensor_scalar(hT[:, f, :], tbank[0][:, :], w.v["g"][:, f:f + 1], w.v["b"][:, f:f + 1], ALU.mult, ALU.add).then_inc(copied[0], 1)
                    for j in range(GR):
                        b = g * GR + j
                        dve.wait_ge(out_filled, done(b))
                        dve.tensor_tensor(chip.X[:, b, :], chip.X[:, b, :], obank[j % 2][:, 0:D], ALU.add).then_inc(out_added, 1)

            @block.scalar
            def _(act):
                for x in (copied[1], gelu_done, hstd_ready):
                    act.sem_inc(x, LEAD)
                w.wait(act)
                for m, src in enumerate((w.v["fc"], w.v["proj"])):
                    act.activation(mag[:, :], src.rearrange("p c n -> p (c n)"), ACT.Abs, accum_out=rowsum[:, m:m + 1]).then_inc(mags_ready, 1)
                    act.drain()
                ln_stats_scalar(chip, act, s)
                copy_weight(act, 1)
                with act.Fori(0, NG) as g:
                    act.wait_ge(turned[1], done(g * PER + weight_turns))
                    act.copy(yT[:, 1, :], tbank[1][:, :]).then_inc(copied[1], 1)
                    for j in range(GR):
                        for c in range(2):
                            act.wait_ge(h_filled, done(g * (2 * GR) + (2 * j + c)))
                            act.activation(h[:, j, c * 512:(c + 1) * 512], hbank[c][:, :], ACT.Gelu).then_inc(gelu_done, 1)
                    act.wait_ge(hvar_ready, done(g))
                    act.activation(hstd[:, :], hvar[:, :], ACT.Sqrt).then_inc(hstd_ready, 1)
                    for f in range(1, FC, 2):
                        act.wait_ge(turned[1], done(g * PER + weight_turns + 1 + f // 2))
                        act.activation(hT[:, f, :], tbank[1][:, :], ACT.Identity, bias=w.v["b"][:, f:f + 1], scale=w.v["g"][:, f:f + 1]).then_inc(copied[1], 1)


def l1_xattn_weights(chip, side):
    i, w = chip.ins, Weights(chip, "l1x", side)
    n = "L1_xattn_"
    q = w.room(KC * 192).rearrange("p (c n) -> p c n", c=KC)
    w.dmas.append((q[:, :, 0:128], i[n + "w_off"].rearrange("(c p) n -> p c n", p=P)))
    w.dmas.append((q[:, :, 128:192], i[n + "w_attw"].rearrange("(c p) n -> p c n", p=P)))
    bq = w.room(192, False)[0:1, :]
    w.dmas.append((bq[:, 0:128], i[n + "b_off"].rearrange("(a n) -> a n", a=1)))
    w.dmas.append((bq[:, 128:192], i[n + "b_attw"].rearrange("(a n) -> a n", a=1)))
    w.v = dict(q=q, bq=bq, v=w.matrix(i[n + "w_value"]), o=w.matrix(i[n + "w_out"]), bv=w.row(i[n + "b_value"]), bo=w.row(i[n + "b_out"]))
    return w


def deform_block(chip, w, prefetch, have_stats):
    nc, ins = chip.nc, chip.ins
    H, NPT, HD = 16, 4, 16
    HP = H * NPT
    J0 = P // 2 - 1
    NJ = P - J0
    QW = 3 * HP
    with ExitStack() as scope:
        sb = lambda n, s, d=F32: chip.sb(f"l1x_{n}", s, d, scope)
        sem = lambda n: chip.sem(f"l1x_{n}")
        yn = sb("yn", [P, GR, D])
        yT = sb("yT", [P, KC, TG])
        cn = sb("cn", [NJ, GR, D])
        cT = sb("cT", [P, KC, GR, NJ])
        v = sb("v", [NJ, GR, D])
        q = sb("q", [P, GR, QW])
        ix = sb("ix", [P, GR, HP])
        hy = sb("hy", [P, GR, HP])
        aw = sb("aw", [P, GR, HP])
        amax = sb("amax", [P, GR * H])
        asum = sb("asum", [P, GR * H])
        rows_i = sb("rows_i", [P, NJ], I32)
        rows = sb("rows", [P, NJ])
        ref_i = sb("ref_i", [P, 1], I32)
        ref = sb("ref", [P, 1])
        hat = sb("hat", [P, 2, HP, NJ])
        wsum = sb("wsum", [P, 2, H, NJ])
        wT = sb("wT", [NJ, 2, H // 2, P])
        on = sb("on", [P, D])
        oT = sb("oT", [P, KC, P])
        bank = [chip.ps(f"l1x_bank{i}", scope) for i in range(8)]
        s = {n: sem(n) for n in ("var_ready", "std_ready")}
        iota_ready = sem("iota_ready")
        rows_ready = sem("rows_ready")
        ctx_loaded = sem("ctx_loaded")
        yn_ready = sem("yn_ready")
        turned = [sem("turned0"), sem("turned1")]
        copied = [sem("copied0"), sem("copied1")]
        q_filled = [sem("q0_filled"), sem("q1_filled")]
        q_copied = [sem("q0_copied"), sem("q1_copied")]
        v_filled, v_copied = sem("v_filled"), sem("v_copied")
        logits_ready, exp_ready = sem("logits_ready"), sem("exp_ready")
        points_ready = sem("points_ready")
        dist_ready = sem("dist_ready")
        hat_ready = sem("hat_ready")
        wsum_ready = sem("wsum_ready")
        w_turned = sem("w_turned")
        w_copied = sem("w_copied")
        o_filled, o_copied = sem("o_filled"), sem("o_copied")
        oT_filled, oT_copied = sem("oT_filled"), sem("oT_copied")
        y_filled, y_added = sem("y_filled"), sem("y_added")

        with nc.Block() as block:
            @block.sync
            def _(sp):
                sp.dma_start(cn[:, :, :], ins["ctx_1024"][0:GR, J0:P, :].rearrange("b s d -> s b d")).then_inc(ctx_loaded, 16)
                if prefetch:
                    prefetch.load(sp)
                with sp.Fori(0, NG - 1) as g:
                    for kc in range(KC):
                        sp.wait_ge(turned[kc], done(g * 2 + 1))
                    sp.dma_start(cn[:, :, :], ins["ctx_1024"][bass.ds(g * GR + GR, GR), J0:P, :].rearrange("b s d -> s b d")).then_inc(ctx_loaded, 16)

            @block.gpsimd
            def _(pool):
                pool.iota(rows_i[:, :], [[1, NJ]], base=J0, channel_multiplier=0).then_inc(iota_ready, 1)
                pool.iota(ref_i[:, :], [[0, 1]], base=0, channel_multiplier=1).then_inc(iota_ready, 1)
                pool.sem_inc(dist_ready, LEAD)
                pool.wait_ge(rows_ready, 1)
                with pool.Fori(0, NG) as g:
                    pool.wait_ge(points_ready, done(g))
                    for j in range(GR):
                        pool.wait_ge(wsum_ready, done(g * GR + j - 2))
                        pool.tensor_tensor(hat[:, j % 2, :, :], rows[:, :].unsqueeze(1).to_broadcast([P, HP, NJ]),
                                           ix[:, j, :].unsqueeze(2).to_broadcast([P, HP, NJ]), ALU.subtract).then_inc(dist_ready, 1)

            @block.tensor
            def _(pe):
                for x in (*turned, *q_filled, v_filled, w_turned, o_filled, oT_filled, y_filled):
                    pe.sem_inc(x, LEAD)
                w.wait(pe)
                with pe.Fori(0, NG) as g:
                    pe.wait_ge(yn_ready, done(g))
                    for kc in range(KC):
                        pe.wait_ge(copied[kc], done(g * 2 - 1))
                        for j in range(GR):
                            mm = pe.transpose(bank[kc][:, j * P:(j + 1) * P], yn[:, j, kc * P:(kc + 1) * P], chip.ident[:, :])
                        mm.then_inc(turned[kc], 1)
                    pe.wait_ge(ctx_loaded, g * 16 + 16)
                    for kc in range(KC):
                        pe.wait_ge(copied[kc], done(g * 2))
                        for j in range(GR):
                            mm = pe.transpose(bank[kc][:, j * NJ:(j + 1) * NJ], cn[:, j, kc * P:(kc + 1) * P], chip.ident[0:NJ, 0:NJ])
                        mm.then_inc(turned[kc], 1)
                    for i in range(2):
                        for j in range(2):
                            o = bank[2 + i][:, j * QW:(j + 1) * QW]
                            for kc in range(KC):
                                pe.matmul(o, yT[:, kc, (2 * i + j) * P:(2 * i + j + 1) * P], w.v["q"][:, kc, :], start=(kc == 0), stop=False)
                            mm = pe.matmul(o, chip.ones[0:1, 0:P], w.v["bq"], start=False, stop=True)
                        mm.then_inc(q_filled[i], 1)
                    for kc in range(KC):
                        pe.wait_ge(copied[kc], done(g * 2 + 1))
                    for j in range(GR):
                        pe.wait_ge(v_copied, done(g * GR + j - 1))
                        for kc in range(KC):
                            pe.matmul(bank[4][0:NJ, 0:D], cT[:, kc, j, :], w.v["v"][:, kc, :], start=(kc == 0), stop=False)
                        pe.matmul(bank[4][0:NJ, 0:D], chip.ones[0:1, 0:NJ], w.v["bv"], start=False, stop=True).then_inc(v_filled, 1)
                    for i in range(2):
                        pe.wait_ge(q_copied[i], done(g))
                    pe.wait_ge(v_copied, done(g * GR + GR - 1))
                    for j in range(GR):
                        n = g * GR + j
                        pe.wait_ge(wsum_ready, done(n))
                        pe.wait_ge(o_copied, done(n - 1))
                        for u in range(H // 4):
                            m = n * (H // 4) + u
                            pe.wait_ge(w_copied, done(m - 2))
                            for i in range(4):
                                mm = pe.transpose(bank[5 + u % 2][0:NJ, i * P:(i + 1) * P], wsum[:, j % 2, u * 4 + i, :], chip.ident[:, :])
                            mm.then_inc(w_turned, 1)
                            pe.wait_ge(w_copied, done(m))
                            for i in range(4):
                                h = u * 4 + i
                                mm = pe.matmul(bank[7][:, h * HD:(h + 1) * HD], wT[:, u % 2, i, :], v[:, j, h * HD:(h + 1) * HD], start=True, stop=True)
                        mm.then_inc(o_filled, 1)
                        pe.wait_ge(o_copied, done(n))
                        pe.wait_ge(oT_copied, done(n - 1))
                        for c in range(KC):
                            mm = pe.transpose(bank[2][:, c * P:(c + 1) * P], on[:, c * P:(c + 1) * P], chip.ident[:, :])
                        mm.then_inc(oT_filled, 1)
                        pe.wait_ge(oT_copied, done(n))
                        pe.wait_ge(y_added, done(n - 1))
                        for c in range(KC):
                            pe.matmul(bank[3][:, 0:D], oT[:, c, :], w.v["o"][:, c, :], start=(c == 0), stop=False)
                        pe.matmul(bank[3][:, 0:D], chip.ones[0:1, 0:P], w.v["bo"], start=False, stop=True).then_inc(y_filled, 1)

            @block.vector
            def _(dve):
                for x in (copied[0], q_copied[0], yn_ready, logits_ready, points_ready, wsum_ready, o_copied, y_added):
                    dve.sem_inc(x, LEAD)
                dve.wait_ge(iota_ready, 2)
                dve.tensor_copy(rows[:, :], rows_i[:, :])
                dve.tensor_copy(ref[:, :], ref_i[:, :])
                dve.drain()
                dve.sem_inc(rows_ready, 1)
                dve.tensor_scalar(ref[:, :], ref[:, :], 1.0 / (P - 1), None, ALU.mult)
                ln_stats_vector(chip, dve, chip.X, s, have=have_stats)
                w.wait(dve)
                with dve.Fori(0, NG) as g:
                    for j in range(GR):
                        b = g * GR + j
                        op = dve.tensor_scalar(yn[:, j, :], chip.X[:, b, :], chip.mv[:, b, 0:1], chip.rstd[:, bass.ds(b, 1)], ALU.subtract, ALU.mult)
                    op.then_inc(yn_ready, 1)
                    dve.wait_ge(turned[0], done(g * 2))
                    dve.tensor_copy(yT[:, 0, :], bank[0][:, :]).then_inc(copied[0], 1)
                    dve.wait_ge(turned[0], done(g * 2 + 1))
                    dve.tensor_copy(cT[:, 0, :, :], bank[0][:, 0:GR * NJ].rearrange("p (j t) -> p j t", j=GR)).then_inc(copied[0], 1)
                    dve.wait_ge(q_filled[0], done(g))
                    dve.tensor_copy(q[:, 0:2, :], bank[2][:, 0:2 * QW].rearrange("p (j n) -> p j n", j=2)).then_inc(q_copied[0], 1)
                    dve.drain()
                    dve.wait_ge(q_copied[1], done(g))
                    offs = q[:, :, 0:2 * HP].rearrange("p j (n t) -> p j n t", t=2)
                    logit = q[:, :, 2 * HP:QW]
                    four = lambda x: x[:, :, :].rearrange("p j (h t) -> p (j h) t", t=NPT)
                    per_head = lambda x: x[:, :].unsqueeze(2).to_broadcast([P, GR * H, NPT])
                    dve.tensor_copy(aw[:, :, :], logit)
                    dve.drain()
                    dve.tensor_reduce(amax[:, :], four(aw), AX.X, ALU.max)
                    dve.drain()
                    dve.tensor_tensor(four(aw), four(aw), per_head(amax), ALU.subtract).then_inc(logits_ready, 1)
                    dve.tensor_scalar(ix[:, :, :], offs[:, :, :, 0], 0.0, 1.0, ALU.max, ALU.min)
                    dve.tensor_scalar(hy[:, :, :], offs[:, :, :, 1], ref[:, 0:1], 0.0, ALU.add, ALU.max)
                    dve.drain()
                    dve.tensor_scalar(ix[:, :, :], ix[:, :, :], 1.0, float(P), ALU.add, ALU.mult)
                    dve.tensor_scalar(hy[:, :, :], hy[:, :, :], 1.0, 1.0, ALU.min, ALU.add)
                    dve.drain()
                    dve.tensor_scalar(ix[:, :, :], ix[:, :, :], -1.0, 0.5, ALU.add, ALU.mult)
                    dve.tensor_scalar(hy[:, :, :], hy[:, :, :], -1.0, -0.5, ALU.add, ALU.mult)
                    dve.drain()
                    dve.tensor_scalar(hy[:, :, :], hy[:, :, :], 1.0, None, ALU.add)
                    dve.wait_ge(exp_ready, done(g))
                    dve.tensor_reduce(asum[:, :], four(aw), AX.X, ALU.add)
                    dve.drain()
                    dve.reciprocal(asum[:, :], asum[:, :])
                    dve.tensor_tensor(aw[:, :, :], aw[:, :, :], hy[:, :, :], ALU.mult)
                    dve.drain()
                    dve.tensor_tensor(four(aw), four(aw), per_head(asum), ALU.mult).then_inc(points_ready, 1)
                    dve.drain()

                    def add(j):
                        b = g * GR + j
                        dve.wait_ge(y_filled, done(b))
                        dve.tensor_tensor(chip.X[:, b, :], chip.X[:, b, :], bank[3][:, 0:D], ALU.add).then_inc(y_added, 1)

                    def copy_out(j):
                        dve.wait_ge(o_filled, done(g * GR + j))
                        dve.tensor_copy(on[:, :], bank[7][:, 0:D]).then_inc(o_copied, 1)

                    for j in range(GR):
                        n = g * GR + j
                        dve.wait_ge(hat_ready, done(n))
                        dve.tensor_tensor(hat[:, j % 2, :, :], hat[:, j % 2, :, :], aw[:, j, :].unsqueeze(2).to_broadcast([P, HP, NJ]), ALU.mult)
                        dve.drain()
                        if j >= 2:
                            add(j - 2)
                        dve.tensor_reduce(wsum[:, j % 2, :, :], hat[:, j % 2, :, :].rearrange("p (h t) n -> p h n t", t=NPT), AX.X, ALU.add).then_inc(wsum_ready, 1)
                        if j >= 1:
                            copy_out(j - 1)
                    add(GR - 2)
                    copy_out(GR - 1)
                    add(GR - 1)

            @block.scalar
            def _(act):
                for x in (copied[1], q_copied[1], v_copied, exp_ready, hat_ready, w_copied, oT_copied):
                    act.sem_inc(x, LEAD)
                ln_stats_scalar(chip, act, s)
                act.preload_act_table(ACT.Exp)
                with act.Fori(0, NG) as g:
                    act.wait_ge(turned[1], done(g * 2))
                    act.copy(yT[:, 1, :], bank[1][:, :]).then_inc(copied[1], 1)
                    act.wait_ge(turned[1], done(g * 2 + 1))
                    act.copy(cT[:, 1, :, :], bank[1][:, 0:GR * NJ].rearrange("p (j t) -> p j t", j=GR)).then_inc(copied[1], 1)
                    act.wait_ge(q_filled[1], done(g))
                    act.copy(q[:, 2:4, :], bank[3][:, 0:2 * QW].rearrange("p (j n) -> p j n", j=2)).then_inc(q_copied[1], 1)
                    for j in range(GR):
                        act.wait_ge(v_filled, done(g * GR + j))
                        act.copy(v[:, j, :], bank[4][0:NJ, 0:D]).then_inc(v_copied, 1)
                    act.wait_ge(logits_ready, done(g))
                    act.activation(aw[:, :, :], aw[:, :, :], ACT.Exp).then_inc(exp_ready, 1)

                    def weigh(j):
                        act.wait_ge(dist_ready, done(g * GR + j))
                        act.activation(hat[:, j % 2, :, :], hat[:, j % 2, :, :], ACT.Abs)
                        act.drain()
                        act.activation(hat[:, j % 2, :, :], hat[:, j % 2, :, :], ACT.Relu, bias=1.0, scale=-1.0).then_inc(hat_ready, 1)

                    weigh(0)
                    for j in range(GR):
                        if j + 1 < GR:
                            weigh(j + 1)
                        n = g * GR + j
                        for u in range(H // 4):
                            act.wait_ge(w_turned, done(n * (H // 4) + u))
                            act.copy(wT[:, u % 2, 0:4, :], bank[5 + u % 2][0:NJ, :].rearrange("p (i q) -> p i q", i=4)).then_inc(w_copied, 1)
                        act.wait_ge(oT_filled, done(n))
                        act.copy(oT[:, :, :], bank[2][:, 0:D].rearrange("p (c q) -> p c q", c=KC)).then_inc(oT_copied, 1)


def rwkv_weights(chip, side):
    i, w = chip.ins, Weights(chip, "rwkv", side)
    n = "L0_attn_"
    w.v = dict(k=w.matrix(i[n + "W_key"]), v=w.matrix(i[n + "W_value"]), r=w.matrix(i[n + "W_recept"]), o=w.matrix(i[n + "W_out"]),
               k2=w.matrix(i[n + "W_key2"]), v2=w.matrix(i[n + "W_value2"]), r2=w.matrix(i[n + "W_recept2"]))
    for m in ("ln1_w", "ln2_w", "time_decay", "time_first", "time_mix_k", "time_mix_v", "time_mix_r", "time_mix_k2", "time_mix_r2"):
        w.v[m] = w.columns(i[n + m])
    return w


def rwkv_block(chip, w, prefetch, have_stats):
    nc = chip.nc
    W1 = P + 1
    F = 1024
    FC = F // P
    with ExitStack() as scope:
        sb = lambda n, s, d=F32: chip.sb(f"rwkv_{n}", s, d, scope)
        sem = lambda n: chip.sem(f"rwkv_{n}")
        y = sb("y", [P, GR, D])
        hn = sb("hn", [P, GR, D])
        hT = sb("hT", [P, KC, GR, W1])
        diff = sb("diff", [P, KC, GR, P])
        mix = [sb(f"mix_{m}", [P, KC, TG]) for m in "kvr"]
        decay = sb("decay", [P, KC])
        decays = sb("decays", [P, KC, GR, W1])
        kc_ = sb("k_clipped", [P, TG])
        ku = sb("ku_clipped", [P, TG])
        ek = sb("ek", [P, KC, GR, W1])
        ekv = sb("ekv", [P, KC, GR, W1])
        eku = sb("eku", [P, TG])
        er = sb("er", [P, TG])
        sa = sb("sum_ekv", [P, GR, W1])
        sbk = sb("sum_ek", [P, GR, W1])
        num = sb("num", [P, TG])
        den = sb("den", [P, TG])
        rw = sb("rw", [P, KC, TG])
        sq = sb("sq", [P, D])
        ms = sb("ms", [P, GR])
        root = sb("root", [P, GR])
        rms = sb("rms", [P, GR])
        kr = sb("kr", [P, 2, TG])
        k2 = sb("k2", [P, FC, TG])
        r2 = sb("r2", [P, 2, D])
        kv = sb("kv", [P, D])
        bank = [chip.ps(f"rwkv_bank{i}", scope) for i in range(8)]
        s = {n: sem(n) for n in ("var_ready", "std_ready")}
        decay_step = sem("decay_step")
        decay_back = sem("decay_back")
        hn_ready = sem("hn_ready")
        filled = [sem("bank0_filled"), sem("bank1_filled")]
        emptied = [sem("bank0_emptied"), sem("bank1_emptied")]
        mix_ready = sem("mix_ready")
        kvr_filled = sem("kvr_filled")
        clipped = sem("clipped")
        exps_ready = sem("exps_ready")
        rw_ready = sem("rw_ready")
        y_filled, y_ready = sem("y_filled"), sem("y_ready")
        ms_ready, root_ready = sem("ms_ready"), sem("root_ready")
        relu_ready = [sem("relu0_ready"), sem("relu1_ready")]
        k2_ready = sem("k2_ready")
        r2_filled, r2_exp = sem("r2_filled"), sem("r2_exp")
        r2_used = sem("r2_used")
        kv_filled, kv_added = sem("kv_filled"), sem("kv_added")
        PER = 2 + FC // 2

        with nc.Block() as block:
            @block.sync
            def _(sp):
                if prefetch:
                    prefetch.load(sp)

            @block.tensor
            def _(pe):
                for x in (*filled, kvr_filled, y_filled, r2_filled, kv_filled):
                    pe.sem_inc(x, LEAD)
                w.wait(pe)
                with pe.Fori(0, NG) as g:
                    def turn(n):
                        pe.wait_ge(hn_ready, done(g * 2 + n))
                        for kc in range(KC):
                            pe.wait_ge(emptied[kc], done(g * PER + n - 1))
                            for j in range(GR):
                                mm = pe.transpose(bank[kc][:, j * P:(j + 1) * P], hn[:, j, kc * P:(kc + 1) * P], chip.ident[:, :])
                            mm.then_inc(filled[kc], 1)

                    turn(0)
                    pe.wait_ge(mix_ready, done(g * 2))
                    for m in range(KC):
                        for i, name in enumerate("kvr"):
                            for kc in range(KC):
                                mm = pe.matmul(bank[2 + 2 * i + m][:, :], w.v[name][:, kc, m * P:(m + 1) * P], mix[i][:, kc, :],
                                               start=(kc == 0), stop=(kc == KC - 1))
                        mm.then_inc(kvr_filled, 1)
                    pe.wait_ge(rw_ready, done(g * 2 + 1))
                    for j in range(GR):
                        pe.wait_ge(y_ready, done(g * GR + j - 2))
                        for kc in range(KC):
                            mm = pe.matmul(bank[2 + j % 2][:, 0:D], rw[:, kc, j * P:(j + 1) * P], w.v["o"][:, kc, :], start=(kc == 0), stop=(kc == KC - 1))
                        mm.then_inc(y_filled, 1)
                    turn(1)
                    pe.wait_ge(mix_ready, done(g * 2 + 1))
                    for f in range(FC):
                        b = f % 2
                        pe.wait_ge(emptied[b], done(g * PER + 1 + f // 2))
                        for kc in range(KC):
                            mm = pe.matmul(bank[b][:, :], w.v["k2"][:, kc, f * P:(f + 1) * P], mix[0][:, kc, :], start=(kc == 0), stop=(kc == KC - 1))
                        mm.then_inc(filled[b], 1)
                    for j in range(GR):
                        pe.wait_ge(r2_exp, done(g * GR + j - 2))
                        for kc in range(KC):
                            mm = pe.matmul(bank[4 + j % 2][:, 0:D], mix[2][:, kc, j * P:(j + 1) * P], w.v["r2"][:, kc, :], start=(kc == 0), stop=(kc == KC - 1))
                        mm.then_inc(r2_filled, 1)
                        if j == 0:
                            pe.wait_ge(k2_ready, done(g * FC + FC - 1))
                        pe.wait_ge(kv_added, done(g * GR + j - 2))
                        for f in range(FC):
                            mm = pe.matmul(bank[6 + j % 2][:, 0:D], k2[:, f, j * P:(j + 1) * P], w.v["v2"][:, f, :], start=(f == 0), stop=(f == FC - 1))
                        mm.then_inc(kv_filled, 1)

            @block.vector
            def _(dve):
                for x in (hn_ready, emptied[0], mix_ready, clipped, rw_ready, y_ready, ms_ready, relu_ready[0], r2_used, kv_added):
                    dve.sem_inc(x, LEAD)
                w.wait(dve)
                for z in (hT, ek, ekv):
                    dve.memset(z[:, :, :, 0:1], 0.0)
                ln_stats_vector(chip, dve, chip.X, s, twice=True, second_eps=1e-6, have=have_stats)
                dve.wait_ge(decay_step, 1)
                dve.tensor_scalar(decay[:, :], decay[:, :], -1.0, -20.0, ALU.mult, ALU.max)
                dve.drain()
                dve.tensor_scalar(decay[:, :], decay[:, :], 20.0, None, ALU.min).then_inc(decay_back, 1)
                dve.wait_ge(decay_step, 2)
                for kc in range(KC):
                    for j in range(GR):
                        dve.tensor_scalar(decays[:, kc, j, 1:W1], chip.ones[:, 0:P], decay[:, kc:kc + 1], None, ALU.mult)
                dve.memset(decays[:, :, :, 0:1], 0.0)
                dve.drain()
                with dve.Fori(0, NG) as g:
                    def shift(n, weight, mixes):
                        dve.wait_ge(filled[0], done(g * PER + n))
                        dve.tensor_scalar(hT[:, 0, :, 1:W1], bank[0][:, :].rearrange("p (j t) -> p j t", j=GR), weight[:, 0:1], None, ALU.mult).then_inc(emptied[0], 1)
                        dve.drain()
                        dve.wait_ge(emptied[1], done(g * PER + n))
                        dve.tensor_tensor(diff[:, :, :, :], hT[:, :, :, 1:W1], hT[:, :, :, 0:P], ALU.subtract)
                        dve.drain()
                        for i, name in mixes:
                            for kc in range(KC):
                                op = dve.scalar_tensor_tensor(out=mix[i][:, kc, :].rearrange("p (j t) -> p j t", j=GR), in0=diff[:, kc, :, :],
                                                              scalar=w.v[name][:, kc:kc + 1], in1=hT[:, kc, :, 0:P], op0=ALU.mult, op1=ALU.add)
                        op.then_inc(mix_ready, 1)

                    for j in range(GR):
                        b = g * GR + j
                        dve.tensor_scalar(y[:, j, :], chip.X[:, b, :], chip.mv[:, b, 0:1], chip.rstd[:, bass.ds(b, 1)], ALU.subtract, ALU.mult)
                        op = dve.tensor_scalar(hn[:, j, :], chip.X[:, b, :], chip.mv[:, b, 0:1], chip.rstd2[:, bass.ds(b, 1)], ALU.subtract, ALU.mult)
                    op.then_inc(hn_ready, 1)
                    shift(0, w.v["ln1_w"], [(0, "time_mix_k"), (1, "time_mix_v"), (2, "time_mix_r")])
                    as3 = lambda x: x.rearrange("p (j t) -> p j t", j=GR)
                    for m in range(KC):
                        dve.wait_ge(kvr_filled, done(g * KC + m))
                        u = w.v["time_first"][:, m:m + 1]
                        dve.tensor_scalar(ku[:, :], bank[2 + m][:, :], u, -20.0, ALU.add, ALU.max)
                        dve.tensor_scalar(kc_[:, :], bank[2 + m][:, :], -20.0, 20.0, ALU.max, ALU.min)
                        dve.drain()
                        dve.tensor_scalar(ku[:, :], ku[:, :], 20.0, None, ALU.min).then_inc(clipped, 1)
                        dve.wait_ge(exps_ready, done(g * KC + m))
                        dve.tensor_tensor(ekv[:, m, :, 1:W1], ek[:, m, :, 1:W1], as3(bank[4 + m][:, :]), ALU.mult)
                        dve.tensor_tensor(num[:, :], eku[:, :], bank[4 + m][:, :], ALU.mult)
                        dve.drain()
                        flat = lambda x: x.rearrange("p j t -> p (j t)")
                        dve.tensor_tensor_scan(flat(sa[:, :, :]), flat(decays[:, m, :, :]), flat(ekv[:, m, :, :]), 0.0, ALU.mult, ALU.add)
                        dve.tensor_tensor_scan(flat(sbk[:, :, :]), flat(decays[:, m, :, :]), flat(ek[:, m, :, :]), 0.0, ALU.mult, ALU.add)
                        dve.drain()
                        dve.tensor_tensor(as3(num[:, :]), as3(num[:, :]), sa[:, :, 0:P], ALU.add)
                        dve.scalar_tensor_tensor(out=as3(den[:, :]), in0=as3(eku[:, :]), scalar=1e-8, in1=sbk[:, :, 0:P], op0=ALU.add, op1=ALU.add)
                        dve.drain()
                        dve.scalar_tensor_tensor(out=den[:, :], in0=er[:, :], scalar=1.0, in1=den[:, :], op0=ALU.add, op1=ALU.mult)
                        dve.drain()
                        dve.reciprocal(den[:, :], den[:, :])
                        dve.drain()
                        dve.tensor_tensor(rw[:, m, :], num[:, :], den[:, :], ALU.mult).then_inc(rw_ready, 1)
                    for j in range(GR):
                        dve.wait_ge(y_filled, done(g * GR + j))
                        dve.tensor_tensor(y[:, j, :], y[:, j, :], bank[2 + j % 2][:, 0:D], ALU.add).then_inc(y_ready, 1)
                        dve.drain()
                        dve.tensor_tensor_reduce(sq[:, :], y[:, j, :], y[:, j, :], 1.0 / D, 0.0, ALU.mult, ALU.add, ms[:, j:j + 1])
                    dve.drain()
                    dve.tensor_scalar(ms[:, :], ms[:, :], 1e-6, None, ALU.add).then_inc(ms_ready, 1)
                    dve.wait_ge(root_ready, done(g))
                    dve.reciprocal(rms[:, :], root[:, :])
                    dve.drain()
                    for j in range(GR):
                        op = dve.tensor_scalar(hn[:, j, :], y[:, j, :], rms[:, j:j + 1], None, ALU.mult)
                    op.then_inc(hn_ready, 1)
                    for j in range(GR):
                        b = g * GR + j
                        dve.tensor_tensor(chip.X[:, b, :], chip.X[:, b, :], y[:, j, :], ALU.add)
                    shift(1, w.v["ln2_w"], [(0, "time_mix_k2"), (2, "time_mix_r2")])
                    for f in range(0, FC, 2):
                        dve.wait_ge(filled[0], done(g * PER + 2 + f // 2))
                        dve.wait_ge(k2_ready, done(g * FC + f - 2))
                        dve.tensor_scalar(kr[:, 0, :], bank[0][:, :], 0.0, None, ALU.max).then_inc(relu_ready[0], 1)
                        dve.drain()
                        dve.sem_inc(emptied[0], 1)
                    for j in range(GR):
                        b = g * GR + j
                        dve.wait_ge(r2_exp, done(g * GR + j))
                        dve.tensor_scalar(r2[:, j % 2, :], r2[:, j % 2, :], 1.0, None, ALU.add)
                        dve.drain()
                        dve.reciprocal(r2[:, j % 2, :], r2[:, j % 2, :])
                        dve.drain()
                        dve.wait_ge(kv_filled, done(g * GR + j))
                        dve.tensor_tensor(kv[:, :], r2[:, j % 2, :], bank[6 + j % 2][:, 0:D], ALU.mult).then_inc(kv_added, 1)
                        dve.drain()
                        dve.tensor_tensor(chip.X[:, b, :], chip.X[:, b, :], kv[:, :], ALU.add).then_inc(r2_used, 1)

            @block.gpsimd
            def _(pool):
                pool.sem_inc(k2_ready, LEAD)
                with pool.Fori(0, NG) as g:
                    for f in range(FC):
                        pool.wait_ge(relu_ready[f % 2], done(g * (FC // 2) + f // 2))
                        pool.tensor_tensor(k2[:, f, :], kr[:, f % 2, :], kr[:, f % 2, :], ALU.mult).then_inc(k2_ready, 1)

            @block.scalar
            def _(act):
                for x in (emptied[1], exps_ready, root_ready, relu_ready[1], r2_exp):
                    act.sem_inc(x, LEAD)
                w.wait(act)
                ln_stats_scalar(chip, act, s, twice=True)
                act.activation(decay[:, :], w.v["time_decay"], ACT.Exp).then_inc(decay_step, 1)
                act.wait_ge(decay_back, 1)
                act.activation(decay[:, :], decay[:, :], ACT.Exp).then_inc(decay_step, 1)
                with act.Fori(0, NG) as g:
                    def half(n, weight):
                        act.wait_ge(filled[1], done(g * PER + n))
                        act.activation(hT[:, 1, :, 1:W1], bank[1][:, :].rearrange("p (j t) -> p j t", j=GR), ACT.Copy, scale=weight[:, 1:2]).then_inc(emptied[1], 1)

                    half(0, w.v["ln1_w"])
                    for m in range(KC):
                        act.wait_ge(kvr_filled, done(g * KC + m))
                        act.wait_ge(rw_ready, done(g * KC + m - 1))
                        act.activation(er[:, :], bank[6 + m][:, :], ACT.Exp, scale=-1.0)
                        act.wait_ge(clipped, done(g * KC + m))
                        act.activation(ek[:, m, :, 1:W1], kc_[:, :].rearrange("p (j t) -> p j t", j=GR), ACT.Exp)
                        act.activation(eku[:, :], ku[:, :], ACT.Exp)
                        act.drain()
                        act.sem_inc(exps_ready, 1)
                    act.wait_ge(ms_ready, done(g))
                    act.activation(root[:, :], ms[:, :], ACT.Sqrt).then_inc(root_ready, 1)
                    half(1, w.v["ln2_w"])
                    for f in range(1, FC, 2):
                        act.wait_ge(filled[1], done(g * PER + 2 + f // 2))
                        act.wait_ge(k2_ready, done(g * FC + f - 2))
                        act.activation(kr[:, 1, :], bank[1][:, :], ACT.Relu).then_inc(relu_ready[1], 1)
                        act.drain()
                        act.sem_inc(emptied[1], 1)
                    for j in range(GR):
                        act.wait_ge(r2_filled, done(g * GR + j))
                        act.wait_ge(r2_used, done(g * GR + j - 2))
                        act.activation(r2[:, j % 2, :], bank[4 + j % 2][:, 0:D], ACT.Exp, scale=-1.0).then_inc(r2_exp, 1)


def attention_entry(name):
    weights, plan = PLANS[name]
    return weights, lambda chip, w, prefetch, have_stats: attention_block(chip, plan, w, prefetch, have_stats)


def experts_entry(name, weights, block):
    return weights, lambda chip, w, prefetch, have_stats: block(chip, EXPERTS[name], w, prefetch, have_stats)


SUBLAYERS = [["rwkv"], ["l0x"], ["l0f"], ["l1a"], ["l1x"], ["l1f"], ["l2a"], ["l2x"], ["l2fa", "l2fm"], ["gau"], ["l3x"], ["l3f"]]
BLOCKS = {name: attention_entry(name) for name in PLANS}
BLOCKS["l1f"] = experts_entry("l1f", l1_ffn_weights, small_experts_block)
BLOCKS["l2fm"] = experts_entry("l2fm", l2_ffn_moe_weights, streamed_experts_block)
BLOCKS["l3f"] = experts_entry("l3f", l3_ffn_weights, streamed_experts_block)
BLOCKS["l0f"] = (l0_ffn_weights, ternary_ffn_block)
BLOCKS["l1x"] = (l1_xattn_weights, deform_block)
BLOCKS["gau"] = (gau_weights, gau_block)
BLOCKS["rwkv"] = (rwkv_weights, rwkv_block)


LEAVES_STATS = set(PLANS)


def decoder_program(nc, ins, out):
    with ExitStack() as ctx:
        chip = Chip(nc, ins, out, ctx)
        todo = [b for m in STAGES for b in SUBLAYERS[m]]
        weights = [BLOCKS[b][0](chip, n % 2) for n, b in enumerate(todo)]
        setup_block(chip, weights[0])
        chip.end_block()
        for n, b in enumerate(todo):
            nxt = weights[n + 1] if n + 1 < len(todo) else None
            have_stats = n > 0 and todo[n - 1] in LEAVES_STATS
            if b == "l2fa":
                y_room = ExitStack()
                chip.Y = chip.sb("Y", [P, NB, D], ctx=y_room)
            BLOCKS[b][1](chip, weights[n], nxt, have_stats)
            chip.end_block()
            if b == "l2fm":
                y_room.close()
        store_block(chip)


def kernel(**inputs):
    import numpy as _np
    import concourse.bacc as _bacc
    from concourse import mybir as _mybir
    from concourse.bass_utils import run_bass_kernel_spmd as _run

    nc = _bacc.Bacc("TRN2", target_bir_lowering=False, num_devices=1)
    arrays, args = {}, {}
    for name in inputs:
        a = _np.ascontiguousarray(inputs[name])
        if a.ndim == 0:
            a = a.reshape(1)
        arrays[f"in_{name}"] = a
        args[name] = nc.dram_tensor(f"in_{name}", a.shape, _mybir.dt.from_np(a.dtype), kind="ExternalInput").ap()
    out = nc.dram_tensor("out_0", (NB, P, D), F32, kind="ExternalOutput").ap()
    decoder_program(nc, args, out)
    r = _run(nc, [arrays], core_ids=[0])
    return r.results[0]["out_0"]
```

```python
import concourse.bass as bass
from concourse import mybir
from contextlib import ExitStack

F32 = mybir.dt.float32
U8 = mybir.dt.uint8
I32 = mybir.dt.int32
ALU = mybir.AluOpType
ACT = mybir.ActivationFunctionType
AX = mybir.AxisListType

P = 128
NB = 16
D = 256
KC = D // P
GR = 4
NG = NB // GR
TG = GR * P
ARENA = 8192
VECS = 2560
LEAD = 3
NE = 8
MAX_TILES = 2 * NB + NE - 1
IOTA = 64
FMAX = 3.0e38
LN_EPS = 1e-5

STAGES = range(0, 12)


def done(n):
    return n + (1 + LEAD)


class Chip:

    def __init__(self, nc, ins, out, ctx):
        self.nc, self.ins, self.out, self.ctx = nc, ins, out, ctx
        self.block_sems = []
        self.X = self.sb("X", [P, NB, D])
        self.ident = self.sb("ident", [P, P])
        self.upper = self.sb("upper", [P, P])
        self.causal = self.sb("causal", [P, P])
        self.ones = self.sb("ones", [P, TG])
        self.block_of = {hd: self.sb(f"block_of_{hd}", [P, P // hd]) for hd in (16, 64)}
        self.room = self.sb("room", [P, 4 * ARENA])
        self.arena = [self.room[:, 0:ARENA], self.room[:, ARENA:2 * ARENA]]
        self.Y = self.sb("Y", [P, NB, D])
        self.zeros = self.sb("zeros", [P, D])
        self.iota = self.sb("iota", [P, IOTA])
        self.iota_i = self.sb("iota_i", [P, IOTA], I32)
        self.sorted_rows = nc.dram_tensor("sorted_rows", (MAX_TILES * P, D), F32, kind="Internal").ap()
        self.sorted_out = nc.dram_tensor("sorted_out", (MAX_TILES * P, D), F32, kind="Internal").ap()
        self.rows_zeroed = self.lasting_sem("rows_zeroed")
        self.vecs = [self.sb("vecs0", [P, VECS]), self.sb("vecs1", [P, VECS])]
        self.bn = self.sb("bn", [P, NB, 6])
        self.mv = self.sb("mv", [P, NB, 2])
        self.var = self.sb("var", [P, NB])
        self.std = self.sb("std", [P, NB])
        self.rstd = self.sb("rstd", [P, NB])
        self.rstd2 = self.sb("rstd2", [P, NB])

    def sb(self, name, shape, dt=F32, ctx=None):
        return (ctx or self.ctx).enter_context(self.nc.sbuf_tensor(name, shape, dt))

    def block_sb(self, name, shape, dt, ctx):
        n = 1
        for d in shape[1:]:
            n *= d
        for part in self.spare:
            whole, at = part
            if dt == F32 and at + n <= whole.shape[1]:
                part[1] = at + n
                dims = "abcd"[:len(shape) - 1]
                return whole[0:shape[0], at:at + n].rearrange(f"p ({' '.join(dims)}) -> p {' '.join(dims)}", **dict(zip(dims, shape[1:])))
        return self.sb(name, shape, dt, ctx)

    def begin_block(self, w, y_in_use):
        self.spare = [[self.arena[w.side], w.at[True]], [self.room[:, 2 * ARENA:4 * ARENA], 0]]
        if not y_in_use:
            self.spare.append([self.Y[:, :, :].rearrange("p b d -> p (b d)"), 0])

    def ps(self, name, ctx, cols=512):
        return ctx.enter_context(self.nc.psum_tensor(name, [P, cols], F32))

    def sem(self, name):
        self.block_sems.append(self.nc.alloc_semaphore(name=name))
        return self.block_sems[-1]

    def lasting_sem(self, name):
        return self.ctx.enter_context(self.nc.semaphore(name))

    def end_block(self):
        self.nc.clear_and_free_semaphores(self.block_sems)
        self.block_sems = []
        self.nc.all_engine_barrier()


class Weights:

    def __init__(self, chip, tag, side):
        self.chip, self.side = chip, side
        self.loaded = chip.lasting_sem(f"{tag}_weights_loaded")
        self.at = {True: 0, False: 0}
        self.dmas = []
        self.streams = []

    def room(self, n, big=True):
        a = self.chip.arena[self.side] if big else self.chip.vecs[self.side]
        o = self.at[big]
        self.at[big] = o + n
        assert self.at[big] <= (ARENA if big else VECS), (big, self.at)
        return a[:, o:o + n]

    def matrix(self, src, big=True):
        k, n = src.shape
        v = self.room(k // P * n, big).rearrange("p (c n) -> p c n", c=k // P)
        self.dmas.append((v, src.rearrange("(c p) n -> p c n", p=P)))
        return v

    def repeated(self, src, copies):
        k, n = src.shape
        h = n // 16
        v = self.room(k // P * n * copies).rearrange("p (c n) -> p c n", c=k // P)
        w = v.rearrange("p c (h r d) -> p c h r d", r=copies, d=16)
        s = src.rearrange("(c p) (h d) -> p c h d", p=P, d=16)
        for c in range(k // P):
            for r in range(copies):
                self.dmas.append((w[:, c, :, r, :], s[:, c]))
        return v

    def columns(self, src):
        n = src.shape[0] // P
        v = self.room(n, False)
        self.dmas.append((v, src.rearrange("(c p) -> p c", p=P)))
        return v

    def row(self, src):
        n = src.shape[0]
        v = self.room(n, False)[0:1, :]
        self.dmas.append((v, src.rearrange("(a n) -> a n", a=1)))
        return v

    def everywhere(self, src):
        n = src.shape[0]
        v = self.room(n, False)
        self.dmas.append((v, src.partition_broadcast(P)))
        return v

    def load(self, sp):
        for dst, src in self.dmas:
            sp.dma_start(dst, src, allow_slow_non_contiguous=True).then_inc(self.loaded, 16)
        for dst, src, signal in self.streams:
            sp.dma_start(dst, src).then_inc(signal, 16)

    def wait(self, eng):
        eng.wait_ge(self.loaded, 16 * len(self.dmas))


def ln_stats_vector(chip, dve, src, s, twice=False, eps=LN_EPS, second_eps=LN_EPS, have=False):
    if not have:
        with dve.Fori(0, NB) as b:
            dve.bn_stats(chip.bn[:, b, :], src[:, b, :])
        dve.drain()
    for b in range(NB):
        dve.bn_aggr(chip.mv[:, b, :], chip.bn[:, b, :])
    dve.drain()
    dve.tensor_scalar(chip.var[:, :], chip.mv[:, :, 1], eps, None, ALU.add).then_inc(s["var_ready"], 1)
    dve.wait_ge(s["std_ready"], 1)
    dve.reciprocal(chip.rstd[:, :], chip.std[:, :])
    dve.drain()
    if twice:
        dve.tensor_tensor(chip.rstd2[:, :], chip.rstd[:, :], chip.rstd[:, :], ALU.mult)
        dve.drain()
        dve.tensor_tensor(chip.rstd2[:, :], chip.rstd2[:, :], chip.mv[:, :, 1], ALU.mult)
        dve.drain()
        dve.tensor_scalar(chip.var[:, :], chip.rstd2[:, :], second_eps, None, ALU.add).then_inc(s["var_ready"], 1)
        dve.wait_ge(s["std_ready"], 2)
        dve.reciprocal(chip.rstd2[:, :], chip.std[:, :])
        dve.drain()
        dve.tensor_tensor(chip.rstd2[:, :], chip.rstd2[:, :], chip.rstd[:, :], ALU.mult)
        dve.drain()


def ln_stats_scalar(chip, act, s, twice=False):
    for n in range(2 if twice else 1):
        act.wait_ge(s["var_ready"], n + 1)
        act.activation(chip.std[:, :], chip.var[:, :], ACT.Sqrt).then_inc(s["std_ready"], 1)


def setup_block(chip, first):
    nc = chip.nc
    const_step = chip.sem("const_step")
    zeros_ready = chip.sem("zeros_ready")
    iota_ready = chip.sem("iota_ready")
    x_loaded = chip.sem("x_loaded")
    with nc.Block() as block:
        @block.gpsimd
        def _(pool):
            pool.memset(chip.ident[:, :], 0.0).then_inc(const_step, 1)
            pool.memset(chip.upper[:, :], 1.0).then_inc(const_step, 1)
            pool.memset(chip.causal[:, :], 0.0).then_inc(const_step, 1)
            pool.memset(chip.ones[:, :], 1.0).then_inc(const_step, 1)
            for m in chip.block_of.values():
                pool.memset(m[:, :], 1.0).then_inc(const_step, 1)
            pool.iota(chip.iota_i[:, :], pattern=[[1, IOTA]], base=0, channel_multiplier=0).then_inc(iota_ready, 1)
            pool.wait_ge(const_step, 6)
            pool.affine_select(out=chip.ident[:, :], in_=chip.ident[:, :], compare_op=ALU.not_equal, fill=1.0,
                               base=0, pattern=[[-1, P]], channel_multiplier=1).then_inc(const_step, 1)
            pool.affine_select(out=chip.upper[:, :], in_=chip.upper[:, :], compare_op=ALU.is_ge, fill=0.0,
                               base=0, pattern=[[1, P]], channel_multiplier=-1).then_inc(const_step, 1)
            pool.affine_select(out=chip.causal[:, :], in_=chip.causal[:, :], compare_op=ALU.is_ge, fill=-1e30,
                               base=0, pattern=[[-1, P]], channel_multiplier=1).then_inc(const_step, 1)
            for hd, m in chip.block_of.items():
                pool.affine_select(out=m[:, :], in_=m[:, :], compare_op=ALU.is_ge, fill=0.0,
                                   base=0, pattern=[[-hd, P // hd]], channel_multiplier=1).then_inc(const_step, 1)
            pool.wait_ge(const_step, 11)
            for hd, m in chip.block_of.items():
                pool.affine_select(out=m[:, :], in_=m[:, :], compare_op=ALU.is_ge, fill=0.0,
                                   base=hd - 1, pattern=[[hd, P // hd]], channel_multiplier=-1).then_inc(const_step, 1)
            pool.wait_ge(const_step, 13)
            m = chip.block_of[16]
            pool.tensor_tensor(m[:, 0:4], m[:, 0:4], m[:, 4:8], ALU.add)

        @block.vector
        def _(dve):
            dve.memset(chip.zeros[:, :], 0.0).then_inc(zeros_ready, 1)
            dve.wait_ge(iota_ready, 1)
            dve.tensor_copy(chip.iota[:, :], chip.iota_i[:, :])

        @block.sync
        def _(sp):
            sp.dma_start(chip.X[:, :, :], chip.ins["x"].rearrange("b s d -> s b d")).then_inc(x_loaded, 16)
            first.load(sp)
            sp.wait_ge(zeros_ready, 1)
            sp.dma_start(chip.sorted_rows.rearrange("(t p) d -> p t d", p=P),
                         chip.zeros[:, :].unsqueeze(1).to_broadcast([P, MAX_TILES, D])).then_inc(chip.rows_zeroed, 16)
            sp.wait_ge(x_loaded, 16)


def store_block(chip):
    nc = chip.nc
    stored = chip.sem("x_stored")
    with nc.Block() as block:
        @block.sync
        def _(sp):
            sp.dma_start(chip.out.rearrange("b s d -> s b d"), chip.X[:, :, :]).then_inc(stored, 16)
            sp.wait_ge(chip.rows_zeroed, 16)
            sp.wait_ge(stored, 16)


UNIT = 4


class AttentionPlan:

    def __init__(self, tag, heads, hd, scale, mask, source="self", kv_heads=None, causal_gap=None,
                 double_ln=False, residual="X"):
        self.tag, self.heads, self.hd, self.scale, self.mask, self.source = tag, heads, hd, scale, mask, source
        self.kv_heads = kv_heads or heads
        self.double_ln, self.residual = double_ln, residual
        self.causal_gap = causal_gap
        self.per_chunk = P // hd
        self.chunks = heads // self.per_chunk
        self.blocks = min(UNIT, self.per_chunk)
        self.parts = self.per_chunk // self.blocks
        self.vw = self.kv_heads * hd
        self.ow = heads * hd


def attention_block(chip, plan, w, prefetch, have_stats):
    nc, ins = chip.nc, chip.ins
    t, H, hd = plan.tag, plan.heads, plan.hd
    ctxsrc = plan.source == "ctx"
    pads = plan.mask == "support"
    UH = UNIT
    U = H // UH
    NU = GR * U
    SW = P + 1 if pads else P
    OW, VW, C = plan.ow, plan.vw, plan.chunks
    vrows = max(1, 512 // VW) if VW >= 256 else 2
    vcols = min(VW, 512)
    vtasks = [(j, c) for j in range(0, GR, vrows) for c in range(0, VW, vcols)]
    ocs = OW // P
    otasks = [(c, min(c + 4, ocs)) for c in range(0, ocs, 4)]
    masks = {"timebias": [("ct", 0), ("km", 0)], "support": [("valid", 0), ("count", 0)]}.get(plan.mask, [])
    turns = [("c", 0), ("c", 1), ("y", 0), ("y", 1)] if ctxsrc else [("y", 0), ("y", 1)]
    ks, qs = [[(x, c) for c in range(C)] for x in "kq"]
    early, late = turns + ks + qs, masks + [("v", n) for n in range(len(vtasks))]
    where, per_group, load = {}, [0, 0], [len(vtasks) if "bv" in w.v else 0, 0]
    bank_no, before = {}, {}
    last_user = [{}, {}]
    for f in early + late:
        kind, i = f
        if f in turns:
            b = i
        elif f in masks:
            b = {"ct": 0, "km": 1, "valid": 0, "count": 1}[kind]
        else:
            b = 0 if kind == "v" and "bv" in w.v else int(load[1] < load[0])
            load[b] += plan.blocks if kind == "k" else plan.parts if kind == "q" else 0 if kind == "v" and "bv" in w.v else 1
        where[f] = (b, per_group[b])
        bank_no[f] = min((0, 1) if f in early else (0, 1, 2), key=lambda k: last_user[b].get(k, -1))
        before[f] = last_user[b].get(bank_no[f])
        last_user[b][bank_no[f]] = per_group[b]
        per_group[b] += 1
    n_feat = len(otasks)

    def task(g, f):
        b, n = where[f]
        return g * per_group[b] + n

    obufs = 2 if OW <= 512 else 1

    with ExitStack() as scope:
        sb = lambda n, s, d=F32: chip.block_sb(f"{t}_{n}", s, d, scope)
        sem = lambda n: chip.sem(f"{t}_{n}")
        yn = sb("yn", [P, GR, D])
        yT = sb("yT", [P, KC, TG])
        if ctxsrc:
            cn = sb("cn", [P, GR, D])
            cT = sb("cT", [P, KC, TG])
        else:
            cT = yT
        qT = sb("qT", [P, C, plan.parts, TG])
        part_of = chip.block_of[plan.blocks * hd] if plan.parts > 1 else None
        kB = sb("kB", [P, C, GR, plan.blocks, P])
        if "bk" in w.v:
            bkB = sb("bkB", [P, C, plan.blocks])
        if "bq" in w.v and plan.parts > 1:
            bqB = sb("bqB", [P, C, plan.parts])
        v = sb("v", [P, GR, VW])
        sm = sb("sm", [P, 2, UH, SW])
        nmx = sb("nmx", [P, 2, UH])
        p = sb("p", [P, 3, UH, SW])
        pT = sb("pT", [P, 3, UH, P])
        rsum = sb("rsum", [P, GR, H])
        rinv = sb("rinv", [P, H])
        on = sb("on", [P, OW])
        oT = sb("oT", [P, ocs, P])
        maskadd = sb("maskadd", [P, GR, P])
        if plan.mask == "keymask":
            raw = sb("raw", [P, GR, P], U8)
        if pads:
            raw = sb("raw", [P, GR, P], I32)
            valid = sb("valid", [P, GR, P])
            count = sb("count", [P, GR, P])
            npad = sb("npad", [P, GR])
            npad1 = sb("npad1", [P, GR])
            lnpad = sb("lnpad", [P, GR])
            padcol = sb("padcol", [P, GR])
        if plan.mask == "timebias":
            deltas = sb("deltas", [P, NB])
            ctcol = sb("ctcol", [P, NB])
            dwide = sb("dwide", [P, GR, P])
            gap = sb("gap", [P, GR, P])
            bias = sb("bias", [P, GR, P])
            keyrow = sb("keyrow", [1, NB * P])
            keyadd = sb("keyadd", [P, GR, P])
        proj = [chip.ps(f"{t}_proj0", scope), chip.ps(f"{t}_proj1", scope)]
        psS = [chip.ps(f"{t}_scores0", scope), chip.ps(f"{t}_scores1", scope)]
        psT = [chip.ps(f"{t}_probsT0", scope), chip.ps(f"{t}_probsT1", scope)]
        psO = chip.ps(f"{t}_out", scope, 1024)
        bank_of = lambda f: (psS, psT, proj)[bank_no[f]][where[f][0]]

        s = {n: sem(n) for n in ("var_ready", "std_ready")}
        stats_ready = sem("stats_ready")
        yn_ready = sem("yn_ready")
        filled = [sem("proj0_filled"), sem("proj1_filled")]
        emptied = [sem("proj0_emptied"), sem("proj1_emptied")]
        feat_filled = sem("feat_filled")
        feat_emptied = sem("feat_emptied")
        out_filled = sem("out_filled")
        out_emptied = sem("out_emptied")
        scores_ready = sem("scores_ready")
        masked_ready = sem("masked_ready")
        probs_ready = sem("probs_ready")
        probsT_ready = sem("probsT_ready")
        probsT_copied = sem("probsT_copied")
        unit_begun = sem("unit_begun")
        bias_added = sem("bias_added")
        bkB_ready = sem("bkB_ready")
        sp_turn = sem("sp_turn")
        pv_done = sem("pv_done")
        out_normal = sem("out_normal")
        ctx_loaded = sem("ctx_loaded")
        mask_loaded = sem("mask_loaded")
        step_done = sem("mask_step")
        step_back = sem("mask_back")
        wide_ready = sem("wide_ready")

        with nc.Block() as block:
            @block.sync
            def _(sp):
                if ctxsrc:
                    sp.dma_start(cn[:, :, :], ins["ctx_1024"][0:GR].rearrange("b s d -> s b d")).then_inc(ctx_loaded, 16)
                if plan.mask == "keymask":
                    src = ins["mask_Bx1xSxS2_bk1"].rearrange("b a q k -> q (b a) k")
                if pads:
                    src = ins["mask_BxS2xS_ik0"].rearrange("b v t -> v b t")
                if plan.mask in ("keymask", "support"):
                    sp.dma_start(raw[:, :, :], src[:, 0:GR, :]).then_inc(mask_loaded, 16)
                if plan.mask == "timebias":
                    sp.dma_start(deltas[:, :], ins["fside_BxS2_0"].rearrange("b s -> s b"), allow_slow_non_contiguous=True).then_inc(mask_loaded, 16)
                    sp.dma_start(keyrow[:, :], ins["mask_BxS2_ff1"].rearrange("b s -> (b s)").rearrange("(a n) -> a n", a=1)).then_inc(mask_loaded, 16)
                if prefetch:
                    prefetch.load(sp)
                if ctxsrc:
                    with sp.Fori(0, NG - 1) as g:
                        for kc in range(KC):
                            sp.wait_ge(filled[kc], done(task(g, ("c", kc))))
                        sp.sem_inc(sp_turn, 1)
                        sp.dma_start(cn[:, :, :], ins["ctx_1024"][bass.ds(g * GR + GR, GR)].rearrange("b s d -> s b d")).then_inc(ctx_loaded, 16)
                        if plan.mask in ("keymask", "support"):
                            sp.wait_ge(wide_ready, done(g))
                            sp.sem_inc(sp_turn, 1)
                            sp.dma_start(raw[:, :, :], src[:, bass.ds(g * GR + GR, GR), :]).then_inc(mask_loaded, 16)

            @block.tensor
            def _(pe):
                for x in (filled[0], filled[1], feat_filled, out_filled, scores_ready, probsT_ready, pv_done):
                    pe.sem_inc(x, LEAD)
                w.wait(pe)
                if plan.mask == "timebias":
                    pe.wait_ge(mask_loaded, 32)
                    pe.matmul(psO[:, 0:NB], chip.upper[:, :], deltas[:, :], start=True, stop=True).then_inc(step_back, 1)

                def project(g, f):
                    b, n = where[f]
                    kind, i = f
                    bank = bank_of(f)
                    needs = {}
                    if before[f] is not None:
                        needs[b] = before[f]
                    if i == 0:
                        for k in {"k": "c" if ctxsrc else "y", "q": "y"}.get(kind, ""):
                            for kc in range(KC):
                                needs[kc] = max(needs.get(kc, 0), where[(k, kc)][1])
                    for o, n in needs.items():
                        pe.wait_ge(emptied[o], done(g * per_group[o] + n))
                    if bank_no[f] == 2 and b == 0:
                        pe.wait_ge(out_emptied, done(g * GR - 1))
                    if bank_no[f] == 2 and b == 1:
                        pe.wait_ge(feat_emptied, done(g * GR * n_feat - 1))
                    if kind == "y" and i == 0:
                        pe.wait_ge(yn_ready, done(g))
                    if kind == "c" and i == 0:
                        pe.wait_ge(ctx_loaded, g * 16 + 16)
                    if kind in ("ct", "valid"):
                        pe.wait_ge(wide_ready, done(g))
                    if kind in "yc":
                        x = yn if kind == "y" else cn
                        for j in range(GR):
                            mm = pe.transpose(bank[:, j * P:(j + 1) * P], x[:, j, i * P:(i + 1) * P], chip.ident[:, :])
                    elif kind in "qk":
                        for kc in range(KC):
                            mm = pe.matmul(bank[:, :], w.v[kind][:, kc, i * P:(i + 1) * P],
                                           (yT if kind == "q" else cT)[:, kc, :], start=(kc == 0), stop=(kc == KC - 1))
                    elif kind == "v":
                        j0, c0 = vtasks[i]
                        for j in range(j0, j0 + vrows):
                            o = bank[:, (j - j0) * vcols:(j - j0 + 1) * vcols]
                            for kc in range(KC):
                                mm = pe.matmul(o, cT[:, kc, j * P:(j + 1) * P], w.v["v"][:, kc, c0:c0 + vcols], start=(kc == 0), stop=(kc == KC - 1))
                    elif kind == "ct":
                        for j in range(GR):
                            mm = pe.matmul(bank[:, j * P:(j + 1) * P], dwide[:, j, :], chip.upper[:, :], start=True, stop=True)
                    elif kind == "km":
                        mm = pe.matmul(bank[:, :], chip.ones[0:1, 0:P], keyrow[0:1, bass.ds(g * TG, TG)], start=True, stop=True)
                    elif kind == "valid":
                        for j in range(GR):
                            mm = pe.matmul(bank[:, j * P:(j + 1) * P], valid[:, j, :], chip.ident[:, :], start=True, stop=True)
                    elif kind == "count":
                        for j in range(GR):
                            mm = pe.matmul(bank[:, j * P:(j + 1) * P], valid[:, j, :], chip.upper[:, :], start=True, stop=True)
                    mm.then_inc(filled[b], 1)

                for f in early:
                    project(0, f)

                def group(g, more):
                    for f in late:
                        project(g, f)
                    for b in range(2):
                        pe.wait_ge(emptied[b], done(g * per_group[b] + per_group[b] - 1))

                    for st in range(NU + 7):
                        if st < NU:
                            u = st
                            j = u // U
                            pe.wait_ge(masked_ready, done(g * NU + u - 2))
                            width = plan.blocks
                            for i in range(0, UH, width):
                                c, o = divmod(u % U * UH + i, plan.per_chunk)
                                mm = pe.matmul(psS[u % 2][:, i * P:(i + width) * P], qT[:, c, o // width, j * P:(j + 1) * P],
                                               kB[:, c, j, :, :], start=True, stop=True)
                            mm.then_inc(scores_ready, 1)
                        if 0 <= st - 2 < NU:
                            u = st - 2
                            pe.wait_ge(probs_ready, done(g * NU + u))
                            pe.wait_ge(probsT_copied, done(g * NU + u - 2))
                            for i in range(UH):
                                mm = pe.transpose(psT[u % 2][:, i * P:(i + 1) * P], p[:, u % 3, i, 0:P], chip.ident[:, :])
                            mm.then_inc(probsT_ready, 1)
                        if 0 <= st - 4 < NU:
                            u = st - 4
                            j = u // U
                            ob = j % obufs * 512
                            if u % U == 0:
                                pe.wait_ge(out_normal, done(g * GR + j - obufs))
                            pe.wait_ge(probsT_copied, done(g * NU + u))
                            for i in range(UH):
                                h = u % U * UH + i
                                hv = h * plan.kv_heads // H
                                mm = pe.matmul(psO[:, ob + h * hd:ob + (h + 1) * hd], pT[:, u % 3, i, :],
                                               v[:, j, hv * hd:(hv + 1) * hd], start=True, stop=True)
                            if u % U == U - 1:
                                mm.then_inc(pv_done, 1)
                        if 0 <= st - 5 < NU and (st - 5) % U == U - 1:
                            j = (st - 5) // U
                            pe.wait_ge(out_normal, done(g * GR + j))
                            for n, (c0, c1) in enumerate(otasks):
                                pe.wait_ge(feat_emptied, done((g * GR + j) * n_feat + n - 1))
                                for c in range(c0, c1):
                                    mm = pe.transpose(proj[1][:, (c - c0) * P:(c - c0 + 1) * P], on[:, c * P:(c + 1) * P], chip.ident[:, :])
                                mm.then_inc(feat_filled, 1)
                        if 0 <= st - 6 < NU and (st - 6) % U == U - 1:
                            j = (st - 6) // U
                            pe.wait_ge(out_emptied, done(g * GR + j - 1))
                            pe.wait_ge(feat_emptied, done((g * GR + j) * n_feat + n_feat - 1))
                            for c in range(ocs):
                                mm = pe.matmul(proj[0][:, 0:D], oT[:, c, :], w.v["o"][:, c, :], start=(c == 0), stop=(c == ocs - 1))
                            mm.then_inc(out_filled, 1)
                        if more and st in (NU + 3, NU + 4, NU + 6):
                            for f in {NU + 3: turns, NU + 4: ks, NU + 6: qs}[st]:
                                project(g + 1, f)

                with pe.Fori(0, NG - 1) as g:
                    group(g, True)
                group(NG - 1, False)

            def empty_bank(eng, b, g, f):
                kind, i = f
                eng.wait_ge(filled[b], done(task(g, f)))
                bank = bank_of(f)
                add = mul = None
                if kind == "y":
                    dst, src = yT[:, i, :], bank[:, :]
                    if "g" in w.v:
                        mul, add = w.v["g"][:, i:i + 1], w.v["b"][:, i:i + 1]
                elif kind == "c":
                    dst, src = cT[:, i, :], bank[:, :]
                elif kind == "q" and plan.parts > 1:
                    for o in range(plan.parts):
                        dst, own = qT[:, i, o, :], part_of[:, o:o + 1]
                        if b == 0:
                            op = eng.tensor_scalar(dst, bank[:, :], w.v["bq"][:, i:i + 1] if "bq" in w.v else 0.0, own, ALU.add, ALU.mult)
                        elif "bq" in w.v:
                            op = eng.activation(dst, bank[:, :], ACT.Identity, bias=bqB[:, i, o:o + 1], scale=own)
                        else:
                            op = eng.activation(dst, bank[:, :], ACT.Copy, scale=own)
                    return op
                elif kind == "q":
                    dst, src = qT[:, i, 0, :], bank[:, :]
                    if "bq" in w.v:
                        add = w.v["bq"][:, i:i + 1]
                elif kind == "k":
                    src = bank[:, :].rearrange("p (j t) -> p j t", j=GR)
                    for o in range(plan.blocks):
                        dst, own = kB[:, i, :, o, :], chip.block_of[hd][:, o:o + 1]
                        if b == 0:
                            op = eng.tensor_scalar(dst, src, w.v["bk"][:, i:i + 1] if "bk" in w.v else 0.0, own, ALU.add, ALU.mult)
                        elif "bk" in w.v:
                            op = eng.activation(dst, src, ACT.Identity, bias=bkB[:, i, o:o + 1], scale=own)
                        else:
                            op = eng.activation(dst, src, ACT.Copy, scale=own)
                    return op
                elif kind == "v":
                    j0, c0 = vtasks[i]
                    dst = v[:, j0:j0 + vrows, c0:c0 + vcols]
                    src = bank[:, 0:vrows * vcols].rearrange("p (j c) -> p j c", j=vrows)
                    if "bv" in w.v:
                        return eng.tensor_tensor(dst, src, w.v["bv"][:, c0:c0 + vcols].unsqueeze(1).to_broadcast([P, vrows, vcols]), ALU.add)
                elif kind == "km":
                    dst, src = keyadd[:, :, :], bank[:, :].rearrange("p (j k) -> p j k", j=GR)
                    return eng.tensor_scalar(dst, src, 1e9 / plan.scale, -1e9 / plan.scale, ALU.mult, ALU.add) if b == 0 else \
                        eng.activation(dst, src, ACT.Copy, bias=-1e9 / plan.scale, scale=1e9 / plan.scale)
                elif kind == "count":
                    dst, src = count[:, :, :], bank[:, :].rearrange("p (j k) -> p j k", j=GR)
                if b == 0:
                    if mul is not None:
                        return eng.tensor_scalar(dst, src, mul, add, ALU.mult, ALU.add)
                    if add is not None:
                        return eng.tensor_scalar(dst, src, add, None, ALU.add)
                    return eng.tensor_copy(dst, src)
                if mul is not None:
                    return eng.activation(dst, src, ACT.Identity, bias=add, scale=mul)
                if add is not None:
                    return eng.activation(dst, src, ACT.Identity, bias=add)
                return eng.copy(dst, src)

            @block.vector
            def _(dve):
                for x in (emptied[0], out_emptied, masked_ready, probsT_copied, out_normal, wide_ready):
                    dve.sem_inc(x, LEAD)
                w.wait(dve)
                if "bk" in w.v:
                    for c in range(C):
                        if "bq" in w.v and plan.parts > 1:
                            dve.tensor_scalar(bqB[:, c, :], part_of[:, 0:plan.parts], w.v["bq"][:, c:c + 1], None, ALU.mult)
                        op = dve.tensor_scalar(bkB[:, c, :], chip.block_of[hd][:, 0:plan.blocks], w.v["bk"][:, c:c + 1], None, ALU.mult)
                    op.then_inc(bkB_ready, 1)
                ln_stats_vector(chip, dve, chip.X, s, plan.double_ln, have=have_stats)
                dve.sem_inc(stats_ready, 1)
                if plan.mask == "timebias":
                    dve.wait_ge(step_back, 1)
                    dve.tensor_copy(ctcol[:, :], psO[:, 0:NB])
                    dve.drain()
                if plan.mask == "none":
                    dve.memset(maskadd[:, 0, :], 0.0)
                    dve.drain()
                resid = chip.X if plan.residual == "X" else chip.Y
                def empty_mine(g, tasks):
                    for f in tasks:
                        if where[f][0] == 0:
                            empty_bank(dve, 0, g, f).then_inc(emptied[0], 1)

                empty_mine(0, early)

                def group(g, more):
                    if plan.mask == "keymask":
                        dve.wait_ge(mask_loaded, g * 16 + 16)
                        dve.tensor_scalar(maskadd[:, :, :], raw[:, :, :], -1e15 / plan.scale, None, ALU.mult).then_inc(wide_ready, 1)
                    if pads:
                        dve.wait_ge(mask_loaded, g * 16 + 16)
                        dve.tensor_scalar(valid[:, :, :], raw[:, :, :], 0.0, None, ALU.not_equal).then_inc(wide_ready, 1)
                    if plan.mask == "timebias":
                        dve.tensor_copy(dwide[:, :, :], deltas[:, bass.ds(g * GR, GR)].unsqueeze(2).to_broadcast([P, GR, P])).then_inc(wide_ready, 1)
                    for f in late:
                        if where[f][0]:
                            continue
                        if f[0] == "ct":
                            dve.wait_ge(filled[0], done(task(g, f)))
                            for j in range(GR):
                                op = dve.tensor_scalar(gap[:, j, :], bank_of(f)[:, j * P:(j + 1) * P], ctcol[:, bass.ds(g * GR + j, 1)], None, ALU.subtract)
                            op.then_inc(emptied[0], 1)
                            dve.drain()
                            dve.sem_inc(step_done, 1)
                        elif f[0] == "valid":
                            dve.wait_ge(filled[0], done(task(g, f)))
                            dve.wait_ge(emptied[1], done(task(g, ("count", 0))))
                            dve.scalar_tensor_tensor(out=maskadd[:, :, :], in0=count[:, :, :], scalar=plan.causal_gap + 0.5,
                                                     in1=bank_of(f)[:, :].rearrange("p (j k) -> p j k", j=GR),
                                                     op0=ALU.is_lt, op1=ALU.mult).then_inc(emptied[0], 1)
                            dve.tensor_scalar(npad[:, :], count[:, :, P - 1], -1.0, plan.causal_gap, ALU.mult, ALU.add)
                            dve.drain()
                            dve.tensor_scalar(maskadd[:, :, :], maskadd[:, :, :], -1.0, 1e30, ALU.add, ALU.mult)
                            dve.tensor_scalar(npad1[:, :], npad[:, :], 1.0, None, ALU.max)
                            dve.drain()
                            dve.sem_inc(step_done, 1)
                            dve.tensor_scalar(npad[:, :], npad[:, :], 0.5, 1e30, ALU.is_lt, ALU.mult)
                            dve.drain()
                            dve.wait_ge(step_back, g + 1)
                            dve.tensor_tensor(padcol[:, :], npad[:, :], lnpad[:, :], ALU.subtract)
                            dve.drain()
                            dve.tensor_scalar(padcol[:, :], padcol[:, :], 1e4, None, ALU.add)
                            dve.drain()
                        else:
                            empty_bank(dve, 0, g, f).then_inc(emptied[0], 1)
                    if plan.mask == "timebias":
                        dve.wait_ge(step_back, g + 2)
                        dve.wait_ge(emptied[1], done(task(g, ("km", 0))))
                        dve.tensor_scalar(bias[:, :, :], bias[:, :, :], w.v["tb"], 1.0 / plan.scale, ALU.mult, ALU.mult)
                        dve.drain()
                        dve.tensor_tensor(maskadd[:, :, :], bias[:, :, :], keyadd[:, :, :], ALU.add)
                        dve.drain()

                    for st in range(NU + 8):
                        if st < NU:
                            u = st
                            j = u // U
                            dve.wait_ge(scores_ready, done(g * NU + u))
                            dve.wait_ge(probs_ready, done(g * NU + u - 2))
                            if pads:
                                dve.tensor_copy(sm[:, u % 2, :, P], padcol[:, j:j + 1].to_broadcast([P, UH]))
                            dve.sem_inc(unit_begun, 1)
                            for i in range(UH):
                                m = {"causal": chip.causal[:, :], "none": maskadd[:, 0, :]}.get(plan.mask, maskadd[:, j, :])
                                op = dve.tensor_tensor_reduce(sm[:, u % 2, i, 0:P], psS[u % 2][:, i * P:(i + 1) * P], m, -plan.scale,
                                                              padcol[:, j:j + 1] if pads else FMAX,
                                                              ALU.add, ALU.min, nmx[:, u % 2, i:i + 1])
                            op.then_inc(masked_ready, 1)
                        if 0 <= st - 2 < NU:
                            u = st - 2
                            dve.wait_ge(probsT_ready, done(g * NU + u))
                            dve.tensor_copy(pT[:, u % 3, :, :], psT[u % 2][:, :].rearrange("p (i q) -> p i q", i=UH)).then_inc(probsT_copied, 1)
                        if 0 <= st - 7 < NU and (st - 7) % U == U - 1:
                            b = g * GR + (st - 7) // U
                            dve.wait_ge(out_filled, done(b))
                            if "bo" in w.v and (st - 7) // U == 0:
                                dve.wait_ge(bias_added, done(g))
                            dve.tensor_tensor(resid[:, b, :], resid[:, b, :], proj[0][:, 0:D], ALU.add).then_inc(out_emptied, 1)
                            dve.drain()
                            dve.bn_stats(chip.bn[:, b, :], resid[:, b, :])
                        if more and st in (NU + 4, NU + 5, NU + 7):
                            empty_mine(g + 1, {NU + 4: turns, NU + 5: ks, NU + 7: qs}[st])
                        if 0 <= st - 4 < NU and (st - 4) % U == U - 1:
                            j = (st - 4) // U
                            dve.wait_ge(pv_done, done(g * GR + j))
                            dve.reciprocal(rinv[:, :], rsum[:, j, :])
                            dve.drain()
                            dve.wait_ge(feat_filled, done((g * GR + j) * n_feat - 1))
                            o = psO[:, j % obufs * 512:j % obufs * 512 + OW].rearrange("p (h d) -> p h d", h=H)
                            dve.tensor_tensor(on[:, :].rearrange("p (h d) -> p h d", h=H), o,
                                              rinv[:, :].unsqueeze(2).to_broadcast([P, H, hd]), ALU.mult).then_inc(out_normal, 1)

                with dve.Fori(0, NG - 1) as g:
                    group(g, True)
                group(NG - 1, False)

            @block.gpsimd
            def _(pool):
                for x in (yn_ready, bias_added):
                    pool.sem_inc(x, LEAD)
                w.wait(pool)
                rows = chip.X if plan.residual == "X" else chip.Y
                scale = chip.rstd2 if plan.double_ln else chip.rstd
                pool.wait_ge(stats_ready, 1)

                def normalise(g, dst, scale):
                    those = bass.ds(g * GR, GR)
                    pool.tensor_tensor(dst, chip.X[:, those, :], chip.mv[:, those, 0:1].to_broadcast([P, GR, D]), ALU.subtract)
                    pool.drain()
                    return pool.tensor_tensor(dst, dst, scale[:, those].unsqueeze(2).to_broadcast([P, GR, D]), ALU.mult)

                def prepare_residual(g):
                    if plan.residual == "Y":
                        normalise(g, chip.Y[:, bass.ds(g * GR, GR), :], chip.rstd)
                        pool.drain()
                    if "bo" in w.v:
                        pool.tensor_tensor(rows[:, bass.ds(g * GR, GR), :], rows[:, bass.ds(g * GR, GR), :],
                                           w.v["bo"][:, :].unsqueeze(1).to_broadcast([P, GR, D]), ALU.add).then_inc(bias_added, 1)

                normalise(0, yn[:, :, :], scale).then_inc(yn_ready, 1)
                with pool.Fori(0, NG - 1) as g:
                    prepare_residual(g)
                    for kc in range(KC):
                        pool.wait_ge(filled[kc], done(task(g, ("y", kc))))
                    normalise(g + 1, yn[:, :, :], scale).then_inc(yn_ready, 1)
                prepare_residual(NG - 1)

            @block.scalar
            def _(act):
                for x in (emptied[1], feat_emptied, probs_ready):
                    act.sem_inc(x, LEAD)
                ln_stats_scalar(chip, act, s, plan.double_ln)
                w.wait(act)
                if "bk" in w.v:
                    act.wait_ge(bkB_ready, 1)
                act.preload_act_table(ACT.Exp)
                def empty_mine(g, tasks):
                    for f in tasks:
                        if where[f][0] == 1:
                            empty_bank(act, 1, g, f).then_inc(emptied[1], 1)

                empty_mine(0, early)

                def group(g, more):
                    for f in late:
                        empty_mine(g, [f])
                        if f[0] == "count":
                            act.wait_ge(step_done, g + 1)
                            act.activation(lnpad[:, :], npad1[:, :], ACT.Ln).then_inc(step_back, 1)
                        if f[0] == "km":
                            act.wait_ge(step_done, g + 1)
                            act.activation(gap[:, :, :], gap[:, :, :], ACT.Abs)
                            act.drain()
                            act.activation(bias[:, :, :], gap[:, :, :], ACT.Ln, bias=1.0).then_inc(step_back, 1)
                    for st in range(NU + 6):
                        if st < NU:
                            u = st
                            j = u // U
                            act.wait_ge(masked_ready, done(g * NU + u))
                            act.wait_ge(probsT_ready, done(g * NU + u - 3))
                            for i in range(UH):
                                h = u % U * UH + i
                                op = act.activation(p[:, u % 3, i, :], sm[:, u % 2, i, :], ACT.Exp, bias=nmx[:, u % 2, i:i + 1], scale=-1.0,
                                                    accum_out=rsum[:, j, h:h + 1])
                            op.then_inc(probs_ready, 1)
                        if 0 <= st - 5 < NU and (st - 5) % U == U - 1:
                            j = (st - 5) // U
                            for n, (c0, c1) in enumerate(otasks):
                                act.wait_ge(feat_filled, done((g * GR + j) * n_feat + n))
                                act.copy(oT[:, c0:c1, :], proj[1][:, 0:(c1 - c0) * P].rearrange("p (c q) -> p c q", c=c1 - c0)).then_inc(feat_emptied, 1)
                        if more and st in (NU + 3, NU + 5):
                            empty_mine(g + 1, turns if st == NU + 3 else ks + qs)

                with act.Fori(0, NG - 1) as g:
                    group(g, True)
                group(NG - 1, False)


def l0_xattn_weights(chip, side):
    i, w = chip.ins, Weights(chip, "l0x", side)
    w.v = dict(q=w.matrix(i["L0_xattn_Wq"]), k=w.matrix(i["L0_xattn_Wk"]), v=w.matrix(i["L0_xattn_Wv"]), o=w.matrix(i["L0_xattn_Wo"]),
               bq=w.columns(i["L0_xattn_bq"]), bk=w.columns(i["L0_xattn_bk"]), bv=w.everywhere(i["L0_xattn_bv"]), bo=w.everywhere(i["L0_xattn_bo"]))
    return w


def l1_attn_weights(chip, side):
    i, w = chip.ins, Weights(chip, "l1a", side)
    wa, ba = i["L1_attn_W_attn"], i["L1_attn_b_attn"]
    w.v = dict(q=w.matrix(wa[:, 0:D]), k=w.matrix(wa[:, D:2 * D]), v=w.matrix(wa[:, 2 * D:3 * D]), o=w.matrix(i["L1_attn_W_proj"]),
               bq=w.columns(ba[0:D]), bk=w.columns(ba[D:2 * D]), bv=w.everywhere(ba[2 * D:3 * D]), bo=w.everywhere(i["L1_attn_b_proj"]))
    return w


def l2_attn_weights(chip, side):
    i, w = chip.ins, Weights(chip, "l2a", side)

    def heads(src):
        v = w.room(KC * 1024).rearrange("p (c h a) -> p c h a", c=KC, a=64)
        for c in range(KC):
            w.dmas.append((v[:, c], src[:, c * P:(c + 1) * P, :].rearrange("h p a -> p h a")))
        return v.rearrange("p c h a -> p c (h a)")

    w.v = dict(q=heads(i["L2_attn_Wq"]), k=heads(i["L2_attn_Wk"]), v=heads(i["L2_attn_Wv"]),
               o=w.matrix(i["L2_attn_Wo"].rearrange("h a d -> (h a) d")),
               bq=w.columns(i["L2_attn_bq"].rearrange("h a -> (h a)")), bk=w.columns(i["L2_attn_bk"].rearrange("h a -> (h a)")),
               bv=w.everywhere(i["L2_attn_bv"].rearrange("h a -> (h a)")), bo=w.everywhere(i["L2_attn_bo"]))
    return w


def l2_xattn_weights(chip, side):
    i, w = chip.ins, Weights(chip, "l2x", side)
    kv = i["L2_xattn_Wkv"]
    w.v = dict(q=w.matrix(i["L2_xattn_Wq"]), k=w.matrix(kv[:, 0:512]), v=w.matrix(kv[:, 512:1024]), o=w.matrix(i["L2_xattn_Wout"]),
               g=w.columns(i["L2_xattn_ln_w"]), b=w.columns(i["L2_xattn_ln_b"]))
    return w


def l2_ffn_attn_weights(chip, side):
    i, w = chip.ins, Weights(chip, "l2fa", side)
    w.v = dict(q=w.matrix(i["L2_ffn_wq"]), k=w.matrix(i["L2_ffn_wk"]), v=w.matrix(i["L2_ffn_wv"]), o=w.matrix(i["L2_ffn_wo"]),
               bq=w.columns(i["L2_ffn_bq"]), bk=w.columns(i["L2_ffn_bk"]), bv=w.everywhere(i["L2_ffn_bv"]), bo=w.everywhere(i["L2_ffn_bo"]),
               g=w.columns(i["L2_ffn_ln1_g"]), b=w.columns(i["L2_ffn_ln1_b"]))
    return w


def l3_xattn_weights(chip, side):
    i, w = chip.ins, Weights(chip, "l3x", side)
    w.v = dict(q=w.matrix(i["L3_xattn_Wq"]), k=w.repeated(i["L3_xattn_Wk"], 4), v=w.matrix(i["L3_xattn_Wv"]), o=w.matrix(i["L3_xattn_Wo"]),
               tb=w.everywhere(i["L3_xattn_time_bias_weight"]))
    return w


PLANS = {
    "l0x": (l0_xattn_weights, AttentionPlan("l0x", 16, 16, 0.25, "keymask", "ctx")),
    "l1a": (l1_attn_weights, AttentionPlan("l1a", 16, 16, 0.25, "causal")),
    "l2a": (l2_attn_weights, AttentionPlan("l2a", 16, 64, 0.125, "causal")),
    "l2x": (l2_xattn_weights, AttentionPlan("l2x", 8, 64, 0.125, "support", "ctx", causal_gap=5.0, double_ln=True)),
    "l2fa": (l2_ffn_attn_weights, AttentionPlan("l2fa", 16, 16, 0.25, "none", double_ln=True, residual="Y")),
    "l3x": (l3_xattn_weights, AttentionPlan("l3x", 16, 16, 0.25, "timebias", "ctx", kv_heads=4)),
}


HC = 8
HS = HC // 2
SLOT = 2 * HC * D


class ExpertPlan:

    def __init__(self, tag, names, hidden, keep, deep_router=False, from_y=False):
        self.tag, self.names, self.hidden, self.keep = tag, names, hidden, keep
        self.deep_router, self.from_y = deep_router, from_y


def gates_vector(chip, dve, act_sems, plan, logits, tiles):
    iota, lg, hit, one, two, best, best2, at, e, g1, gates = tiles
    over_e = lambda x: x[:, :].unsqueeze(2).to_broadcast([P, NB, NE])
    ranks = iota[:, :].unsqueeze(1).to_broadcast([P, NB, NE])
    for i in range(NE):
        dve.memset(iota[:, i:i + 1], float(i - NE))
    dve.tensor_copy(lg[:, :, :], logits)
    dve.drain()

    def first_max(best, onehot):
        dve.tensor_reduce(best[:, :], lg[:, :, :], AX.X, ALU.max)
        dve.drain()
        dve.tensor_tensor(hit[:, :, :], lg[:, :, :], over_e(best), ALU.is_equal)
        dve.drain()
        dve.tensor_tensor(hit[:, :, :], hit[:, :, :], ranks, ALU.mult)
        dve.drain()
        dve.tensor_reduce(at[:, :], hit[:, :, :], AX.X, ALU.min)
        dve.drain()
        dve.tensor_tensor(onehot[:, :, :], over_e(at), ranks, ALU.is_equal)
        dve.drain()

    if plan.keep == 1:
        first_max(best, gates)
        return
    first_max(best, one)
    dve.scalar_tensor_tensor(out=lg[:, :, :], in0=one[:, :, :], scalar=-1e30, in1=lg[:, :, :], op0=ALU.mult, op1=ALU.add)
    dve.drain()
    first_max(best2, two)
    dve.tensor_tensor(e[:, :], best2[:, :], best[:, :], ALU.subtract).then_inc(act_sems["gap_ready"], 1)
    dve.wait_ge(act_sems["exp_ready"], 1)
    dve.tensor_scalar(g1[:, :], e[:, :], 1.0, None, ALU.add)
    dve.drain()
    dve.reciprocal(g1[:, :], g1[:, :])
    dve.drain()
    dve.tensor_tensor(e[:, :], e[:, :], g1[:, :], ALU.mult)
    dve.drain()
    dve.tensor_tensor(gates[:, :, :], one[:, :, :], over_e(g1), ALU.mult)
    dve.tensor_tensor(hit[:, :, :], two[:, :, :], over_e(e), ALU.mult)
    dve.drain()
    dve.tensor_tensor(gates[:, :, :], gates[:, :, :], hit[:, :, :], ALU.add)
    dve.drain()


def gates_scalar(act, act_sems, plan, tiles):
    e = tiles[8]
    if plan.keep == 2:
        act.wait_ge(act_sems["gap_ready"], 1)
        act.activation(e[:, :], e[:, :], ACT.Exp).then_inc(act_sems["exp_ready"], 1)


def gate_tiles(sb):
    return (sb("ranks", [P, NE]), sb("logits", [P, NB, NE]), sb("hit", [P, NB, NE]), sb("one", [P, NB, NE]), sb("two", [P, NB, NE]),
            sb("best", [P, NB]), sb("best2", [P, NB]), sb("at", [P, NB]), sb("e", [P, NB]), sb("g1", [P, NB]), sb("gates", [P, NB, NE]))


def small_experts_block(chip, plan, w, prefetch, have_stats):
    nc, t = chip.nc, plan.tag
    NX = NE + 2
    with ExitStack() as scope:
        sb = lambda n, s, d=F32: chip.block_sb(f"{t}_{n}", s, d, scope)
        sem = lambda n: chip.sem(f"{t}_{n}")
        yn = sb("yn", [P, 2, GR, D])
        yT = sb("yT", [P, KC, NB * P])
        silu = sb("silu", [P, 2, TG])
        hT = sb("hT", [P, 2, TG])
        tiles = gate_tiles(sb)
        gates = tiles[-1]
        bank = [chip.ps(f"{t}_bank{i}", scope) for i in range(8)]
        s = {n: sem(n) for n in ("var_ready", "std_ready")}
        act_sems = {n: sem(n) for n in ("gap_ready", "exp_ready")}
        yn_ready = sem("yn_ready")
        turned = [sem("turned0"), sem("turned1")]
        yT_ready = [sem("yT0_ready"), sem("yT1_ready")]
        logits_ready = sem("logits_ready")
        gate_ready, up_ready = sem("gate_ready"), sem("up_ready")
        silu_ready = sem("silu_ready")
        hidden_ready = sem("hidden_ready")
        out_ready = sem("out_ready")
        out_added = sem("out_added")

        with nc.Block() as block:
            @block.sync
            def _(sp):
                if prefetch:
                    prefetch.load(sp)

            @block.tensor
            def _(pe):
                for x in (gate_ready, up_ready, out_ready):
                    pe.sem_inc(x, LEAD)
                w.wait(pe)
                for g in range(NG):
                    pe.wait_ge(yn_ready, g + 1)
                    for kc in range(KC):
                        if g:
                            pe.wait_ge(yT_ready[kc], g)
                        for j in range(GR):
                            mm = pe.transpose(bank[kc][:, j * P:(j + 1) * P], yn[:, g % 2, j, kc * P:(kc + 1) * P], chip.ident[:, :])
                        mm.then_inc(turned[kc], 1)
                for b in range(NB):
                    if b % GR == 0:
                        for kc in range(KC):
                            pe.wait_ge(yT_ready[kc], b // GR + 1)
                    o = bank[2][:, b * NE:(b + 1) * NE]
                    pe.matmul(o, chip.ones[0:1, 0:P], w.v["rb"], start=True, stop=False)
                    for kc in range(KC):
                        mm = pe.matmul(o, yT[:, kc, b * P:(b + 1) * P], w.v["rw"][:, kc, :], start=False, stop=(kc == KC - 1))
                mm.then_inc(logits_ready, 1)
                pe.wait_ge(hidden_ready, LEAD)
                with pe.Fori(0, NG) as g:
                    for i in range(NX + 1):
                        if i < NX:
                            n = g * NX + i
                            for m, ready, freed in (("w1", gate_ready, silu_ready), ("w3", up_ready, hidden_ready)):
                                pe.wait_ge(freed, done(n - 2))
                                o = bank[(0 if m == "w1" else 2) + i % 2]
                                for kc in range(KC):
                                    mm = pe.matmul(o[:, :], w.v[m][:, i, kc, :], yT[:, kc, bass.ds(g * TG, TG)], start=(kc == 0), stop=(kc == KC - 1))
                                mm.then_inc(ready, 1)
                        if i >= 1:
                            x = i - 1
                            pe.wait_ge(hidden_ready, done(g * NX + x))
                            if x <= NE:
                                pe.wait_ge(out_added, done(g * (NE + 1) + x - 1))
                            for j in range(GR):
                                mm = pe.matmul(bank[4 + j][:, 0:D], hT[:, x % 2, j * P:(j + 1) * P], w.v["w2"][:, x, :],
                                               start=(x <= NE), stop=(x != NE))
                            if x != NE:
                                mm.then_inc(out_ready, 1)

            @block.vector
            def _(dve):
                for x in (out_added,):
                    dve.sem_inc(x, LEAD)
                ln_stats_vector(chip, dve, chip.X, s, have=have_stats)
                w.wait(dve)
                for g in range(NG):
                    if g >= 2:
                        for kc in range(KC):
                            dve.wait_ge(turned[kc], g - 1)
                    for j in range(GR):
                        b = g * GR + j
                        op = dve.tensor_scalar(yn[:, g % 2, j, :], chip.X[:, b, :], chip.mv[:, b, 0:1], chip.rstd[:, b:b + 1], ALU.subtract, ALU.mult)
                    op.then_inc(yn_ready, 1)
                    dve.wait_ge(turned[0], g + 1)
                    dve.tensor_copy(yT[:, 0, g * TG:(g + 1) * TG], bank[0][:, :]).then_inc(yT_ready[0], 1)
                dve.wait_ge(logits_ready, 1)
                gates_vector(chip, dve, act_sems, plan, bank[2][:, 0:NB * NE].rearrange("p (b e) -> p b e", b=NB), tiles)
                dve.sem_inc(hidden_ready, LEAD)
                with dve.Fori(0, NG) as g:
                    for i in range(NX + 2):
                        if i < NX:
                            n = g * NX + i
                            dve.wait_ge(silu_ready, done(n))
                            dve.wait_ge(up_ready, done(n))
                            dve.tensor_tensor(hT[:, i % 2, :], silu[:, i % 2, :], bank[2 + i % 2][:, :], ALU.mult).then_inc(hidden_ready, 1)
                        x = i - 1
                        if 0 <= x < NE or x == NX - 1:
                            m = min(x, NE)
                            dve.wait_ge(out_ready, done(g * (NE + 1) + m))
                            for j in range(GR):
                                b = g * GR + j
                                if x < NE:
                                    op = dve.scalar_tensor_tensor(out=chip.X[:, b, :], in0=bank[4 + j][:, 0:D], scalar=gates[:, b, x:x + 1],
                                                                  in1=chip.X[:, b, :], op0=ALU.mult, op1=ALU.add)
                                else:
                                    op = dve.tensor_tensor(chip.X[:, b, :], chip.X[:, b, :], bank[4 + j][:, 0:D], ALU.add)
                            op.then_inc(out_added, 1)
                            if x == NX - 1:
                                dve.drain()
                                for b in [g * GR + j for j in range(GR)]:
                                    dve.bn_stats(chip.bn[:, b, :], chip.X[:, b, :])

            @block.scalar
            def _(act):
                act.sem_inc(silu_ready, LEAD)
                ln_stats_scalar(chip, act, s)
                for g in range(NG):
                    act.wait_ge(turned[1], g + 1)
                    act.copy(yT[:, 1, g * TG:(g + 1) * TG], bank[1][:, :]).then_inc(yT_ready[1], 1)
                gates_scalar(act, act_sems, plan, tiles)
                act.preload_act_table(ACT.Silu)
                act.wait_ge(hidden_ready, LEAD)
                with act.Fori(0, NG) as g:
                    for i in range(NX):
                        n = g * NX + i
                        act.wait_ge(gate_ready, done(n))
                        act.wait_ge(hidden_ready, done(n - 2))
                        act.activation(silu[:, i % 2, :], bank[i % 2][:, :], ACT.Silu).then_inc(silu_ready, 1)


def sorted_experts_block(chip, plan, w, prefetch, have_stats):
    nc, t, keep = chip.nc, plan.tag, plan.keep
    side = w.side
    F, TOK = plan.hidden, NB * P
    NT = NB * keep + NE - 1
    assert NT % 2 == 1 and F == HC * P
    half_f = F // 2
    src = chip.Y if plan.from_y else chip.X
    slot = lambda n: chip.room[:, n * SLOT:(n + 1) * SLOT]
    late = {NE - 1} | ({NE - 2, 2 * side + 1} if plan.deep_router else set())
    with ExitStack() as scope:
        sb = lambda n, s, d=F32: chip.sb(f"{t}_{n}", s, d, scope)
        sem = lambda n: chip.sem(f"{t}_{n}")
        yn = chip.Y
        yT = slot(NE - 1).rearrange("p (c t) -> p c t", c=KC)
        rT = slot(NE - 2).rearrange("p (f t) -> p f t", f=HC)
        tiles = gate_tiles(sb)
        one, two, second_weight, first_weight, gates = tiles[3], tiles[4], tiles[8], tiles[9], tiles[10]
        choices = [gates] if keep == 1 else [one, two]
        strict = sb("strict", [P, P])
        lower = sb("lower", [P, NE, NE])
        hot = sb("hot", [P, NB, NE]) if keep == 2 else gates
        wide = sb("wide", [P, MAX_TILES, NE])
        count, ntiles, end, begin = [sb(n, [P, NE]) for n in ("count", "ntiles", "end", "begin")]
        exceeds = sb("exceeds", [P, NE, NB])
        thresholds = sb("thresholds", [P, NB])
        place = sb("place", [P, NB, NE])
        chosen = sb("chosen", [P, NB, NE])
        place_f = sb("place_f", [P, NB])
        place_i = [sb(f"place{c}_i", [P, NB], mybir.dt.uint32) for c in range(keep)]
        owner, wrap, scaled = [sb(n, [P, NT]) for n in ("owner", "wrap", "scaled")]
        weights_at, bias_at = sb("weights_at", [P, NT], I32), sb("bias_at", [P, NT], I32)
        gT = sb("gT", [NE, TOK])
        cut = chip.Y[:, :, :].rearrange("p b d -> p (b d)")
        rows = cut[:, 0:2 * D].rearrange("p (a d) -> p a d", a=2)
        rowsT = cut[:, 2 * D:4 * D].rearrange("p (a c t) -> p a c t", a=2, c=KC)
        h = cut[:, 4 * D:4 * D + F].rearrange("p (a f) -> p a f", a=2)
        hT = cut[:, 4 * D + F:4 * D + 2 * F].rearrange("p (f t) -> p f t", f=HC)
        result = cut[:, 4 * D + 2 * F:6 * D + 2 * F].rearrange("p (a d) -> p a d", a=2)
        back = [chip.Y, chip.room[:, 0:NB * D].rearrange("p (b d) -> p b d", b=NB)]

        hbank = [chip.ps(f"{t}_hidden{i}", scope) for i in range(2)]
        tbank = [chip.ps(f"{t}_hiddenT{i}", scope) for i in range(2)]
        obank = [chip.ps(f"{t}_out{i}", scope) for i in range(2)]
        lbank = chip.ps(f"{t}_logits_ps", scope)
        rbank = chip.ps(f"{t}_ranks_ps", scope)
        s = {n: sem(n) for n in ("var_ready", "std_ready")}
        act_sems = {n: sem(n) for n in ("gap_ready", "exp_ready")}
        yn_ready = sem("yn_ready")
        filled = [sem("hidden0_filled"), sem("hidden1_filled")]
        emptied = [sem("hidden0_emptied"), sem("hidden1_emptied")]
        logits_ready = sem("logits_ready")
        gates_ready = sem("gates_ready")
        ranks_ready = sem("ranks_ready")
        gT_filled = sem("gT_filled")
        gT_copied = sem("gT_copied")
        bias_filled = sem("bias_filled")
        bias_added = sem("bias_added")
        places_ready = sem("places_ready")
        owners_ready = sem("owners_ready")
        scattered = sem("scattered")
        rows_in = [sem("rows0_in"), sem("rows1_in")]
        turned = sem("turned")
        rowsT_ready = sem("rowsT_ready")
        h_filled = [sem("h0_filled"), sem("h1_filled")]
        h_copied = [sem("h0_copied"), sem("h1_copied")]
        hT_filled = [sem("hT0_filled"), sem("hT1_filled")]
        hT_ready = [sem("hT0_ready"), sem("hT1_ready")]
        out_filled = sem("out_filled")
        out_copied = sem("out_copied")
        stored = [sem("stored0"), sem("stored1")]
        gathered = [sem(f"gathered{g}") for g in range(NG)]
        act_turn = sem("act_turn")

        with nc.Block() as block:
            @block.sync
            def _(sp):
                for x in stored:
                    sp.sem_inc(x, 16)
                ahead = len(w.streams) // 2
                rest = [(e, (e + 2 * side) % NE) for e in range(ahead, NE)]
                for e, n in [r for r in rest if r[1] not in late] + [r for r in rest if r[1] in late]:
                    if n in late:
                        sp.wait_ge(logits_ready, 1)
                    for dst, part in expert_loads(chip, plan, e, side):
                        sp.dma_start(dst, part).then_inc(w.v["landed"], 16)

                def load(i, par):
                    sp.dma_start(rows[:, par, :], chip.sorted_rows[bass.ds(i * (2 * P) + par * P, P), :]).then_inc(rows_in[par], 16)

                def step(i, par, more):
                    n = i * 2 + par
                    if more:
                        sp.wait_ge(turned, done(n))
                        load(i + 1, par)
                    sp.wait_ge(out_copied, done(n))
                    sp.dma_start(chip.sorted_out[bass.ds(i * (2 * P) + par * P, P), :], result[:, par, :]).then_inc(stored[par], 16)

                sp.wait_ge(scattered, 16 * NB * keep)
                load(0, 0)
                load(0, 1)
                with sp.Fori(0, NT // 2 - 1) as i:
                    step(i, 0, True)
                    step(i, 1, True)
                step(NT // 2 - 1, 0, True)
                step(NT // 2 - 1, 1, False)
                step(NT // 2, 0, False)
                if prefetch:
                    sp.wait_ge(out_filled, done(NT - 1))
                    prefetch.load(sp)

            @block.tensor
            def _(pe):
                for x in (*filled, turned, *h_filled, *hT_filled, out_filled):
                    pe.sem_inc(x, LEAD)
                w.wait(pe)
                for g in range(NG):
                    pe.wait_ge(yn_ready, g + 1)
                    for kc in range(KC):
                        pe.wait_ge(emptied[kc], done(g - 1))
                        for j in range(GR):
                            mm = pe.transpose(hbank[kc][:, j * P:(j + 1) * P], yn[:, g * GR + j, kc * P:(kc + 1) * P], chip.ident[:, :])
                        mm.then_inc(filled[kc], 1)
                for kc in range(KC):
                    pe.wait_ge(emptied[kc], done(NG - 1))
                base = NG
                for g in range(NG):
                    if plan.deep_router:
                        for f in range(HC):
                            b = f % 2
                            pe.wait_ge(emptied[b], done(base + f // 2 - 1))
                            for kc in range(KC):
                                mm = pe.matmul(hbank[b][:, :], w.v["rw1"][:, kc, f * P:(f + 1) * P], yT[:, kc, g * TG:(g + 1) * TG],
                                               start=(kc == 0), stop=(kc == KC - 1))
                            mm.then_inc(filled[b], 1)
                        base += HC // 2
                    for j in range(GR):
                        b = g * GR + j
                        o = lbank[:, b * NE:(b + 1) * NE]
                        pe.matmul(o, chip.ones[0:1, 0:P], w.v["rb"], start=True, stop=False)
                        if plan.deep_router:
                            for f in range(HC):
                                pe.wait_ge(emptied[f % 2], done(base - HC // 2 + f // 2))
                                mm = pe.matmul(o, rT[:, f, j * P:(j + 1) * P], w.v["rw"][:, f, :], start=False, stop=(f == HC - 1))
                        else:
                            for kc in range(KC):
                                mm = pe.matmul(o, yT[:, kc, b * P:(b + 1) * P], w.v["rw"][:, kc, :], start=False, stop=(kc == KC - 1))
                mm.then_inc(logits_ready, 1)

                pe.wait_ge(gates_ready, 1)
                flat = hot[:, :, :].rearrange("p b e -> p (b e)")
                for b in range(NB):
                    pe.matmul(rbank[:, NB * NE:NB * NE + NE], chip.ones[:, 0:P], flat[:, b * NE:(b + 1) * NE], start=(b == 0), stop=(b == NB - 1))
                pe.matmul(rbank[:, 0:NB * NE], strict[:, :], flat, start=True, stop=False)
                for k in range(1, NB):
                    mm = pe.matmul(rbank[:, k * NE:NB * NE], chip.ones[:, 0:P], flat[:, 0:(NB - k) * NE], start=False, stop=(k == NB - 1))
                mm.then_inc(ranks_ready, 1)
                for g in range(NG):
                    if g >= 2:
                        pe.wait_ge(gT_copied, g - 1)
                    for j in range(GR):
                        mm = pe.transpose(hbank[g % 2][0:NE, j * P:(j + 1) * P], gates[:, g * GR + j, :], chip.ident[:, :])
                    mm.then_inc(gT_filled, 1)
                for b in range(NB):
                    if b % GR == 0:
                        pe.wait_ge(gT_copied, b // GR + 1)
                    pair = b // 2
                    if b % 2 == 0 and pair >= 2:
                        pe.wait_ge(bias_added, pair - 1)
                    mm = pe.matmul(obank[pair % 2][:, b % 2 * D:(b % 2 + 1) * D], gT[:, b * P:(b + 1) * P], w.v["b2"], start=True, stop=True)
                    if b % 2:
                        mm.then_inc(bias_filled, 1)

                def weights_of(i, par):
                    return pe.value_load(weights_at[0:1, bass.ds(i * 2 + par, 1)], min_val=0, max_val=(NE - 1) * SLOT)

                def turn(i, par):
                    pe.wait_ge(rows_in[par], i * 16 + 16)
                    pe.wait_ge(rowsT_ready, done(i * 2 + (par - 1)))
                    for kc in range(KC):
                        mm = pe.transpose(lbank[:, kc * P:(kc + 1) * P], rows[:, par, kc * P:(kc + 1) * P], chip.ident[:, :])
                    mm.then_inc(turned, 1)

                def first_layer(i, par):
                    at, n = weights_of(i, par), i * 2 + par
                    pe.wait_ge(rowsT_ready, done(n))
                    for a in range(2):
                        pe.wait_ge(h_copied[a], done(n - 1))
                        for kc in range(KC):
                            mm = pe.matmul(hbank[a][:, :], rowsT[:, par, kc, :], chip.room[:, bass.ds(at + (kc * F + a * half_f), half_f)],
                                           start=(kc == 0), stop=(kc == KC - 1))
                        mm.then_inc(h_filled[a], 1)

                def turn_hidden(i, par):
                    n = i * 2 + par
                    for a in range(2):
                        pe.wait_ge(h_copied[a], done(n))
                        pe.wait_ge(hT_ready[a], done(n - 1))
                        for q in range(HS):
                            mm = pe.transpose(tbank[a][:, q * P:(q + 1) * P], h[:, a, q * P:(q + 1) * P], chip.ident[:, :])
                        mm.then_inc(hT_filled[a], 1)

                def second_layer(i, par):
                    at, n = weights_of(i, par), i * 2 + par
                    pe.wait_ge(out_copied, done(n - 2))
                    for f in range(HC):
                        if f % HS == 0:
                            pe.wait_ge(hT_ready[f // HS], done(n))
                        mm = pe.matmul(obank[par][:, 0:D], hT[:, f, :], chip.room[:, bass.ds(at + (SLOT // 2 + f * D), D)],
                                       start=(f == 0), stop=(f == HC - 1))
                    mm.then_inc(out_filled, 1)

                def step(i, par):
                    turn(i + par, 1 - par)
                    turn_hidden(i, par)
                    first_layer(i + par, 1 - par)
                    second_layer(i, par)

                pe.wait_ge(owners_ready, 1)
                pe.wait_ge(w.v["landed"], 32 * NE)
                pe.wait_ge(bias_added, NB // 2)
                turn(0, 0)
                first_layer(0, 0)
                with pe.Fori(0, NT // 2) as i:
                    step(i, 0)
                    step(i, 1)
                turn_hidden(NT // 2, 0)
                second_layer(NT // 2, 0)

            def y_affine(eng, kc, dst, src):
                if "g" in w.v:
                    mul, add = w.v["g"][:, kc:kc + 1], w.v["b"][:, kc:kc + 1]
                    if eng is nc.vector:
                        return eng.tensor_scalar(dst, src, mul, add, ALU.mult, ALU.add)
                    return eng.activation(dst, src, ACT.Identity, bias=add, scale=mul)
                return eng.tensor_copy(dst, src) if eng is nc.vector else eng.copy(dst, src)

            def router_relu(eng, b, base):
                for f in range(b, HC, 2):
                    eng.wait_ge(filled[b], done(base + f // 2))
                    if b == 0:
                        op = eng.tensor_scalar(rT[:, f, :], hbank[0][:, :], w.v["rb1"][:, f:f + 1], 0.0, ALU.add, ALU.max)
                    else:
                        op = eng.activation(rT[:, f, :], hbank[1][:, :], ACT.Relu, bias=w.v["rb1"][:, f:f + 1])
                    op.then_inc(emptied[b], 1)

            @block.vector
            def _(dve):
                for x in (emptied[0], rowsT_ready, h_copied[0], hT_ready[0]):
                    dve.sem_inc(x, LEAD)
                w.wait(dve)
                ln_stats_vector(chip, dve, src, s, have=have_stats)
                if plan.from_y:
                    dve.tensor_tensor(chip.X[:, :, :], chip.X[:, :, :], chip.Y[:, :, :], ALU.add)
                    dve.drain()
                for b in range(NB):
                    op = dve.tensor_scalar(yn[:, b, :], src[:, b, :], chip.mv[:, b, 0:1], chip.rstd[:, b:b + 1], ALU.subtract, ALU.mult)
                    if b % GR == GR - 1:
                        op.then_inc(yn_ready, 1)
                for g in range(NG):
                    dve.wait_ge(filled[0], done(g))
                    y_affine(dve, 0, yT[:, 0, g * TG:(g + 1) * TG], hbank[0][:, :]).then_inc(emptied[0], 1)
                dve.tensor_tensor(strict[:, :], chip.upper[:, :], chip.ident[:, :], ALU.subtract)
                experts = chip.iota[:, 0:NE]
                dve.tensor_tensor(lower[:, :, :], experts.unsqueeze(2).to_broadcast([P, NE, NE]), experts.unsqueeze(1).to_broadcast([P, NE, NE]), ALU.is_ge)
                dve.tensor_scalar(thresholds[:, :], chip.iota[:, 0:NB], float(P), None, ALU.mult)
                if plan.deep_router:
                    for g in range(NG):
                        router_relu(dve, 0, NG + g * (HC // 2))
                dve.wait_ge(logits_ready, 1)
                gates_vector(chip, dve, act_sems, plan, lbank[:, 0:NB * NE].rearrange("p (b e) -> p b e", b=NB), tiles)
                if keep == 2:
                    dve.tensor_tensor(hot[:, :, :], one[:, :, :], two[:, :, :], ALU.add)
                    dve.drain()
                dve.sem_inc(gates_ready, 1)

                dve.wait_ge(ranks_ready, 1)
                dve.tensor_copy(count[:, :], rbank[:, NB * NE:NB * NE + NE])
                dve.drain()
                dve.tensor_tensor(exceeds[:, :, :], count[:, :].unsqueeze(2).to_broadcast([P, NE, NB]),
                                  thresholds[:, :].unsqueeze(1).to_broadcast([P, NE, NB]), ALU.is_gt)
                dve.drain()
                dve.tensor_reduce(ntiles[:, :], exceeds[:, :, :], AX.X, ALU.add)
                dve.drain()
                dve.tensor_tensor(lower[:, :, :], lower[:, :, :], ntiles[:, :].unsqueeze(1).to_broadcast([P, NE, NE]), ALU.mult)
                dve.drain()
                dve.tensor_reduce(end[:, :], lower[:, :, :], AX.X, ALU.add)
                dve.drain()
                dve.tensor_tensor(begin[:, :], end[:, :], ntiles[:, :], ALU.subtract)
                dve.drain()
                dve.scalar_tensor_tensor(out=place[:, :, :], in0=begin[:, :].unsqueeze(1).to_broadcast([P, NB, NE]), scalar=float(P),
                                         in1=rbank[:, 0:NB * NE].rearrange("p (b e) -> p b e", b=NB), op0=ALU.mult, op1=ALU.add)
                dve.drain()
                for c in range(keep):
                    dve.tensor_tensor(chosen[:, :, :], place[:, :, :], choices[c][:, :, :], ALU.mult)
                    dve.drain()
                    dve.tensor_reduce(place_f[:, :], chosen[:, :, :], AX.X, ALU.add)
                    dve.drain()
                    dve.tensor_copy(place_i[c][:, :], place_f[:, :]).then_inc(places_ready, 1)
                dve.tensor_tensor(wide[:, 0:NT, :], chip.iota[:, 0:NT].unsqueeze(2).to_broadcast([P, NT, NE]),
                                  end[:, :].unsqueeze(1).to_broadcast([P, NT, NE]), ALU.is_ge)
                dve.drain()
                dve.tensor_reduce(owner[:, :], wide[:, 0:NT, :], AX.X, ALU.add)
                dve.drain()
                dve.tensor_scalar(owner[:, :], owner[:, :], float(NE - 1), None, ALU.min)
                dve.drain()
                if side:
                    dve.tensor_scalar(wrap[:, :], owner[:, :], float(NE - 2 * side), -float(NE), ALU.is_ge, ALU.mult)
                    dve.drain()
                    dve.scalar_tensor_tensor(out=owner[:, :], in0=owner[:, :], scalar=float(2 * side), in1=wrap[:, :], op0=ALU.add, op1=ALU.add)
                    dve.drain()
                for n, (scale, to) in enumerate(((SLOT, weights_at), (HC, bias_at))):
                    dve.tensor_scalar(scaled[:, :], owner[:, :], float(scale), None, ALU.mult)
                    dve.drain()
                    dve.tensor_copy(to[:, :], scaled[:, :])
                    dve.drain()
                dve.sem_inc(owners_ready, 1)
                for i in range(NB // 2):
                    dve.wait_ge(bias_filled, i + 1)
                    dve.tensor_tensor(chip.X[:, 2 * i:2 * i + 2, :], chip.X[:, 2 * i:2 * i + 2, :],
                                      obank[i % 2][:, :].rearrange("p (b d) -> p b d", b=2), ALU.add).then_inc(bias_added, 1)

                def empty_rows(i, par):
                    dve.wait_ge(turned, done(i * 2 + par))
                    if "g" in w.v:
                        for kc in range(KC):
                            op = y_affine(dve, kc, rowsT[:, par, kc, :], lbank[:, kc * P:(kc + 1) * P])
                    else:
                        op = dve.tensor_copy(rowsT[:, par, :, :].rearrange("p c t -> p (c t)"), lbank[:, 0:D])
                    op.then_inc(rowsT_ready, 1)

                def empty_hidden(i, par):
                    dve.wait_ge(h_filled[0], done(i * 2 + par))
                    dve.tensor_copy(h[:, 0, :], hbank[0][:, :]).then_inc(h_copied[0], 1)

                def relu(i, par):
                    at = dve.value_load(bias_at[0:1, bass.ds(i * 2 + par, 1)], min_val=0, max_val=(NE - 1) * HC)
                    dve.wait_ge(hT_filled[0], done(i * 2 + par))
                    for q in range(HS):
                        op = dve.tensor_scalar(hT[:, q, :], tbank[0][:, q * P:(q + 1) * P], w.v["b1"][:, bass.ds(at + q, 1)], 0.0, ALU.add, ALU.max)
                    op.then_inc(hT_ready[0], 1)

                def step(i, par):
                    empty_rows(i + par, 1 - par)
                    relu(i, par)
                    empty_hidden(i + par, 1 - par)

                empty_rows(0, 0)
                empty_hidden(0, 0)
                with dve.Fori(0, NT // 2) as i:
                    step(i, 0)
                    step(i, 1)
                relu(NT // 2, 0)
                for g in range(NG):
                    dve.wait_ge(gathered[g], 16 * GR * keep)
                    x = chip.X[:, g * GR:(g + 1) * GR, :]
                    if keep == 1:
                        dve.tensor_tensor(x, x, back[0][:, g * GR:(g + 1) * GR, :], ALU.add)
                    for b in range(g * GR, (g + 1) * GR):
                        if keep == 2:
                            for c, weight in enumerate((first_weight, second_weight)):
                                if c:
                                    dve.drain()
                                dve.scalar_tensor_tensor(out=chip.X[:, b, :], in0=back[c][:, b, :], scalar=weight[:, b:b + 1],
                                                         in1=chip.X[:, b, :], op0=ALU.mult, op1=ALU.add)
                    if prefetch:
                        dve.drain()
                        for b in range(g * GR, (g + 1) * GR):
                            dve.bn_stats(chip.bn[:, b, :], chip.X[:, b, :])
                dve.drain()

            @block.scalar
            def _(act):
                for x in (emptied[1], h_copied[1], hT_ready[1], out_copied):
                    act.sem_inc(x, LEAD)
                ln_stats_scalar(chip, act, s)
                w.wait(act)
                for g in range(NG):
                    act.wait_ge(filled[1], done(g))
                    y_affine(act, 1, yT[:, 1, g * TG:(g + 1) * TG], hbank[1][:, :]).then_inc(emptied[1], 1)
                if plan.deep_router:
                    for g in range(NG):
                        router_relu(act, 1, NG + g * (HC // 2))
                gates_scalar(act, act_sems, plan, tiles)
                for g in range(NG):
                    act.wait_ge(gT_filled, g + 1)
                    act.copy(gT[:, g * TG:(g + 1) * TG], hbank[g % 2][0:NE, :]).then_inc(gT_copied, 1)

                def empty_hidden(i, par):
                    act.wait_ge(h_filled[1], done(i * 2 + par))
                    act.copy(h[:, 1, :], hbank[1][:, :]).then_inc(h_copied[1], 1)

                def relu(i, par):
                    at = act.value_load(bias_at[0:1, bass.ds(i * 2 + par, 1)], min_val=0, max_val=(NE - 1) * HC)
                    act.wait_ge(hT_filled[1], done(i * 2 + par))
                    act.sem_inc(act_turn, 1)
                    for q in range(HS):
                        op = act.activation(hT[:, HS + q, :], tbank[1][:, q * P:(q + 1) * P], ACT.Relu, bias=w.v["b1"][:, bass.ds(at + (HS + q), 1)])
                    op.then_inc(hT_ready[1], 1)

                def empty_out(i, par):
                    act.wait_ge(out_filled, done(i * 2 + par))
                    act.wait_ge(stored[par], i * 16 + 16)
                    act.copy(result[:, par, :], obank[par][:, 0:D]).then_inc(out_copied, 1)

                def step(i, par):
                    relu(i, par)
                    empty_hidden(i + par, 1 - par)
                    empty_out(i, par)

                act.wait_ge(owners_ready, 1)
                empty_hidden(0, 0)
                with act.Fori(0, NT // 2) as i:
                    step(i, 0)
                    step(i, 1)
                relu(NT // 2, 0)
                empty_out(NT // 2, 0)

            @block.gpsimd
            def _(pool):
                pool.wait_ge(chip.rows_zeroed, 16)
                for c in range(keep):
                    pool.wait_ge(places_ready, c + 1)
                    for b in range(NB):
                        pool.indirect_dma_start(chip.sorted_rows[0:NT * P, :], bass.IndirectOffsetOnAxis(place_i[c][:, b:b + 1], 0),
                                                yn[:, b, :], None).then_inc(scattered, 16)
                for par in range(2):
                    pool.wait_ge(stored[par], 16 + 16 * ((NT + 1 - par) // 2))
                for g in range(NG):
                    for b in range(g * GR, (g + 1) * GR):
                        for c in range(keep):
                            pool.indirect_dma_start(back[c][:, b, :], None, chip.sorted_out[0:NT * P, :],
                                                    bass.IndirectOffsetOnAxis(place_i[c][:, b:b + 1], 0)).then_inc(gathered[g], 16)


def l1_ffn_weights(chip, side):
    i, w = chip.ins, Weights(chip, "l1f", side)
    NX = NE + 2

    def both(m, split):
        n = 2 * P if split else D
        v = w.room(NX * n)
        routed, shared = i["L1_ffn_routed_" + m], i["L1_ffn_shared_" + m]
        if split:
            v = v.rearrange("p (e c h) -> p e c h", e=NX, c=KC)
            for c in range(KC):
                w.dmas.append((v[:, 0:NE, c], routed[:, c * P:(c + 1) * P, :].rearrange("e p h -> p e h")))
                w.dmas.append((v[:, NE:NX, c], shared[:, c * P:(c + 1) * P, :].rearrange("e p h -> p e h")))
            return v
        v = v.rearrange("p (e d) -> p e d", e=NX)
        w.dmas.append((v[:, 0:NE], routed.rearrange("e p d -> p e d")))
        w.dmas.append((v[:, NE:NX], shared.rearrange("e p d -> p e d")))
        return v

    w.v = dict(w1=both("w1", True), w3=both("w3", True), w2=both("w2", False), rw=w.matrix(i["L1_ffn_router_w"], False), rb=w.row(i["L1_ffn_router_b"]))
    return w


def expert_loads(chip, plan, e, side):
    W1, W2 = chip.ins[plan.names[0]], chip.ins[plan.names[1]]
    at = (e + 2 * side) % NE * SLOT
    first = chip.room[:, at:at + SLOT // 2].rearrange("p (c f) -> p c f", c=KC)
    second = chip.room[:, at + SLOT // 2:at + SLOT].rearrange("p (c d) -> p c d", d=D)
    return ((first, W1[e].rearrange("(c p) f -> p c f", p=P)), (second, W2[e].rearrange("(c p) d -> p c d", p=P)))


def experts_weights(chip, plan, side, ahead, b1, b2):
    w = Weights(chip, plan.tag, side)
    landed = chip.lasting_sem(f"{plan.tag}_experts_landed")
    for e in range(ahead):
        w.room(SLOT)
        w.streams += [(dst, src, landed) for dst, src in expert_loads(chip, plan, e, side)]
    cols, lead = w.room(NE * HC, False), 2 * side
    flat = b1.rearrange("e (c p) -> p (e c)", p=P)
    w.dmas.append((cols[:, lead * HC:], flat[:, 0:(NE - lead) * HC]))
    if lead:
        w.dmas.append((cols[:, 0:lead * HC], flat[:, (NE - lead) * HC:]))
    rows = w.room(D, False)[0:NE, :]
    w.dmas.append((rows, b2))
    w.v = dict(landed=landed, b1=cols, b2=rows)
    return w


def l2_ffn_moe_weights(chip, side):
    i = chip.ins
    w = experts_weights(chip, EXPERTS["l2fm"], side, 2, i["L2_ffn_b1"], i["L2_ffn_b2"])
    w.v.update(rw=w.matrix(i["L2_ffn_gate_w"], False), rb=w.row(i["L2_ffn_gate_b"]), g=w.columns(i["L2_ffn_ln2_g"]), b=w.columns(i["L2_ffn_ln2_b"]))
    return w


def l3_ffn_weights(chip, side):
    i = chip.ins
    w = experts_weights(chip, EXPERTS["l3f"], side, 1, i["L3_ffn_b1"], i["L3_ffn_b2"])
    w.v.update(rw1=w.matrix(i["L3_ffn_rw1"]), rw=w.matrix(i["L3_ffn_rw2"], False), rb=w.row(i["L3_ffn_rb2"]), rb1=w.columns(i["L3_ffn_rb1"]))
    return w


EXPERTS = {
    "l1f": ExpertPlan("l1f", None, P, 2),
    "l2fm": ExpertPlan("l2fm", ("L2_ffn_w1", "L2_ffn_w2"), 1024, 1, from_y=True),
    "l3f": ExpertPlan("l3f", ("L3_ffn_W1", "L3_ffn_W2"), 1024, 2, deep_router=True),
}


def gau_weights(chip, side):
    i, w = chip.ins, Weights(chip, "gau", side)
    n = "L3_attn_"
    w.v = dict(v=w.matrix(i[n + "Wv"]), g=w.matrix(i[n + "Wg"]), x=w.matrix(i[n + "Win"]), o=w.matrix(i[n + "Wout"]),
               bv=w.everywhere(i[n + "bv"]), bg=w.everywhere(i[n + "bg"]), bo=w.everywhere(i[n + "bout"]), bx=w.columns(i[n + "bin_"]),
               mul=[w.columns(i[n + "g_" + k]) for k in ("qq", "qk", "lq", "lk")],
               add=[w.columns(i[n + "b_" + k]) for k in ("qq", "qk", "lq", "lk")])
    return w


def gau_block(chip, w, prefetch, have_stats):
    nc = chip.nc
    INNER, CH = 512, 64
    OC = INNER // P
    with ExitStack() as scope:
        sb = lambda n, s, d=F32: chip.block_sb(f"gau_{n}", s, d, scope)
        sem = lambda n: chip.sem(f"gau_{n}")
        yn = sb("yn", [P, GR, D])
        yT = sb("yT", [P, KC, TG])
        xs = sb("xs", [P, TG])
        feats = [sb(n, [P, TG]) for n in ("qq", "qk", "lq", "lk")]
        v = sb("v", [P, GR, INNER])
        gate = sb("gate", [P, GR, INNER])
        within = sb("within", [P, P])
        pos = sb("pos", [P, GR, P])
        aT = sb("aT", [P, GR, P])
        o = sb("o", [P, 2, INNER])
        oT = sb("oT", [P, OC, P])
        bank = [chip.ps(f"gau_bank{i}", scope) for i in range(8)]
        s = {n: sem(n) for n in ("var_ready", "std_ready")}
        yn_ready = sem("yn_ready")
        turned = [sem("turned0"), sem("turned1")]
        yT_ready = [sem("yT0_ready"), sem("yT1_ready")]
        x_filled = sem("x_filled")
        xs_ready = sem("xs_ready")
        feats_ready = sem("feats_ready")
        vg_filled = sem("vg_filled")
        vg_biased = sem("vg_biased")
        vg_ready = sem("vg_ready")
        bias_added = sem("bias_added")
        scores_ready = sem("scores_ready")
        aT_ready = sem("aT_ready")
        o_filled = sem("o_filled")
        o_ready = sem("o_ready")
        oT_filled = sem("oT_filled")
        oT_ready = sem("oT_ready")
        y_filled = sem("y_filled")
        y_added = sem("y_added")

        with nc.Block() as block:
            @block.sync
            def _(sp):
                if prefetch:
                    prefetch.load(sp)

            @block.tensor
            def _(pe):
                for x in (*turned, x_filled, vg_filled, scores_ready, o_filled, oT_filled, y_filled):
                    pe.sem_inc(x, LEAD)
                w.wait(pe)
                with pe.Fori(0, NG) as g:
                    pe.wait_ge(yn_ready, done(g))
                    for kc in range(KC):
                        pe.wait_ge(yT_ready[kc], done(g - 1))
                        for j in range(GR):
                            mm = pe.transpose(bank[kc][:, j * P:(j + 1) * P], yn[:, j, kc * P:(kc + 1) * P], chip.ident[:, :])
                        mm.then_inc(turned[kc], 1)
                    for kc in range(KC):
                        pe.wait_ge(yT_ready[kc], done(g))
                    for kc in range(KC):
                        mm = pe.matmul(bank[2][:, :], w.v["x"][:, kc, :], yT[:, kc, :], start=(kc == 0), stop=(kc == KC - 1))
                    mm.then_inc(x_filled, 1)
                    for j in range(GR):
                        for m in range(2):
                            n = g * (2 * GR) + (2 * j + m)
                            pe.wait_ge(vg_biased, done(n - 2))
                            for kc in range(KC):
                                mm = pe.matmul(bank[4 + m][:, :], yT[:, kc, j * P:(j + 1) * P], w.v["vg"[m]][:, kc, :], start=(kc == 0), stop=(kc == KC - 1))
                            mm.then_inc(vg_filled, 1)
                    pe.wait_ge(feats_ready, done(g))
                    qq, qk, lq, lk = feats
                    for j in range(GR):
                        pe.matmul(bank[2][:, j * P:(j + 1) * P], qk[:, j * P:(j + 1) * P], qq[:, j * P:(j + 1) * P], start=True, stop=True)
                    for j in range(GR):
                        mm = pe.matmul(bank[3][0:CH, j * CH:(j + 1) * CH], lk[:, j * P:j * P + CH], lq[:, j * P + CH:(j + 1) * P], start=True, stop=True)
                    mm.then_inc(scores_ready, 1)
                    pe.wait_ge(aT_ready, done(g))
                    pe.wait_ge(vg_ready, done(g * (2 * GR) + 2 * GR - 1))

                    def attend(j):
                        pe.wait_ge(o_ready, done(g * GR + j - 2))
                        pe.matmul(bank[6 + j % 2][:, :], aT[:, j, :], v[:, j, :], start=True, stop=True).then_inc(o_filled, 1)

                    def project(j):
                        pe.wait_ge(o_ready, done(g * GR + j))
                        pe.wait_ge(oT_ready, done(g * GR + j - 1))
                        for c in range(OC):
                            mm = pe.transpose(bank[3][:, c * P:(c + 1) * P], o[:, j % 2, c * P:(c + 1) * P], chip.ident[:, :])
                        mm.then_inc(oT_filled, 1)
                        pe.wait_ge(oT_ready, done(g * GR + j))
                        pe.wait_ge(y_added, done(g * GR + j - 1))
                        for c in range(OC):
                            mm = pe.matmul(bank[2][:, 0:D], oT[:, c, :], w.v["o"][:, c, :], start=(c == 0), stop=(c == OC - 1))
                        mm.then_inc(y_filled, 1)

                    attend(0)
                    for j in range(GR):
                        if j + 1 < GR:
                            attend(j + 1)
                        project(j)

            @block.vector
            def _(dve):
                for x in (yn_ready, yT_ready[0], vg_biased, feats_ready, aT_ready, o_ready, y_added):
                    dve.sem_inc(x, LEAD)
                dve.tensor_copy(within[:, :], chip.upper[:, :])
                dve.drain()
                dve.memset(within[0:CH, CH:P], 0.0)
                ln_stats_vector(chip, dve, chip.X, s, have=have_stats)
                w.wait(dve)
                with dve.Fori(0, NG) as g:
                    for j in range(GR):
                        b = g * GR + j
                        op = dve.tensor_scalar(yn[:, j, :], chip.X[:, b, :], chip.mv[:, b, 0:1], chip.rstd[:, bass.ds(b, 1)], ALU.subtract, ALU.mult)
                    op.then_inc(yn_ready, 1)
                    dve.wait_ge(turned[0], done(g))
                    dve.tensor_copy(yT[:, 0, :], bank[0][:, :]).then_inc(yT_ready[0], 1)

                    def add_vg_bias(j):
                        for m, dst in enumerate((v, gate)):
                            dve.wait_ge(vg_filled, done(g * (2 * GR) + (2 * j + m)))
                            dve.tensor_tensor(dst[:, j, :], bank[4 + m][:, :], w.v[("bv", "bg")[m]], ALU.add).then_inc(vg_biased, 1)

                    add_vg_bias(0)
                    dve.wait_ge(xs_ready, done(g))
                    for f, mul, add in zip(feats, w.v["mul"], w.v["add"]):
                        op = dve.tensor_scalar(f[:, :], xs[:, :], mul, add, ALU.mult, ALU.add)
                    op.then_inc(feats_ready, 1)
                    for j in range(1, GR):
                        add_vg_bias(j)
                    dve.wait_ge(scores_ready, done(g))
                    dve.tensor_scalar(pos[:, :, :], bank[2][:, :].rearrange("p (j q) -> p j q", j=GR), INNER ** -0.5, 0.0, ALU.mult, ALU.max)
                    dve.drain()
                    dve.tensor_tensor(aT[:, :, :], pos[:, :, :], within[:, :].unsqueeze(1).to_broadcast([P, GR, P]), ALU.mult)
                    dve.drain()
                    dve.tensor_tensor(aT[:, :, :], aT[:, :, :], pos[:, :, :], ALU.mult)
                    dve.drain()
                    dve.tensor_copy(aT[0:CH, :, CH:P], bank[3][0:CH, 0:GR * CH].rearrange("p (j q) -> p j q", j=GR)).then_inc(aT_ready, 1)

                    def add(j):
                        b = g * GR + j
                        dve.wait_ge(y_filled, done(b))
                        if j == 0:
                            dve.wait_ge(bias_added, done(g))
                        dve.tensor_tensor(chip.X[:, b, :], chip.X[:, b, :], bank[2][:, 0:D], ALU.add).then_inc(y_added, 1)
                        dve.drain()
                        dve.bn_stats(chip.bn[:, b, :], chip.X[:, b, :])

                    for j in range(GR):
                        dve.wait_ge(o_filled, done(g * GR + j))
                        if j >= 2:
                            add(j - 2)
                        dve.tensor_tensor(o[:, j % 2, :], bank[6 + j % 2][:, :], gate[:, j, :], ALU.mult).then_inc(o_ready, 1)
                    add(GR - 2)
                    add(GR - 1)

            @block.gpsimd
            def _(pool):
                pool.sem_inc(bias_added, LEAD)
                w.wait(pool)
                with pool.Fori(0, NG) as g:
                    pool.wait_ge(yn_ready, done(g))
                    those = bass.ds(g * GR, GR)
                    pool.tensor_tensor(chip.X[:, those, :], chip.X[:, those, :],
                                       w.v["bo"][:, :].unsqueeze(1).to_broadcast([P, GR, D]), ALU.add).then_inc(bias_added, 1)

            @block.scalar
            def _(act):
                for x in (yT_ready[1], xs_ready, vg_ready, oT_ready):
                    act.sem_inc(x, LEAD)
                ln_stats_scalar(chip, act, s)
                w.wait(act)
                act.preload_act_table(ACT.Silu)
                with act.Fori(0, NG) as g:
                    act.wait_ge(turned[1], done(g))
                    act.copy(yT[:, 1, :], bank[1][:, :]).then_inc(yT_ready[1], 1)
                    act.wait_ge(x_filled, done(g))
                    act.activation(xs[:, :], bank[2][:, :], ACT.Silu, bias=w.v["bx"]).then_inc(xs_ready, 1)
                    for j in range(GR):
                        for m, dst in enumerate((v, gate)):
                            act.wait_ge(vg_biased, done(g * (2 * GR) + (2 * j + m)))
                            act.activation(dst[:, j, :], dst[:, j, :], ACT.Silu).then_inc(vg_ready, 1)
                    for j in range(GR):
                        act.wait_ge(oT_filled, done(g * GR + j))
                        act.copy(oT[:, :, :], bank[3][:, :].rearrange("p (c q) -> p c q", c=OC)).then_inc(oT_ready, 1)


def l0_ffn_weights(chip, side):
    i, w = chip.ins, Weights(chip, "l0f", side)
    w.v = dict(fc=w.matrix(i["L0_ffn_W_fc"]), proj=w.matrix(i["L0_ffn_W_proj"]), g=w.columns(i["L0_ffn_ln_w"]), b=w.columns(i["L0_ffn_ln_b"]))
    return w


def ternary_ffn_block(chip, w, prefetch, have_stats):
    nc = chip.nc
    F = 1024
    FC = F // P
    with ExitStack() as scope:
        sb = lambda n, s, d=F32: chip.block_sb(f"l0f_{n}", s, d, scope)
        sem = lambda n: chip.sem(f"l0f_{n}")
        mag = sb("mag", [P, FC * D])
        below = sb("below", [P, FC * D])
        rowsum = sb("rowsum", [P, 2])
        half = sb("half", [P, 2])
        neghalf = sb("neghalf", [P, 2])
        allones = chip.ones[:, 0:P]
        fcT = sb("fcT", [P, KC, F])
        projT = sb("projT", [P, FC, D])
        yn = sb("yn", [P, GR, D])
        yT = sb("yT", [P, KC, TG])
        h = sb("h", [P, GR, F])
        hT = sb("hT", [P, FC, TG])
        hbn = sb("hbn", [P, GR, 2, 6])
        hmv = sb("hmv", [P, GR, 2])
        hvar = sb("hvar", [P, GR])
        hstd = sb("hstd", [P, GR])
        hrstd = sb("hrstd", [P, GR])
        tbank = [chip.ps(f"l0f_turn{i}", scope) for i in range(2)]
        hbank = [chip.ps(f"l0f_hidden{i}", scope) for i in range(2)]
        obank = [chip.ps(f"l0f_out{i}", scope) for i in range(2)]
        s = {n: sem(n) for n in ("var_ready", "std_ready")}
        mags_ready = sem("mags_ready")
        sums_ready = sem("sums_ready")
        ternary_ready = sem("ternary_ready")
        yn_ready = sem("yn_ready")
        turned = [sem("turned0"), sem("turned1")]
        copied = [sem("copied0"), sem("copied1")]
        h_filled = sem("h_filled")
        gelu_done = sem("gelu_done")
        hvar_ready, hstd_ready = sem("hvar_ready"), sem("hstd_ready")
        hn_ready = sem("hn_ready")
        out_filled, out_added = sem("out_filled"), sem("out_added")
        WT = (FC * KC // 4)
        PER = 1 + FC // 2
        weight_turns = 2 * WT // 2

        with nc.Block() as block:
            @block.sync
            def _(sp):
                if prefetch:
                    prefetch.load(sp)

            @block.tensor
            def _(pe):
                for x in (*turned, h_filled, out_filled):
                    pe.sem_inc(x, LEAD)
                pe.wait_ge(mags_ready, 2)
                pe.matmul(obank[0][:, 0:2], allones, rowsum[:, :], start=True, stop=True).then_inc(sums_ready, 1)
                n = 0
                for m, src in enumerate((w.v["fc"], w.v["proj"])):
                    pe.wait_ge(ternary_ready, m + 1)
                    for q in range(WT):
                        b = n % 2
                        pe.wait_ge(copied[b], done(n // 2 - 1))
                        for i in range(4):
                            r, c = (q % 2 * 4 + i, q // 2) if m == 0 else (q // 2, q % 2 * 4 + i)
                            mm = pe.transpose(tbank[b][:, i * P:(i + 1) * P], src[:, r, c * P:(c + 1) * P], chip.ident[:, :])
                        mm.then_inc(turned[b], 1)
                        n += 1
                with pe.Fori(0, NG) as g:
                    pe.wait_ge(yn_ready, done(g))
                    for kc in range(KC):
                        pe.wait_ge(copied[kc], done(g * PER + weight_turns - 1))
                        for j in range(GR):
                            mm = pe.transpose(tbank[kc][:, j * P:(j + 1) * P], yn[:, j, kc * P:(kc + 1) * P], chip.ident[:, :])
                        mm.then_inc(turned[kc], 1)
                    for kc in range(KC):
                        pe.wait_ge(copied[kc], done(g * PER + weight_turns))
                    for j in range(GR):
                        for c in range(2):
                            pe.wait_ge(gelu_done, done(g * (2 * GR) + (2 * j + c) - 2))
                            for kc in range(KC):
                                mm = pe.matmul(hbank[c][:, :], yT[:, kc, j * P:(j + 1) * P], fcT[:, kc, c * 512:(c + 1) * 512],
                                               start=(kc == 0), stop=(kc == KC - 1))
                            mm.then_inc(h_filled, 1)
                    pe.wait_ge(hn_ready, done(g))
                    for f in range(FC):
                        b = f % 2
                        pe.wait_ge(copied[b], done(g * PER + weight_turns + f // 2))
                        for j in range(GR):
                            mm = pe.transpose(tbank[b][:, j * P:(j + 1) * P], h[:, j, f * P:(f + 1) * P], chip.ident[:, :])
                        mm.then_inc(turned[b], 1)
                    for b in range(2):
                        pe.wait_ge(copied[b], done(g * PER + weight_turns + FC // 2))
                    for j in range(GR):
                        pe.wait_ge(out_added, done(g * GR + j - 2))
                        for f in range(FC):
                            mm = pe.matmul(obank[j % 2][:, 0:D], hT[:, f, j * P:(j + 1) * P], projT[:, f, :], start=(f == 0), stop=(f == FC - 1))
                        mm.then_inc(out_filled, 1)

            def copy_weight(eng, b):
                n = 0
                for m in range(2):
                    for q in range(WT):
                        if n % 2 == b:
                            eng.wait_ge(turned[b], done(n // 2))
                            src = tbank[b][:, :]
                            if m == 0:
                                dst = fcT[:, q // 2, q % 2 * 512:(q % 2 + 1) * 512]
                            else:
                                dst = projT[:, q % 2 * 4:q % 2 * 4 + 4, q // 2 * P:(q // 2 + 1) * P]
                                src = src.rearrange("p (i d) -> p i d", i=4)
                            (eng.tensor_copy(dst, src) if b == 0 else eng.copy(dst, src)).then_inc(copied[b], 1)
                        n += 1

            @block.vector
            def _(dve):
                for x in (copied[0], yn_ready, hvar_ready, hn_ready, out_added):
                    dve.sem_inc(x, LEAD)
                ln_stats_vector(chip, dve, chip.X, s, have=have_stats)
                w.wait(dve)
                dve.wait_ge(sums_ready, 1)
                dve.tensor_scalar(half[:, :], obank[0][:, 0:2], 1.0 / (F * D), 1e-6, ALU.mult, ALU.add)
                dve.drain()
                dve.tensor_scalar(neghalf[:, :], half[:, :], -0.5, None, ALU.mult)
                dve.tensor_scalar(half[:, :], half[:, :], 0.5, None, ALU.mult)
                dve.drain()
                for m, src in enumerate((w.v["fc"], w.v["proj"])):
                    flat = src.rearrange("p c n -> p (c n)")
                    dve.tensor_scalar(below[:, :], flat, neghalf[:, m:m + 1], None, ALU.is_lt)
                    dve.drain()
                    dve.scalar_tensor_tensor(out=flat, in0=flat, scalar=half[:, m:m + 1], in1=below[:, :], op0=ALU.is_gt,
                                             op1=ALU.subtract).then_inc(ternary_ready, 1)
                    dve.drain()
                copy_weight(dve, 0)
                with dve.Fori(0, NG) as g:
                    for j in range(GR):
                        b = g * GR + j
                        op = dve.tensor_scalar(yn[:, j, :], chip.X[:, b, :], chip.mv[:, b, 0:1], chip.rstd[:, bass.ds(b, 1)], ALU.subtract, ALU.mult)
                    op.then_inc(yn_ready, 1)
                    dve.wait_ge(turned[0], done(g * PER + weight_turns))
                    dve.tensor_copy(yT[:, 0, :], tbank[0][:, :]).then_inc(copied[0], 1)
                    for j in range(GR):
                        dve.wait_ge(gelu_done, done(g * (2 * GR) + 2 * j + 1))
                        for c in range(2):
                            dve.bn_stats(hbn[:, j, c, :], h[:, j, c * 512:(c + 1) * 512])
                        dve.drain()
                        dve.bn_aggr(hmv[:, j, :], hbn[:, j, :, :])
                    dve.drain()
                    dve.tensor_scalar(hvar[:, :], hmv[:, :, 1], LN_EPS, None, ALU.add).then_inc(hvar_ready, 1)
                    dve.wait_ge(hstd_ready, done(g))
                    dve.reciprocal(hrstd[:, :], hstd[:, :])
                    dve.drain()
                    for j in range(GR):
                        op = dve.tensor_scalar(h[:, j, :], h[:, j, :], hmv[:, j, 0:1], hrstd[:, j:j + 1], ALU.subtract, ALU.mult)
                    op.then_inc(hn_ready, 1)
                    for f in range(0, FC, 2):
                        dve.wait_ge(turned[0], done(g * PER + weight_turns + 1 + f // 2))
                        dve.tensor_scalar(hT[:, f, :], tbank[0][:, :], w.v["g"][:, f:f + 1], w.v["b"][:, f:f + 1], ALU.mult, ALU.add).then_inc(copied[0], 1)
                    for j in range(GR):
                        b = g * GR + j
                        dve.wait_ge(out_filled, done(b))
                        dve.tensor_tensor(chip.X[:, b, :], chip.X[:, b, :], obank[j % 2][:, 0:D], ALU.add).then_inc(out_added, 1)
                        dve.drain()
                        dve.bn_stats(chip.bn[:, b, :], chip.X[:, b, :])

            @block.scalar
            def _(act):
                for x in (copied[1], gelu_done, hstd_ready):
                    act.sem_inc(x, LEAD)
                w.wait(act)
                for m, src in enumerate((w.v["fc"], w.v["proj"])):
                    act.activation(mag[:, :], src.rearrange("p c n -> p (c n)"), ACT.Abs, accum_out=rowsum[:, m:m + 1]).then_inc(mags_ready, 1)
                    act.drain()
                ln_stats_scalar(chip, act, s)
                copy_weight(act, 1)
                with act.Fori(0, NG) as g:
                    act.wait_ge(turned[1], done(g * PER + weight_turns))
                    act.copy(yT[:, 1, :], tbank[1][:, :]).then_inc(copied[1], 1)
                    for j in range(GR):
                        for c in range(2):
                            act.wait_ge(h_filled, done(g * (2 * GR) + (2 * j + c)))
                            act.activation(h[:, j, c * 512:(c + 1) * 512], hbank[c][:, :], ACT.Gelu).then_inc(gelu_done, 1)
                    act.wait_ge(hvar_ready, done(g))
                    act.activation(hstd[:, :], hvar[:, :], ACT.Sqrt).then_inc(hstd_ready, 1)
                    for f in range(1, FC, 2):
                        act.wait_ge(turned[1], done(g * PER + weight_turns + 1 + f // 2))
                        act.activation(hT[:, f, :], tbank[1][:, :], ACT.Identity, bias=w.v["b"][:, f:f + 1], scale=w.v["g"][:, f:f + 1]).then_inc(copied[1], 1)


def l1_xattn_weights(chip, side):
    i, w = chip.ins, Weights(chip, "l1x", side)
    n = "L1_xattn_"
    q = w.room(KC * 192).rearrange("p (c n) -> p c n", c=KC)
    w.dmas.append((q[:, :, 0:128], i[n + "w_off"].rearrange("(c p) n -> p c n", p=P)))
    w.dmas.append((q[:, :, 128:192], i[n + "w_attw"].rearrange("(c p) n -> p c n", p=P)))
    bq = w.room(192, False)
    w.dmas.append((bq[:, 0:128], i[n + "b_off"].partition_broadcast(P)))
    w.dmas.append((bq[:, 128:192], i[n + "b_attw"].partition_broadcast(P)))
    w.v = dict(q=q, bq=bq, v=w.matrix(i[n + "w_value"]), o=w.matrix(i[n + "w_out"]), bv=w.everywhere(i[n + "b_value"]), bo=w.everywhere(i[n + "b_out"]))
    return w


def deform_block(chip, w, prefetch, have_stats):
    nc, ins = chip.nc, chip.ins
    H, NPT, HD = 16, 4, 16
    HP = H * NPT
    J0 = P // 2 - 1
    NJ = P - J0
    QW = 3 * HP
    with ExitStack() as scope:
        sb = lambda n, s, d=F32: chip.block_sb(f"l1x_{n}", s, d, scope)
        sem = lambda n: chip.sem(f"l1x_{n}")
        hat = sb("hat", [P, 2, HP, NJ])
        product = sb("product", [P, HP, NJ])
        wsum = sb("wsum", [P, 2, H, NJ])
        yn = sb("yn", [P, GR, D])
        yT = sb("yT", [P, KC, TG])
        cn = sb("cn", [NJ, GR, D])
        cT = sb("cT", [P, KC, GR, NJ])
        v = sb("v", [NJ, NB, D])
        q = sb("q", [P, GR, QW])
        ix = sb("ix", [P, NB, HP])
        aw = sb("aw", [P, NB, HP])
        hy = sb("hy", [P, GR, HP])
        amax = sb("amax", [P, GR * H])
        asum = sb("asum", [P, GR * H])
        rows_i = sb("rows_i", [P, NJ], I32)
        rows = sb("rows", [P, NJ])
        ref_i = sb("ref_i", [P, 1], I32)
        ref = sb("ref", [P, 1])
        wT = sb("wT", [NJ, 2, 4, P])
        on = sb("on", [P, D])
        oT = sb("oT", [P, KC, P])
        bank = [chip.ps(f"l1x_bank{i}", scope) for i in range(8)]
        s = {n: sem(n) for n in ("var_ready", "std_ready")}
        iota_ready = sem("iota_ready")
        rows_ready = sem("rows_ready")
        stats_ready = sem("stats_ready")
        ctx_loaded = sem("ctx_loaded")
        yn_ready = sem("yn_ready")
        bias_added = sem("bias_added")
        turned = [sem("turned0"), sem("turned1")]
        copied = [sem("copied0"), sem("copied1")]
        q_filled = [sem("q0_filled"), sem("q1_filled")]
        q_copied = sem("q_copied")
        v_filled, v_copied = sem("v_filled"), sem("v_copied")
        logits_ready, exp_ready = sem("logits_ready"), sem("exp_ready")
        points_ready = sem("points_ready")
        dist_ready = sem("dist_ready")
        hat_ready = sem("hat_ready")
        hat_used = sem("hat_used")
        wsum_ready = sem("wsum_ready")
        w_turned = sem("w_turned")
        w_copied = sem("w_copied")
        o_filled, o_copied = sem("o_filled"), sem("o_copied")
        oT_filled, oT_copied = sem("oT_filled"), sem("oT_copied")
        y_filled, y_added = sem("y_filled"), sem("y_added")
        dve_turn, act_turn = sem("dve_turn"), sem("act_turn")

        def is_first(g):
            return isinstance(g, int) and g == 0

        def is_last(g):
            return isinstance(g, int) and g == NG - 1

        def over_groups(eng, body):
            body(0, 2)
            with eng.Fori(1, NG - 2) as g:
                body(g, g + 2)
            body(NG - 2, None)
            body(NG - 1, None)

        with nc.Block() as block:
            @block.sync
            def _(sp):
                sp.dma_start(cn[:, :, :], ins["ctx_1024"][0:GR, J0:P, :].rearrange("b s d -> s b d")).then_inc(ctx_loaded, 16)
                if prefetch:
                    prefetch.load(sp)
                with sp.Fori(0, NG - 1) as g:
                    for kc in range(KC):
                        sp.wait_ge(turned[kc], done(g * 2))
                    sp.dma_start(cn[:, :, :], ins["ctx_1024"][bass.ds(g * GR + GR, GR), J0:P, :].rearrange("b s d -> s b d")).then_inc(ctx_loaded, 16)

            @block.gpsimd
            def _(pool):
                pool.iota(rows_i[:, :], [[1, NJ]], base=J0, channel_multiplier=0).then_inc(iota_ready, 1)
                pool.iota(ref_i[:, :], [[0, 1]], base=0, channel_multiplier=1).then_inc(iota_ready, 1)
                for x in (dist_ready, yn_ready, bias_added):
                    pool.sem_inc(x, LEAD)
                w.wait(pool)
                pool.wait_ge(stats_ready, 1)

                def normalise(g):
                    those = bass.ds(g * GR, GR)
                    pool.tensor_tensor(yn[:, :, :], chip.X[:, those, :], chip.mv[:, those, 0:1].to_broadcast([P, GR, D]), ALU.subtract)
                    pool.drain()
                    pool.tensor_tensor(yn[:, :, :], yn[:, :, :], chip.rstd[:, those].unsqueeze(2).to_broadcast([P, GR, D]), ALU.mult).then_inc(yn_ready, 1)

                def add_bias(g):
                    those = bass.ds(g * GR, GR)
                    pool.tensor_tensor(chip.X[:, those, :], chip.X[:, those, :],
                                       w.v["bo"][:, :].unsqueeze(1).to_broadcast([P, GR, D]), ALU.add).then_inc(bias_added, 1)

                def body(g, ahead):
                    pool.wait_ge(points_ready, done(g))
                    for j in range(GR):
                        n = g * GR + j
                        pool.wait_ge(hat_used, done(n - 2))
                        pool.tensor_tensor(hat[:, j % 2, :, :], rows[:, :].unsqueeze(1).to_broadcast([P, HP, NJ]),
                                           ix[:, bass.ds(n, 1), :].rearrange("p a n -> p (a n)").unsqueeze(2).to_broadcast([P, HP, NJ]),
                                           ALU.subtract).then_inc(dist_ready, 1)
                        if j == 1:
                            add_bias(g)
                            if ahead is not None:
                                normalise_next(ahead)

                def normalise_next(g):
                    for kc in range(KC):
                        pool.wait_ge(turned[kc], done(g * 2 - 1))
                    normalise(g)

                normalise(0)
                normalise_next(1)
                pool.wait_ge(rows_ready, 1)
                over_groups(pool, body)

            @block.tensor
            def _(pe):
                for x in (*turned, *q_filled, v_filled, w_turned, o_filled, oT_filled, y_filled):
                    pe.sem_inc(x, LEAD)
                w.wait(pe)

                def turn_context(g):
                    pe.wait_ge(ctx_loaded, g * 16 + 16)
                    pe.wait_ge(q_copied, done(g * 2 - 1))
                    pe.wait_ge(v_copied, done(g * (GR // 2) - 1))
                    for kc in range(KC):
                        for j in range(GR):
                            mm = pe.transpose(bank[kc][:, j * NJ:(j + 1) * NJ], cn[:, j, kc * P:(kc + 1) * P], chip.ident[0:NJ, 0:NJ])
                        mm.then_inc(turned[kc], 1)

                def turn_y(g):
                    pe.wait_ge(yn_ready, done(g))
                    for kc in range(KC):
                        pe.wait_ge(copied[kc], done(g * 2))
                        for j in range(GR):
                            mm = pe.transpose(bank[kc][:, j * P:(j + 1) * P], yn[:, j, kc * P:(kc + 1) * P], chip.ident[:, :])
                        mm.then_inc(turned[kc], 1)

                def project_q(g):
                    for kc in range(KC):
                        pe.wait_ge(copied[kc], done(g * 2 + 1))
                    for i in range(2):
                        for j in range(2):
                            for kc in range(KC):
                                mm = pe.matmul(bank[i][:, j * QW:(j + 1) * QW], yT[:, kc, (2 * i + j) * P:(2 * i + j + 1) * P], w.v["q"][:, kc, :],
                                               start=(kc == 0), stop=(kc == KC - 1))
                        mm.then_inc(q_filled[i], 1)

                def project_v(g):
                    for i in range(GR // 2):
                        pe.wait_ge(q_copied, done(g * 2 + i))
                        for j in range(2):
                            for kc in range(KC):
                                mm = pe.matmul(bank[i][0:NJ, j * D:(j + 1) * D], cT[:, kc, 2 * i + j, :], w.v["v"][:, kc, :], start=(kc == 0), stop=(kc == KC - 1))
                        mm.then_inc(v_filled, 1)

                def weights(g, j):
                    n = g * GR + j

                    def turn_weights(u):
                        pe.wait_ge(w_copied, done(n * (H // 4) + u - 2))
                        for i in range(4):
                            mm = pe.transpose(bank[5 + u % 2][0:NJ, i * P:(i + 1) * P], wsum[:, j % 2, u * 4 + i, :], chip.ident[:, :])
                        mm.then_inc(w_turned, 1)

                    pe.wait_ge(wsum_ready, done(n))
                    pe.wait_ge(o_copied, done(n - 1))
                    pe.wait_ge(v_copied, done(g * (GR // 2) + j // 2))
                    turn_weights(0)
                    for u in range(H // 4):
                        if u + 1 < H // 4:
                            turn_weights(u + 1)
                        pe.wait_ge(w_copied, done(n * (H // 4) + u))
                        for i in range(4):
                            h = u * 4 + i
                            mm = pe.matmul(bank[7][:, h * HD:(h + 1) * HD], wT[:, u % 2, i, :],
                                           v[:, bass.ds(n, 1), h * HD:(h + 1) * HD].rearrange("p a d -> p (a d)"), start=True, stop=True)
                    mm.then_inc(o_filled, 1)

                def output(g, j):
                    n = g * GR + j
                    pe.wait_ge(o_copied, done(n))
                    pe.wait_ge(oT_copied, done(n - 1))
                    for c in range(KC):
                        mm = pe.transpose(bank[2][:, c * P:(c + 1) * P], on[:, c * P:(c + 1) * P], chip.ident[:, :])
                    mm.then_inc(oT_filled, 1)
                    pe.wait_ge(oT_copied, done(n))
                    pe.wait_ge(y_added, done(n - 2))
                    for c in range(KC):
                        mm = pe.matmul(bank[3 + j % 2][:, 0:D], oT[:, c, :], w.v["o"][:, c, :], start=(c == 0), stop=(c == KC - 1))
                    mm.then_inc(y_filled, 1)

                def body(g, ahead):
                    for j in range(GR):
                        if j == 2 and ahead is not None:
                            project_q(ahead)
                        weights(g, j)
                        if j == 1 and ahead is not None:
                            turn_y(ahead)
                        if j == 2 and ahead is not None:
                            project_v(ahead)
                        output(g, j)
                        if j == 0 and ahead is not None:
                            turn_context(ahead)

                for g in range(2):
                    turn_context(g)
                    turn_y(g)
                    project_q(g)
                    project_v(g)
                over_groups(pe, body)

            @block.vector
            def _(dve):
                for x in (copied[0], q_copied, v_copied, logits_ready, points_ready, hat_used, wsum_ready, y_added):
                    dve.sem_inc(x, LEAD)
                dve.wait_ge(iota_ready, 2)
                dve.tensor_copy(rows[:, :], rows_i[:, :])
                dve.tensor_copy(ref[:, :], ref_i[:, :])
                dve.drain()
                dve.sem_inc(rows_ready, 1)
                dve.tensor_scalar(ref[:, :], ref[:, :], 1.0 / (P - 1), None, ALU.mult)
                ln_stats_vector(chip, dve, chip.X, s, have=have_stats)
                dve.sem_inc(stats_ready, 1)
                w.wait(dve)
                four = lambda x: x.rearrange("p j (h t) -> p (j h) t", t=NPT)
                per_head = lambda x: x[:, :].unsqueeze(2).to_broadcast([P, GR * H, NPT])

                def copy_context(g):
                    dve.wait_ge(turned[0], done(g * 2))
                    dve.tensor_copy(cT[:, 0, :, :], bank[0][:, 0:GR * NJ].rearrange("p (j t) -> p j t", j=GR)).then_inc(copied[0], 1)

                def copy_y(g):
                    dve.wait_ge(turned[0], done(g * 2 + 1))
                    dve.tensor_copy(yT[:, 0, :], bank[0][:, :]).then_inc(copied[0], 1)

                def place_points(g):
                    those = bass.ds(g * GR, GR)
                    for i in range(2):
                        dve.wait_ge(q_filled[i], done(g))
                        dve.tensor_tensor(q[:, 2 * i:2 * i + 2, :], bank[i][:, 0:2 * QW].rearrange("p (j n) -> p j n", j=2),
                                          w.v["bq"][:, :].unsqueeze(1).to_broadcast([P, 2, QW]), ALU.add).then_inc(q_copied, 1)
                    dve.drain()
                    offs = q[:, :, 0:2 * HP].rearrange("p j (n t) -> p j n t", t=2)
                    logit = q[:, :, 2 * HP:QW]
                    dve.tensor_reduce(amax[:, :], logit.rearrange("p j (h t) -> p j h t", t=NPT), AX.X, ALU.max)
                    dve.tensor_scalar(ix[:, those, :], offs[:, :, :, 0], 0.0, 1.0, ALU.max, ALU.min)
                    dve.tensor_scalar(hy[:, :, :], offs[:, :, :, 1], ref[:, 0:1], 0.0, ALU.add, ALU.max)
                    dve.drain()
                    dve.tensor_tensor(aw[:, those, :].rearrange("p j (h t) -> p j h t", t=NPT), logit.rearrange("p j (h t) -> p j h t", t=NPT),
                                      amax[:, :].rearrange("p (j h) -> p j h", j=GR).unsqueeze(3).to_broadcast([P, GR, H, NPT]), ALU.subtract).then_inc(logits_ready, 1)
                    dve.tensor_scalar(ix[:, those, :], ix[:, those, :], 1.0, float(P), ALU.add, ALU.mult)
                    dve.tensor_scalar(hy[:, :, :], hy[:, :, :], 1.0, 1.0, ALU.min, ALU.add)
                    dve.drain()
                    dve.tensor_scalar(ix[:, those, :], ix[:, those, :], -1.0, 0.5, ALU.add, ALU.mult)
                    dve.tensor_scalar(hy[:, :, :], hy[:, :, :], -1.0, -0.5, ALU.add, ALU.mult)
                    dve.drain()
                    dve.tensor_scalar(hy[:, :, :], hy[:, :, :], 1.0, None, ALU.add)

                def weigh_points(g):
                    those = bass.ds(g * GR, GR)
                    dve.wait_ge(exp_ready, done(g))
                    dve.sem_inc(dve_turn, 1)
                    dve.tensor_reduce(asum[:, :].rearrange("p (j h) -> p j h", j=GR), aw[:, those, :].rearrange("p j (h t) -> p j h t", t=NPT), AX.X, ALU.add)
                    dve.drain()
                    dve.reciprocal(asum[:, :], asum[:, :])
                    dve.tensor_tensor(aw[:, those, :], aw[:, those, :], hy[:, :, :], ALU.mult)
                    dve.drain()
                    dve.tensor_tensor(aw[:, those, :].rearrange("p j (h t) -> p j h t", t=NPT), aw[:, those, :].rearrange("p j (h t) -> p j h t", t=NPT),
                                      asum[:, :].rearrange("p (j h) -> p j h", j=GR).unsqueeze(3).to_broadcast([P, GR, H, NPT]), ALU.mult).then_inc(points_ready, 1)

                def add_v_bias(g):
                    for i in range(GR // 2):
                        dve.wait_ge(v_filled, done(g * (GR // 2) + i))
                        dve.tensor_tensor(v[:, bass.ds(g * GR + 2 * i, 2), :], bank[i][0:NJ, :].rearrange("p (j d) -> p j d", j=2),
                                          w.v["bv"][0:NJ, :].unsqueeze(1).to_broadcast([NJ, 2, D]), ALU.add).then_inc(v_copied, 1)

                def multiply(g, j):
                    n = g * GR + j
                    dve.drain()
                    dve.wait_ge(hat_ready, done(n))
                    dve.tensor_tensor(product[:, :, :], hat[:, j % 2, :, :],
                                      aw[:, bass.ds(n, 1), :].rearrange("p a n -> p (a n)").unsqueeze(2).to_broadcast([P, HP, NJ]), ALU.mult).then_inc(hat_used, 1)

                def reduce(g, j):
                    n = g * GR + j
                    dve.drain()
                    by_point = product[:, :, :].rearrange("p (h t) n -> p h t n", t=NPT)
                    dve.tensor_tensor(by_point[:, :, 0:2, :], by_point[:, :, 0:2, :], by_point[:, :, 2:4, :], ALU.add)
                    dve.drain()
                    if not is_first(g) or j >= 2:
                        dve.wait_ge(w_turned, done(n * (H // 4) - (H // 4 + 1)))
                    dve.tensor_tensor(wsum[:, j % 2, :, :], by_point[:, :, 0, :], by_point[:, :, 1, :], ALU.add).then_inc(wsum_ready, 1)

                def add(g, j):
                    b = g * GR + j
                    dve.wait_ge(y_filled, done(b))
                    if j == 0:
                        dve.wait_ge(bias_added, done(g))
                    dve.tensor_tensor(chip.X[:, b, :], chip.X[:, b, :], bank[3 + j % 2][:, 0:D], ALU.add).then_inc(y_added, 1)
                    dve.drain()
                    dve.bn_stats(chip.bn[:, b, :], chip.X[:, b, :])

                def body(g, ahead):
                    for j in range(GR):
                        if j == 3 and ahead is not None:
                            copy_y(ahead)
                        multiply(g, j)
                        if j == 2 and ahead is not None:
                            copy_context(ahead)
                        if j >= 2:
                            add(g, j - 2)
                        elif not is_first(g):
                            add(g - 1, j + 2)
                        if j == 3 and ahead is not None:
                            place_points(ahead)
                        reduce(g, j)
                    if ahead is not None:
                        weigh_points(ahead)
                        add_v_bias(ahead)

                for g in range(2):
                    copy_context(g)
                    copy_y(g)
                    place_points(g)
                    weigh_points(g)
                    add_v_bias(g)
                over_groups(dve, body)
                add(NG - 1, 2)
                add(NG - 1, 3)

            @block.scalar
            def _(act):
                for x in (copied[1], exp_ready, hat_ready, w_copied, o_copied, oT_copied):
                    act.sem_inc(x, LEAD)
                ln_stats_scalar(chip, act, s)
                act.preload_act_table(ACT.Exp)

                def copy_context(g):
                    act.wait_ge(turned[1], done(g * 2))
                    act.copy(cT[:, 1, :, :], bank[1][:, 0:GR * NJ].rearrange("p (j t) -> p j t", j=GR)).then_inc(copied[1], 1)

                def copy_y(g):
                    act.wait_ge(turned[1], done(g * 2 + 1))
                    act.copy(yT[:, 1, :], bank[1][:, :]).then_inc(copied[1], 1)

                def exp(g):
                    act.wait_ge(logits_ready, done(g))
                    act.sem_inc(act_turn, 1)
                    act.activation(aw[:, bass.ds(g * GR, GR), :], aw[:, bass.ds(g * GR, GR), :], ACT.Exp).then_inc(exp_ready, 1)

                def distance(n, half):
                    act.wait_ge(dist_ready, done(n))
                    act.activation(hat[:, half, :, :], hat[:, half, :, :], ACT.Abs)

                def weigh(half):
                    act.drain()
                    act.activation(hat[:, half, :, :], hat[:, half, :, :], ACT.Relu, bias=1.0, scale=-1.0).then_inc(hat_ready, 1)

                def copy_weights(g, j, u):
                    act.wait_ge(w_turned, done((g * GR + j) * (H // 4) + u))
                    act.copy(wT[:, u % 2, :, :], bank[5 + u % 2][0:NJ, :].rearrange("p (i q) -> p i q", i=4)).then_inc(w_copied, 1)

                def body(g, ahead):
                    for j in range(GR):
                        n = g * GR + j
                        if j == 1 and ahead is not None:
                            copy_context(ahead)
                        copy_weights(g, j, 0)
                        copy_weights(g, j, 1)
                        more = j < GR - 2 or not is_last(g)
                        if more:
                            distance(n + 2, j % 2)
                        copy_weights(g, j, 2)
                        copy_weights(g, j, 3)
                        if j == 2 and ahead is not None:
                            exp(ahead)
                        if more:
                            weigh(j % 2)
                        if j == 1 and ahead is not None:
                            copy_y(ahead)
                        act.wait_ge(o_filled, done(n))
                        act.copy(on[:, :], bank[7][:, 0:D]).then_inc(o_copied, 1)
                        act.wait_ge(oT_filled, done(n))
                        act.copy(oT[:, :, :], bank[2][:, 0:D].rearrange("p (c q) -> p c q", c=KC)).then_inc(oT_copied, 1)

                copy_context(0)
                copy_y(0)
                exp(0)
                for n in range(2):
                    distance(n, n)
                    weigh(n)
                copy_context(1)
                copy_y(1)
                exp(1)
                over_groups(act, body)



def rwkv_weights(chip, side):
    i, w = chip.ins, Weights(chip, "rwkv", side)
    n = "L0_attn_"
    w.v = dict(k=w.matrix(i[n + "W_key"]), v=w.matrix(i[n + "W_value"]), r=w.matrix(i[n + "W_recept"]), o=w.matrix(i[n + "W_out"]),
               k2=w.matrix(i[n + "W_key2"]), v2=w.matrix(i[n + "W_value2"]), r2=w.matrix(i[n + "W_recept2"]))
    for m in ("ln1_w", "ln2_w", "time_decay", "time_first", "time_mix_k", "time_mix_v", "time_mix_r", "time_mix_k2", "time_mix_r2"):
        w.v[m] = w.columns(i[n + m])
    return w


def rwkv_block(chip, w, prefetch, have_stats):
    nc = chip.nc
    W1 = P + 1
    F = 1024
    FC = F // P
    with ExitStack() as scope:
        sb = lambda n, s, d=F32: chip.block_sb(f"rwkv_{n}", s, d, scope)
        sem = lambda n: chip.sem(f"rwkv_{n}")
        y = sb("y", [P, GR, D])
        hn = sb("hn", [P, GR, D])
        hT = sb("hT", [P, KC, GR, W1])
        diff = sb("diff", [P, KC, GR, P])
        mix = [sb(f"mix_{m}", [P, KC, TG]) for m in "kvr"]
        mix2 = [sb(f"mix2_{m}", [P, KC, TG]) for m in "kr"]
        decay = sb("decay", [P, KC])
        decays = sb("decays", [P, KC, GR, W1])
        kc_ = sb("k_clipped", [P, TG])
        ku = sb("ku_clipped", [P, TG])
        ek = sb("ek", [P, KC, GR, W1])
        ekv = sb("ekv", [P, KC, GR, W1])
        eku = sb("eku", [P, TG])
        er = sb("er", [P, TG])
        sa = sb("sum_ekv", [P, GR, W1])
        sbk = sb("sum_ek", [P, GR, W1])
        num = sb("num", [P, TG])
        den = sb("den", [P, TG])
        rw = sb("rw", [P, KC, TG])
        sq = sb("sq", [P, D])
        ms = sb("ms", [P, GR])
        root = sb("root", [P, GR])
        rms = sb("rms", [P, GR])
        kr = sb("kr", [P, 2, TG])
        k2 = sb("k2", [P, FC, TG])
        r2 = sb("r2", [P, 2, D])
        kv = sb("kv", [P, D])
        bank = [chip.ps(f"rwkv_bank{i}", scope) for i in range(8)]
        s = {n: sem(n) for n in ("var_ready", "std_ready")}
        decay_step = sem("decay_step")
        decay_back = sem("decay_back")
        hn_ready = sem("hn_ready")
        filled = [sem("bank0_filled"), sem("bank1_filled")]
        emptied = [sem("bank0_emptied"), sem("bank1_emptied")]
        mix_ready = sem("mix_ready")
        kvr_filled = sem("kvr_filled")
        clipped = sem("clipped")
        exps_ready = sem("exps_ready")
        rw_ready = sem("rw_ready")
        y_filled, y_ready = sem("y_filled"), sem("y_ready")
        ms_ready, root_ready = sem("ms_ready"), sem("root_ready")
        relu_ready = [sem("relu0_ready"), sem("relu1_ready")]
        k2_ready = sem("k2_ready")
        r2_filled, r2_exp = sem("r2_filled"), sem("r2_exp")
        r2_used = sem("r2_used")
        kv_filled, kv_added = sem("kv_filled"), sem("kv_added")
        PER = 2 + FC // 2

        with nc.Block() as block:
            @block.sync
            def _(sp):
                if prefetch:
                    prefetch.load(sp)

            @block.tensor
            def _(pe):
                for x in (*filled, kvr_filled, y_filled, r2_filled, kv_filled):
                    pe.sem_inc(x, LEAD)
                w.wait(pe)

                def turn(g, n):
                    pe.wait_ge(hn_ready, done(g * 2 + n))
                    for kc in range(KC):
                        pe.wait_ge(emptied[kc], done(g * PER + n - 1))
                        for j in range(GR):
                            mm = pe.transpose(bank[kc][:, j * P:(j + 1) * P], hn[:, j, kc * P:(kc + 1) * P], chip.ident[:, :])
                        mm.then_inc(filled[kc], 1)

                def group(g, more):
                    pe.wait_ge(mix_ready, done(g * 2))
                    for m in range(KC):
                        pe.wait_ge(r2_exp, done(g * GR + m - 2))
                        pe.wait_ge(kv_added, done(g * GR + m - 2))
                        for i, name in enumerate("kvr"):
                            for kc in range(KC):
                                mm = pe.matmul(bank[2 + 2 * i + m][:, :], w.v[name][:, kc, m * P:(m + 1) * P], mix[i][:, kc, :],
                                               start=(kc == 0), stop=(kc == KC - 1))
                        mm.then_inc(kvr_filled, 1)
                    pe.wait_ge(rw_ready, done(g * 2 + 1))
                    for j in range(GR):
                        pe.wait_ge(y_ready, done(g * GR + j - 2))
                        for kc in range(KC):
                            mm = pe.matmul(bank[2 + j % 2][:, 0:D], rw[:, kc, j * P:(j + 1) * P], w.v["o"][:, kc, :], start=(kc == 0), stop=(kc == KC - 1))
                        mm.then_inc(y_filled, 1)
                    turn(g, 1)
                    pe.wait_ge(mix_ready, done(g * 2 + 1))
                    for f in range(FC):
                        b = f % 2
                        pe.wait_ge(emptied[b], done(g * PER + 1 + f // 2))
                        for kc in range(KC):
                            mm = pe.matmul(bank[b][:, :], w.v["k2"][:, kc, f * P:(f + 1) * P], mix2[0][:, kc, :], start=(kc == 0), stop=(kc == KC - 1))
                        mm.then_inc(filled[b], 1)
                    for j in range(GR):
                        pe.wait_ge(r2_exp, done(g * GR + j - 2))
                        for kc in range(KC):
                            mm = pe.matmul(bank[4 + j % 2][:, 0:D], mix2[1][:, kc, j * P:(j + 1) * P], w.v["r2"][:, kc, :], start=(kc == 0), stop=(kc == KC - 1))
                        mm.then_inc(r2_filled, 1)
                        if j == 0:
                            pe.wait_ge(k2_ready, done(g * FC + FC - 1))
                        pe.wait_ge(kv_added, done(g * GR + j - 2))
                        for f in range(FC):
                            mm = pe.matmul(bank[6 + j % 2][:, 0:D], k2[:, f, j * P:(j + 1) * P], w.v["v2"][:, f, :], start=(f == 0), stop=(f == FC - 1))
                        mm.then_inc(kv_filled, 1)
                        if j == 0 and more:
                            turn(g + 1, 0)

                turn(0, 0)
                with pe.Fori(0, NG - 1) as g:
                    group(g, True)
                group(NG - 1, False)

            @block.vector
            def _(dve):
                for x in (hn_ready, emptied[0], mix_ready, clipped, rw_ready, y_ready, ms_ready, relu_ready[0], r2_used, kv_added):
                    dve.sem_inc(x, LEAD)
                w.wait(dve)
                for z in (hT, ek, ekv):
                    dve.memset(z[:, :, :, 0:1], 0.0)
                ln_stats_vector(chip, dve, chip.X, s, twice=True, second_eps=1e-6, have=have_stats)
                dve.wait_ge(decay_step, 1)
                dve.tensor_scalar(decay[:, :], decay[:, :], -1.0, -20.0, ALU.mult, ALU.max)
                dve.drain()
                dve.tensor_scalar(decay[:, :], decay[:, :], 20.0, None, ALU.min).then_inc(decay_back, 1)
                dve.wait_ge(decay_step, 2)
                for kc in range(KC):
                    for j in range(GR):
                        dve.tensor_scalar(decays[:, kc, j, 1:W1], chip.ones[:, 0:P], decay[:, kc:kc + 1], None, ALU.mult)
                dve.memset(decays[:, :, :, 0:1], 0.0)
                dve.drain()

                def shift(g, n, weight, mixes):
                    dve.wait_ge(filled[0], done(g * PER + n))
                    dve.tensor_scalar(hT[:, 0, :, 1:W1], bank[0][:, :].rearrange("p (j t) -> p j t", j=GR), weight[:, 0:1], None, ALU.mult).then_inc(emptied[0], 1)
                    dve.drain()
                    dve.wait_ge(emptied[1], done(g * PER + n))
                    dve.tensor_tensor(diff[:, :, :, :], hT[:, :, :, 1:W1], hT[:, :, :, 0:P], ALU.subtract)
                    dve.drain()
                    for dst, name in mixes:
                        for kc in range(KC):
                            op = dve.scalar_tensor_tensor(out=dst[:, kc, :].rearrange("p (j t) -> p j t", j=GR), in0=diff[:, kc, :, :],
                                                          scalar=w.v[name][:, kc:kc + 1], in1=hT[:, kc, :, 0:P], op0=ALU.mult, op1=ALU.add)
                    op.then_inc(mix_ready, 1)

                def prepare(g):
                    for j in range(GR):
                        b = g * GR + j
                        dve.tensor_scalar(y[:, j, :], chip.X[:, b, :], chip.mv[:, b, 0:1], chip.rstd[:, bass.ds(b, 1)], ALU.subtract, ALU.mult)
                        op = dve.tensor_scalar(hn[:, j, :], chip.X[:, b, :], chip.mv[:, b, 0:1], chip.rstd2[:, bass.ds(b, 1)], ALU.subtract, ALU.mult)
                    op.then_inc(hn_ready, 1)

                def time_shift(g):
                    shift(g, 0, w.v["ln1_w"], [(mix[0], "time_mix_k"), (mix[1], "time_mix_v"), (mix[2], "time_mix_r")])

                as3 = lambda x: x.rearrange("p (j t) -> p j t", j=GR)

                def group(g, more):
                    for m in range(KC):
                        dve.wait_ge(kvr_filled, done(g * KC + m))
                        u = w.v["time_first"][:, m:m + 1]
                        dve.tensor_scalar(ku[:, :], bank[2 + m][:, :], u, -20.0, ALU.add, ALU.max)
                        dve.tensor_scalar(kc_[:, :], bank[2 + m][:, :], -20.0, 20.0, ALU.max, ALU.min)
                        dve.drain()
                        dve.tensor_scalar(ku[:, :], ku[:, :], 20.0, None, ALU.min).then_inc(clipped, 1)
                        dve.wait_ge(exps_ready, done(g * KC + m))
                        dve.tensor_tensor(ekv[:, m, :, 1:W1], ek[:, m, :, 1:W1], as3(bank[4 + m][:, :]), ALU.mult)
                        dve.tensor_tensor(num[:, :], eku[:, :], bank[4 + m][:, :], ALU.mult)
                        dve.drain()
                        flat = lambda x: x.rearrange("p j t -> p (j t)")
                        dve.tensor_tensor_scan(flat(sa[:, :, :]), flat(decays[:, m, :, :]), flat(ekv[:, m, :, :]), 0.0, ALU.mult, ALU.add)
                        dve.tensor_tensor_scan(flat(sbk[:, :, :]), flat(decays[:, m, :, :]), flat(ek[:, m, :, :]), 0.0, ALU.mult, ALU.add)
                        dve.drain()
                        dve.tensor_tensor(as3(num[:, :]), as3(num[:, :]), sa[:, :, 0:P], ALU.add)
                        dve.scalar_tensor_tensor(out=as3(den[:, :]), in0=as3(eku[:, :]), scalar=1e-8, in1=sbk[:, :, 0:P], op0=ALU.add, op1=ALU.add)
                        dve.drain()
                        dve.scalar_tensor_tensor(out=den[:, :], in0=er[:, :], scalar=1.0, in1=den[:, :], op0=ALU.add, op1=ALU.mult)
                        dve.drain()
                        dve.reciprocal(den[:, :], den[:, :])
                        dve.drain()
                        dve.tensor_tensor(rw[:, m, :], num[:, :], den[:, :], ALU.mult).then_inc(rw_ready, 1)
                    for j in range(GR):
                        dve.wait_ge(y_filled, done(g * GR + j))
                        dve.tensor_tensor(y[:, j, :], y[:, j, :], bank[2 + j % 2][:, 0:D], ALU.add).then_inc(y_ready, 1)
                        dve.drain()
                        dve.tensor_tensor_reduce(sq[:, :], y[:, j, :], y[:, j, :], 1.0 / D, 0.0, ALU.mult, ALU.add, ms[:, j:j + 1])
                    dve.drain()
                    dve.tensor_scalar(ms[:, :], ms[:, :], 1e-6, None, ALU.add).then_inc(ms_ready, 1)
                    dve.wait_ge(root_ready, done(g))
                    dve.reciprocal(rms[:, :], root[:, :])
                    dve.drain()
                    for j in range(GR):
                        op = dve.tensor_scalar(hn[:, j, :], y[:, j, :], rms[:, j:j + 1], None, ALU.mult)
                    op.then_inc(hn_ready, 1)
                    for j in range(GR):
                        b = g * GR + j
                        dve.tensor_tensor(chip.X[:, b, :], chip.X[:, b, :], y[:, j, :], ALU.add)
                    dve.drain()
                    shift(g, 1, w.v["ln2_w"], [(mix2[0], "time_mix_k2"), (mix2[1], "time_mix_r2")])
                    if more:
                        dve.drain()
                        prepare(g + 1)
                    for f in range(0, FC, 2):
                        dve.wait_ge(filled[0], done(g * PER + 2 + f // 2))
                        dve.wait_ge(k2_ready, done(g * FC + f - 2))
                        dve.tensor_scalar(kr[:, 0, :], bank[0][:, :], 0.0, None, ALU.max).then_inc(relu_ready[0], 1)
                        dve.drain()
                        dve.sem_inc(emptied[0], 1)
                    for j in range(GR):
                        b = g * GR + j
                        dve.wait_ge(r2_exp, done(g * GR + j))
                        dve.tensor_scalar(r2[:, j % 2, :], r2[:, j % 2, :], 1.0, None, ALU.add)
                        dve.drain()
                        dve.reciprocal(r2[:, j % 2, :], r2[:, j % 2, :])
                        dve.drain()
                        dve.wait_ge(kv_filled, done(g * GR + j))
                        dve.tensor_tensor(kv[:, :], r2[:, j % 2, :], bank[6 + j % 2][:, 0:D], ALU.mult).then_inc(kv_added, 1)
                        dve.drain()
                        dve.tensor_tensor(chip.X[:, b, :], chip.X[:, b, :], kv[:, :], ALU.add).then_inc(r2_used, 1)
                        dve.drain()
                        dve.bn_stats(chip.bn[:, b, :], chip.X[:, b, :])
                        if j == 0 and more:
                            time_shift(g + 1)

                prepare(0)
                time_shift(0)
                with dve.Fori(0, NG - 1) as g:
                    group(g, True)
                group(NG - 1, False)

            @block.gpsimd
            def _(pool):
                pool.sem_inc(k2_ready, LEAD)
                with pool.Fori(0, NG) as g:
                    for f in range(FC):
                        pool.wait_ge(relu_ready[f % 2], done(g * (FC // 2) + f // 2))
                        pool.tensor_tensor(k2[:, f, :], kr[:, f % 2, :], kr[:, f % 2, :], ALU.mult).then_inc(k2_ready, 1)

            @block.scalar
            def _(act):
                for x in (emptied[1], exps_ready, root_ready, relu_ready[1], r2_exp):
                    act.sem_inc(x, LEAD)
                w.wait(act)
                ln_stats_scalar(chip, act, s, twice=True)
                act.activation(decay[:, :], w.v["time_decay"], ACT.Exp).then_inc(decay_step, 1)
                act.wait_ge(decay_back, 1)
                act.activation(decay[:, :], decay[:, :], ACT.Exp).then_inc(decay_step, 1)

                def half(g, n, weight):
                    act.wait_ge(filled[1], done(g * PER + n))
                    act.activation(hT[:, 1, :, 1:W1], bank[1][:, :].rearrange("p (j t) -> p j t", j=GR), ACT.Copy, scale=weight[:, 1:2]).then_inc(emptied[1], 1)

                def group(g, more):
                    for m in range(KC):
                        act.wait_ge(kvr_filled, done(g * KC + m))
                        act.wait_ge(rw_ready, done(g * KC + m - 1))
                        act.activation(er[:, :], bank[6 + m][:, :], ACT.Exp, scale=-1.0)
                        act.wait_ge(clipped, done(g * KC + m))
                        act.activation(ek[:, m, :, 1:W1], kc_[:, :].rearrange("p (j t) -> p j t", j=GR), ACT.Exp)
                        act.activation(eku[:, :], ku[:, :], ACT.Exp)
                        act.drain()
                        act.sem_inc(exps_ready, 1)
                    act.wait_ge(ms_ready, done(g))
                    act.activation(root[:, :], ms[:, :], ACT.Sqrt).then_inc(root_ready, 1)
                    half(g, 1, w.v["ln2_w"])
                    for f in range(1, FC, 2):
                        act.wait_ge(filled[1], done(g * PER + 2 + f // 2))
                        act.wait_ge(k2_ready, done(g * FC + f - 2))
                        act.activation(kr[:, 1, :], bank[1][:, :], ACT.Relu).then_inc(relu_ready[1], 1)
                        act.drain()
                        act.sem_inc(emptied[1], 1)
                    for j in range(GR):
                        act.wait_ge(r2_filled, done(g * GR + j))
                        act.wait_ge(r2_used, done(g * GR + j - 2))
                        act.activation(r2[:, j % 2, :], bank[4 + j % 2][:, 0:D], ACT.Exp, scale=-1.0).then_inc(r2_exp, 1)
                        if j == 0 and more:
                            half(g + 1, 0, w.v["ln1_w"])

                half(0, 0, w.v["ln1_w"])
                with act.Fori(0, NG - 1) as g:
                    group(g, True)
                group(NG - 1, False)


def attention_entry(name):
    weights, plan = PLANS[name]
    return weights, lambda chip, w, prefetch, have_stats: attention_block(chip, plan, w, prefetch, have_stats)


def experts_entry(name, weights, block):
    return weights, lambda chip, w, prefetch, have_stats: block(chip, EXPERTS[name], w, prefetch, have_stats)


SUBLAYERS = [["rwkv"], ["l0x"], ["l0f"], ["l1a"], ["l1x"], ["l1f"], ["l2a"], ["l2x"], ["l2fa", "l2fm"], ["gau"], ["l3x"], ["l3f"]]
BLOCKS = {name: attention_entry(name) for name in PLANS}
BLOCKS["l1f"] = experts_entry("l1f", l1_ffn_weights, small_experts_block)
BLOCKS["l2fm"] = experts_entry("l2fm", l2_ffn_moe_weights, sorted_experts_block)
BLOCKS["l3f"] = experts_entry("l3f", l3_ffn_weights, sorted_experts_block)
BLOCKS["l0f"] = (l0_ffn_weights, ternary_ffn_block)
BLOCKS["l1x"] = (l1_xattn_weights, deform_block)
BLOCKS["gau"] = (gau_weights, gau_block)
BLOCKS["rwkv"] = (rwkv_weights, rwkv_block)


LEAVES_STATS = set(PLANS) | {"rwkv", "l0f", "l1x", "l1f", "l2fm", "gau"}


USES_Y = ("l2fa", "l2fm", "l3f")


def decoder_program(nc, ins, out):
    with ExitStack() as ctx:
        chip = Chip(nc, ins, out, ctx)
        todo = [b for m in STAGES for b in SUBLAYERS[m]]
        weights = [BLOCKS[b][0](chip, n % 2) for n, b in enumerate(todo)]
        setup_block(chip, weights[0])
        chip.end_block()
        for n, b in enumerate(todo):
            nxt = weights[n + 1] if n + 1 < len(todo) else None
            have_stats = n > 0 and todo[n - 1] in LEAVES_STATS
            chip.begin_block(weights[n], y_in_use=b in USES_Y)
            BLOCKS[b][1](chip, weights[n], nxt, have_stats)
            chip.end_block()
        store_block(chip)


def kernel(**inputs):
    import numpy as _np
    import concourse.bacc as _bacc
    from concourse import mybir as _mybir
    from concourse.bass_utils import run_bass_kernel_spmd as _run

    nc = _bacc.Bacc("TRN2", target_bir_lowering=False, num_devices=1)
    arrays, args = {}, {}
    for name in inputs:
        a = _np.ascontiguousarray(inputs[name])
        if a.ndim == 0:
            a = a.reshape(1)
        arrays[f"in_{name}"] = a
        args[name] = nc.dram_tensor(f"in_{name}", a.shape, _mybir.dt.from_np(a.dtype), kind="ExternalInput").ap()
    out = nc.dram_tensor("out_0", (NB, P, D), F32, kind="ExternalOutput").ap()
    decoder_program(nc, args, out)
    r = _run(nc, [arrays], core_ids=[0])
    return r.results[0]["out_0"]
```
